# Optimizing a Trainium2 kernel written in Bass

```python
import numpy as np
import jax
import jax.numpy as jnp

def _softmax(x, axis=-1):
    return jax.nn.softmax(x, axis=axis)

def _gelu(x):
    return jax.nn.gelu(x, approximate=True)

def _silu(x):
    return jax.nn.silu(x)

def _sigmoid(x):
    return jax.nn.sigmoid(x)

def _layernorm(x, axis=-1, eps=1e-05):
    m = jnp.mean(x, axis=axis, keepdims=True)
    v = jnp.var(x, axis=axis, keepdims=True)
    return (x - m) / jnp.sqrt(v + eps)

def _scatter_add(tgt, idx, src, axis=0):
    return tgt.at[idx].add(src)

def _segment_sum(src, seg, n):
    return jax.ops.segment_sum(src, seg, n)
kernel_name = 'mk_lm_tower_d1_tok_ids512_r4_26259c'

def setup_inputs(seed: int=0):
    np.random.seed(seed)
    _w = jnp.asarray

    def _rec_inputs():
        import jax
        import jax.numpy as jnp
        _rk = jax.random.key(seed)
        x = jax.random.randint(jax.random.fold_in(_rk, 1), (16, 512), 0, 50226, jnp.int32)
        return x
    x = _rec_inputs()

    def _L0_tok_setup():
        import jax, jax.numpy as jnp
        import numpy as np
        import math
        V, S, D, B = (50257, 512, 128, 4)
        DFF = 4 * D
        EPS = 1e-05

        def layer_norm(z, g, b):
            mu = jnp.mean(z, axis=-1, keepdims=True)
            var = jnp.mean((z - mu) ** 2, axis=-1, keepdims=True)
            return (z - mu) * jax.lax.rsqrt(var + EPS) * g + b

        def pos_embedding(seq_len, d_model):
            pos = jnp.arange(seq_len, dtype=jnp.float32)[:, None]
            i = jnp.arange(d_model, dtype=jnp.float32)[None, :]
            ang = pos / jnp.power(10000.0, 2.0 * i / d_model)
            even = (jnp.arange(d_model) % 2 == 0)[None, :]
            return jnp.where(even, jnp.sin(ang), jnp.cos(ang))
        key = jax.random.key(seed)
        ks = jax.random.split(key, 14)
        w = lambda k, sh: jax.random.normal(k, sh, dtype=jnp.float32) * 0.02
        return {'input_seq': jax.random.randint(ks[0], (B, S), 0, V), 'emb': w(ks[1], (V, D)), 'wk': w(ks[2], (D, D)), 'bk': jnp.zeros((D,), jnp.float32), 'wq': w(ks[3], (D, D)), 'bq': jnp.zeros((D,), jnp.float32), 'wv': w(ks[4], (D, D)), 'bv': jnp.zeros((D,), jnp.float32), 'ln_g': jnp.ones((D,), jnp.float32), 'ln_b': jnp.zeros((D,), jnp.float32), 'w1': w(ks[5], (D, DFF)), 'b1': jnp.zeros((DFF,), jnp.float32), 'w2': w(ks[6], (DFF, D)), 'b2': jnp.zeros((D,), jnp.float32)}
    _L0_tok_all = _L0_tok_setup()
    _L0_tok_in = {k: v for k, v in _L0_tok_all.items() if k in ('emb', 'wk', 'bk', 'wq', 'bq', 'wv', 'bv', 'ln_g', 'ln_b', 'w1', 'b1', 'w2', 'b2')}
    del _L0_tok_all

    def _L0_attn_setup():
        import jax, jax.numpy as jnp
        import numpy as np
        B, S, D = (8, 512, 128)
        QK_DIM = 128
        HID = 2 * D
        EPS = 1e-05

        def _layernorm(x, g, b):
            mu = jnp.mean(x, axis=-1, keepdims=True)
            var = jnp.mean((x - mu) ** 2, axis=-1, keepdims=True)
            return (x - mu) * jax.lax.rsqrt(var + EPS) * g + b
        key = jax.random.key(seed)
        ks = jax.random.split(key, 8)
        std = 0.02
        return {'x': jax.random.normal(ks[0], (B, S, D), dtype=jnp.float32), 'ln_g': jnp.ones((D,), jnp.float32), 'ln_b': jnp.zeros((D,), jnp.float32), 'Wh': jax.random.normal(ks[1], (D, HID * 2), jnp.float32) * std, 'bh': jnp.zeros((HID * 2,), jnp.float32), 'Wqk': jax.random.normal(ks[2], (D, QK_DIM), jnp.float32) * std, 'bqk': jnp.zeros((QK_DIM,), jnp.float32), 'gamma': jax.random.normal(ks[3], (2, QK_DIM), jnp.float32) * std, 'beta': jnp.zeros((2, QK_DIM), jnp.float32), 'Wo': jax.random.normal(ks[4], (HID, D), jnp.float32) * std, 'bo': jnp.zeros((D,), jnp.float32)}
    _L0_attn_all = _L0_attn_setup()
    _L0_attn_in = {k: v for k, v in _L0_attn_all.items() if k in ('ln_g', 'ln_b', 'Wh', 'bh', 'Wqk', 'bqk', 'gamma', 'beta', 'Wo', 'bo')}
    del _L0_attn_all

    def _L0_ffn_setup():
        import jax, jax.numpy as jnp
        import numpy as np
        B, S, D = (8, 512, 128)
        FF = 512
        E = 8
        key = jax.random.key(seed)
        ks = jax.random.split(key, 7)
        s = 1.0 / np.sqrt(D)
        sf = 1.0 / np.sqrt(FF)
        return {'x': jax.random.normal(ks[0], (B, S, D), dtype=jnp.float32), 'Wg': jax.random.uniform(ks[1], (D, E), jnp.float32, -s, s), 'bg': jax.random.uniform(ks[2], (E,), jnp.float32, -s, s), 'W1': jax.random.uniform(ks[3], (E, D, FF), jnp.float32, -s, s), 'b1': jax.random.uniform(ks[4], (E, FF), jnp.float32, -s, s), 'W2': jax.random.uniform(ks[5], (E, FF, D), jnp.float32, -sf, sf), 'b2': jax.random.uniform(ks[6], (E, D), jnp.float32, -sf, sf)}
    _L0_ffn_all = _L0_ffn_setup()
    _L0_ffn_in = {k: v for k, v in _L0_ffn_all.items() if k in ('Wg', 'bg', 'W1', 'b1', 'W2', 'b2')}
    del _L0_ffn_all
    return {'x': x, 'L0_tok_emb': _L0_tok_in['emb'], 'L0_tok_wk': _L0_tok_in['wk'], 'L0_tok_bk': _L0_tok_in['bk'], 'L0_tok_wq': _L0_tok_in['wq'], 'L0_tok_bq': _L0_tok_in['bq'], 'L0_tok_wv': _L0_tok_in['wv'], 'L0_tok_bv': _L0_tok_in['bv'], 'L0_tok_ln_g': _L0_tok_in['ln_g'], 'L0_tok_ln_b': _L0_tok_in['ln_b'], 'L0_tok_w1': _L0_tok_in['w1'], 'L0_tok_b1': _L0_tok_in['b1'], 'L0_tok_w2': _L0_tok_in['w2'], 'L0_tok_b2': _L0_tok_in['b2'], 'L0_attn_ln_g': _L0_attn_in['ln_g'], 'L0_attn_ln_b': _L0_attn_in['ln_b'], 'L0_attn_Wh': _L0_attn_in['Wh'], 'L0_attn_bh': _L0_attn_in['bh'], 'L0_attn_Wqk': _L0_attn_in['Wqk'], 'L0_attn_bqk': _L0_attn_in['bqk'], 'L0_attn_gamma': _L0_attn_in['gamma'], 'L0_attn_beta': _L0_attn_in['beta'], 'L0_attn_Wo': _L0_attn_in['Wo'], 'L0_attn_bo': _L0_attn_in['bo'], 'L0_ffn_Wg': _L0_ffn_in['Wg'], 'L0_ffn_bg': _L0_ffn_in['bg'], 'L0_ffn_W1': _L0_ffn_in['W1'], 'L0_ffn_b1': _L0_ffn_in['b1'], 'L0_ffn_W2': _L0_ffn_in['W2'], 'L0_ffn_b2': _L0_ffn_in['b2']}

def reference(x, L0_tok_emb, L0_tok_wk, L0_tok_bk, L0_tok_wq, L0_tok_bq, L0_tok_wv, L0_tok_bv, L0_tok_ln_g, L0_tok_ln_b, L0_tok_w1, L0_tok_b1, L0_tok_w2, L0_tok_b2, L0_attn_ln_g, L0_attn_ln_b, L0_attn_Wh, L0_attn_bh, L0_attn_Wqk, L0_attn_bqk, L0_attn_gamma, L0_attn_beta, L0_attn_Wo, L0_attn_bo, L0_ffn_Wg, L0_ffn_bg, L0_ffn_W1, L0_ffn_b1, L0_ffn_W2, L0_ffn_b2):
    import jax
    import jax.numpy as jnp

    def _L0_tok_ref(input_seq, emb, wk, bk, wq, bq, wv, bv, ln_g, ln_b, w1, b1, w2, b2):
        import jax, jax.numpy as jnp
        import numpy as np
        import math
        V, S, D, B = (50257, 512, 128, 4)
        DFF = 4 * D
        EPS = 1e-05

        def layer_norm(z, g, b):
            mu = jnp.mean(z, axis=-1, keepdims=True)
            var = jnp.mean((z - mu) ** 2, axis=-1, keepdims=True)
            return (z - mu) * jax.lax.rsqrt(var + EPS) * g + b

        def pos_embedding(seq_len, d_model):
            pos = jnp.arange(seq_len, dtype=jnp.float32)[:, None]
            i = jnp.arange(d_model, dtype=jnp.float32)[None, :]
            ang = pos / jnp.power(10000.0, 2.0 * i / d_model)
            even = (jnp.arange(d_model) % 2 == 0)[None, :]
            return jnp.where(even, jnp.sin(ang), jnp.cos(ang))
        x = emb[input_seq]
        x = (x + pos_embedding(S, D)) * math.sqrt(D)
        k = x @ wk + bk
        q = x @ wq + bq
        v = x @ wv + bv
        scores = jnp.einsum('bid,bjd->bij', k, q) / math.sqrt(D)
        attn = jax.nn.softmax(scores, axis=-1) @ v
        r = layer_norm(x + attn, ln_g, ln_b)
        ff = jax.nn.gelu(r @ w1 + b1, approximate=False) @ w2 + b2
        out = layer_norm(r + ff, ln_g, ln_b)
        return out

    def _L0_attn_ref(x, ln_g, ln_b, Wh, bh, Wqk, bqk, gamma, beta, Wo, bo):
        import jax, jax.numpy as jnp
        import numpy as np
        B, S, D = (8, 512, 128)
        QK_DIM = 128
        HID = 2 * D
        EPS = 1e-05

        def _layernorm(x, g, b):
            mu = jnp.mean(x, axis=-1, keepdims=True)
            var = jnp.mean((x - mu) ** 2, axis=-1, keepdims=True)
            return (x - mu) * jax.lax.rsqrt(var + EPS) * g + b
        seq_len = x.shape[-2]
        normed = _layernorm(x, ln_g, ln_b)
        hid = jax.nn.silu(normed @ Wh + bh)
        v, gate = jnp.split(hid, 2, axis=-1)
        Z = jax.nn.silu(normed @ Wqk + bqk)
        QK = Z[..., None, :] * gamma + beta
        q, k = (QK[..., 0, :], QK[..., 1, :])
        sim = jnp.einsum('bid,bjd->bij', q, k) / seq_len
        A = jnp.square(jax.nn.relu(sim))
        V = jnp.einsum('bij,bjd->bid', A, v) * gate
        out = V @ Wo + bo
        return out + x

    def _L0_ffn_ref(x, Wg, bg, W1, b1, W2, b2):
        import jax, jax.numpy as jnp
        import numpy as np
        B, S, D = (8, 512, 128)
        FF = 512
        E = 8
        b, s, d = x.shape
        xf = x.reshape(-1, d)
        logits = xf @ Wg + bg
        probs = jax.nn.softmax(logits, axis=-1)
        pmax = jnp.max(probs, axis=-1)
        routes = jnp.argmax(probs, axis=-1)
        xs = xf * pmax[:, None]
        out_tok = jnp.zeros_like(xf)
        for e in range(E):
            h = jax.nn.relu(xs @ W1[e] + b1[e])
            y = h @ W2[e] + b2[e]
            out_tok = jnp.where((routes == e)[:, None], y, out_tok)
        order = jnp.argsort(routes)
        return out_tok[order].reshape(b, s, d)
    h = _L0_tok_ref(x, L0_tok_emb, L0_tok_wk, L0_tok_bk, L0_tok_wq, L0_tok_bq, L0_tok_wv, L0_tok_bv, L0_tok_ln_g, L0_tok_ln_b, L0_tok_w1, L0_tok_b1, L0_tok_w2, L0_tok_b2)
    h = h + _L0_attn_ref(_layernorm(h, axis=-1), L0_attn_ln_g, L0_attn_ln_b, L0_attn_Wh, L0_attn_bh, L0_attn_Wqk, L0_attn_bqk, L0_attn_gamma, L0_attn_beta, L0_attn_Wo, L0_attn_bo)
    h = h + _L0_ffn_ref(_layernorm(h, axis=-1), L0_ffn_Wg, L0_ffn_bg, L0_ffn_W1, L0_ffn_b1, L0_ffn_W2, L0_ffn_b2)
    return h

_drawn_inputs = setup_inputs


def setup_inputs(seed=0):
    import zlib

    import numpy as np

    out = dict(_drawn_inputs(seed))
    spreads = {'L0_tok_bk': (0.0, 1.512),
     'L0_tok_bq': (0.0, 2.0),
     'L0_tok_bv': (0.0, 0.325),
     'L0_tok_ln_g': (1.0, 0.2),
     'L0_tok_ln_b': (0.0, 0.1),
     'L0_tok_b1': (0.0, 0.1),
     'L0_tok_b2': (0.0, 0.1),
     'L0_attn_ln_g': (1.0, 0.6),
     'L0_attn_ln_b': (0.0, 0.8),
     'L0_attn_bh': (0.0, 0.8),
     'L0_attn_bqk': (0.0, 0.8),
     'L0_attn_beta': (0.0, 0.8),
     'L0_attn_bo': (0.0, 0.1)}
    factors = {'L0_attn_Wh': 8.0,
     'L0_attn_Wqk': 8.0,
     'L0_attn_gamma': 8.0,
     'L0_attn_Wo': 8.0,
     'L0_ffn_bg': 2.866,
     'L0_ffn_b1': 5.616,
     'L0_ffn_b2': 4.651}
    for name, (base, spread) in spreads.items():
        noise = np.random.default_rng([zlib.crc32(name.encode()), seed]).standard_normal(out[name].shape)
        drawn = base * np.exp(spread * noise) if base else spread * noise
        out[name] = jnp.asarray(drawn.astype(out[name].dtype))
    for name, factor in factors.items():
        out[name] = (out[name] * factor).astype(out[name].dtype)
    return out
```

```python
from contextlib import ExitStack

import concourse.bass as bass
import numpy as np
from concourse import mybir

ALU = mybir.AluOpType
ACT = mybir.ActivationFunctionType
AX = mybir.AxisListType.X
F32 = mybir.dt.float32
BF16 = mybir.dt.bfloat16
I32 = mybir.dt.int32
U32 = mybir.dt.uint32

P = 128
VOCAB = 50257
SEQS, S, D = 16, 512, 128
NT = S // P
TILES = SEQS * NT
DFF = 512
NF = DFF // P
HID = 256
NH = HID // P
E = 8
EPS = 1e-5
SCORE_SCALE = float(D) ** -0.5
SIM_SCALE = 1.0 / S

MT = 2
MROWS = MT * P
MTILES = TILES // MT
STEPS = MTILES + E - 1
PAD = MROWS
REGION = SEQS * S + 2 * PAD
TABLE = STEPS + 2
EXPERT = DFF + NF * D + NF

COLS = ["bk", "bq", "g", "b", "b1_0", "b1_1", "b1_2", "b1_3", "ag", "ab", "bqk", "bh_0", "bh_1",
        "gamma_0", "beta_0", "gamma_1", "beta_1"]
ROWS = {}
_at = 0
for _n, _w in (("bv", D), ("g", D), ("b", D), ("b2", D), ("bo", D), ("bhv", HID), ("bg", E), ("moe_b2", E * D)):
    ROWS[_n] = (_at, _w)
    _at += _w
ROWS_W = _at
MATS = {}
_at = 0
for _n, _w in (("wk", D), ("wq", D), ("wv", D), ("w1", DFF), ("w2", NF * D), ("wh", 2 * HID), ("wqk", D),
               ("wo", NH * D), ("wg", E)):
    MATS[_n] = (_at, _w)
    _at += _w
MATS_W = _at
CONST = {}
_at = 0
for _n, _w in (("pos", NT * D), ("ident", P), ("before", P), ("base", E), ("down", E), ("up", E),
               ("row", TILES), ("step", TABLE)):
    CONST[_n] = (_at, _w)
    _at += _w
CONST_W = _at


def build(nc, ins, out):
    with ExitStack() as ctx:
        def sb(name, shape, dt=F32):
            return ctx.enter_context(nc.sbuf_tensor(name, shape, dt))

        def sem(name):
            return ctx.enter_context(nc.semaphore(name))

        routed = nc.dram_tensor("routed_rows", [E * REGION, D], F32, kind="Internal").ap()

        cols = sb("cols", [P, len(COLS)])
        rows_in = sb("rows_in", [P, ROWS_W])
        mats = sb("mats", [P, MATS_W])
        const = sb("const", [P, CONST_W])
        experts = sb("experts", [P, E * EXPERT])
        tokens = sb("tokens", [P, (SEQS + 1) * NT], I32)

        def col(name):
            i = COLS.index(name)
            return cols[:, i:i + 1]

        def row(name):
            at, w = ROWS[name]
            return rows_in[:, at:at + w]

        def mat(name, lo=0, hi=None):
            at, w = MATS[name]
            return mats[:, at + lo:at + (w if hi is None else hi)]

        def cst(name):
            at, w = CONST[name]
            return const[:, at:at + w]

        def over_tiles(ap, n=NT):
            return ap[:, None, :].to_broadcast([P, n, ap.shape[1]])

        ident = cst("ident")
        before_bf = sb("before_bf", [P, P], BF16)
        ones_bf = sb("ones_bf", [P, P], BF16)
        b_b2 = sb("b_b2", [P, D])
        minus_half = sb("minus_half", [P, NT])
        eps = sb("eps", [P, NT])
        zeros = sb("zeros", [P, MT * D])

        token_now = sb("token_now", [P, NT], I32)
        emb = sb("emb_rows", [P, NT, D])
        x = sb("x", [P, NT, D])
        xT = sb("xT", [P, S])
        kT = sb("kT", [P, S])
        qT = sb("qT", [P, S])
        v = sb("v", [P, NT, D])
        neg_max = sb("neg_max", [P, NT])
        exp_sum = sb("exp_sum", [P, NT])
        exp_inv = sb("exp_inv", [P, NT])
        probs_buf = sb("probs", [P, 2 * EXPERT])
        probs = probs_buf[:, 0:NT * S].rearrange("p (t s) -> p t s", s=S)
        probsT = sb("probsT", [P, NT, S])
        z1 = sb("z1", [P, NT, D])
        r_hat = sb("r_hat", [P, NT, D])
        r_scaled = sb("r_scaled", [P, NT, D])
        r_res = sb("r_res", [P, NT, D])
        rT = sb("rT", [P, S])
        geluT = sb("geluT", [P, NF, S])
        z2 = sb("z2", [P, NT, D])
        h_hat = sb("h_hat", [P, NT, D])
        h_scaled = sb("h_scaled", [P, NT, D])
        h = sb("h", [P, NT, D])
        y = sb("y", [P, NT, D])
        n = sb("n", [P, NT, D])
        hy = sb("hy", [P, NT, D])
        hy_bo = sb("hy_bo", [P, NT, D])
        nT = sb("nT", [P, S])
        zT = sb("zT", [P, S])
        sqT = sb("sqT", [P, S])
        skT = sb("skT", [P, S])
        gateT = sb("gateT", [P, NH, S])
        v_pre = sb("v_pre", [P, NT, HID])
        gv = sb("gv", [P, NT, HID])
        relu = sb("relu", [P, NT, S])
        aT = sb("aT", [P, NT, S])
        gatedT = sb("gatedT", [P, NH, S])
        h2 = sb("h2", [P, TILES, D])
        h2_now = sb("h2_now", [P, NT, D])
        y2 = sb("y2", [P, NT, D])
        y2T = sb("y2T", [P, S])
        xs = sb("xs", [P, NT, D])
        stats = {k: sb(f"stats{k}", [P, NT, 6]) for k in (1, 2, 3, 5)}
        mv = {k: sb(f"mv{k}", [P, NT, 2]) for k in (1, 2, 3, 5)}
        var_eps = {k: sb(f"var_eps{k}", [P, NT]) for k in (1, 2, 3, 5)}
        rstd = {k: sb(f"rstd{k}", [P, NT]) for k in (1, 2, 3, 5)}
        n_tmp = sb("n_tmp", [P, 4, NT])
        n_rstd = sb("n_rstd", [P, NT])
        logits = sb("logits", [P, NT, E])
        lmax = sb("lmax", [P, NT])
        lshift = sb("lshift", [P, NT, E])
        lexp = sb("lexp", [P, NT, E])
        lsum = sb("lsum", [P, NT])
        pmax = sb("pmax", [P, NT])
        is_max = sb("is_max", [P, NT, E])
        ranked = sb("ranked", [P, NT, E])
        best = sb("best", [P, NT])
        route = sb("route", [P, NT, E])
        route_bf = sb("route_bf", [P, NT, E], BF16)
        filled = sb("filled", [P, E])
        slot_all = sb("slot_all", [P, NT, E])
        slot_own = sb("slot_own", [P, NT, E])
        slot = sb("slot", [P, NT])
        slot_u = sb("slot_u", [P, NT], U32)
        count = sb("count", [P, E])
        start = sb("start", [P, E])
        end = sb("end", [P, E])
        pl = sb("plan_tmp", [P, 8, E])
        pli = sb("plan_int", [P, 2, E], I32)
        po = geluT[:].rearrange("p f s -> p (f s)")[:, 0:6 * TABLE * E].rearrange(
            "p (i s e) -> p i s e", s=TABLE, e=E)
        pv = sb("plan_cols", [P, 6, TABLE])
        table = sb("table", [P, TABLE, 4], I32)
        tail = sb("tail", [P, E], I32)
        own = sb("own", [P, E + 1, TILES])
        own2 = sb("own2", [P, E, TILES])
        m_rows = probsT[:, 0].rearrange("p (u t d) -> p u t d", u=2, t=MT)
        m_xT = probsT[:, 1].rearrange("p (u r) -> p u r", u=2)
        m_w = probs_buf[:].rearrange("p (u w) -> p u w", u=2)
        m_hT = relu[:].rearrange("p t (a r) -> p t a r", r=MROWS).rearrange("p (u t) a r -> p u (t a) r", u=2)
        m_y = probsT[:, 2].rearrange("p (u t d) -> p u t d", u=2, t=MT)

        bank = [ctx.enter_context(nc.psum_tensor(f"bank{i}", [P, 512], F32)) for i in range(8)]
        ta, gb = bank[:4], bank[4:]

        loaded = sem("loaded")
        prepared = sem("prepared")
        prepared_pool = sem("prepared_pool")
        token_ready = sem("token_ready")
        emb_ready = sem("emb_ready")
        x_ready = sem("x_ready")
        xT_psum = sem("xT_psum"); xT_ready = sem("xT_ready")
        k_psum = sem("k_psum"); q_psum = sem("q_psum"); v_psum = sem("v_psum")
        kqv_ready = sem("kqv_ready")
        score_psum = sem("score_psum")
        max_ready = sem("max_ready")
        probs_ready = sem("probs_ready")
        probsT_psum = sem("probsT_psum")
        probsT_dve = sem("probsT_dve")
        probsT_act = sem("probsT_act")
        attn_psum = sem("attn_psum")
        inv_ready = sem("inv_ready")
        z1_ready = sem("z1_ready")
        stats_ready = {k: sem(f"stats{k}_ready") for k in (1, 2, 3, 5)}
        mv_ready = {k: sem(f"mv{k}_ready") for k in (1, 2, 3, 5)}
        var_ready = {k: sem(f"var{k}_ready") for k in (1, 2, 3, 5)}
        rstd_ready = {k: sem(f"rstd{k}_ready") for k in (1, 2, 3, 5)}
        rhat_ready = sem("rhat_ready")
        rscaled_ready = sem("rscaled_ready"); rres_ready = sem("rres_ready")
        rT_psum = sem("rT_psum"); rT_ready = sem("rT_ready")
        ff_psum = sem("ff_psum")
        gelu_ready = sem("gelu_ready")
        out_psum = sem("out_psum")
        z2_ready = sem("z2_ready")
        hhat_ready = sem("hhat_ready")
        hscaled_ready = sem("hscaled_ready"); h_ready = sem("h_ready")
        nstd_step = sem("nstd_step")
        y_ready = sem("y_ready")
        n_ready = sem("n_ready")
        hy_ready = sem("hy_ready")
        nT_psum = sem("nT_psum"); nT_ready = sem("nT_ready")
        z_psum = sem("z_psum"); z_ready = sem("z_ready")
        gate_psum = sem("gate_psum"); gate_ready = sem("gate_ready")
        gv_psum = sem("gv_psum"); vpre_ready = sem("vpre_ready"); gv_ready = sem("gv_ready")
        sqk_ready = sem("sqk_ready")
        sim_psum = sem("sim_psum")
        relu_ready = sem("relu_ready")
        aT_pool = sem("aT_pool"); aT_act = sem("aT_act")
        mix_psum = sem("mix_psum"); gated_ready = sem("gated_ready")
        wo_psum = sem("wo_psum"); h2_ready = sem("h2_ready"); h2_kept = sem("h2_kept")
        y2_ready = sem("y2_ready")
        y2T_psum = sem("y2T_psum"); y2T_ready = sem("y2T_ready")
        logit_psum = sem("logit_psum")
        logits_ready = sem("logits_ready")
        route_step = sem("route_step")
        lexp_ready = sem("lexp_ready")
        pmax_step = sem("pmax_step")
        rank_psum = sem("rank_psum")
        slot_step = sem("slot_step")
        xs_ready = sem("xs_ready")
        scattered = sem("scattered")
        padded = sem("padded")
        plan_step = sem("plan_step")
        plan_ready = sem("plan_ready")
        m_loaded = [sem(f"m_loaded{u}") for u in range(2)]
        m_w_ready = [sem(f"m_w_ready{u}") for u in range(2)]
        m_xT_psum = [sem(f"m_xT_psum{u}") for u in range(2)]
        m_xT_ready = [sem(f"m_xT_ready{u}") for u in range(2)]
        m_h_psum = [sem(f"m_h_psum{u}") for u in range(2)]
        m_h_ready = [sem(f"m_h_ready{u}") for u in range(2)]
        m_y_psum = [sem(f"m_y_psum{u}") for u in range(2)]
        m_y_ready = [sem(f"m_y_ready{u}") for u in range(2)]
        m_added = sem("m_added")
        m_stored = sem("m_stored")

        ROUTE = 6
        LOADS = 6

        waited = {e: sem(f"waited_{e}") for e in ("sp", "pool", "dve")}

        def later(i):
            return not (isinstance(i, int) and i <= 0)

        def apart(eng, name):
            eng.sem_inc(waited[name], 1)

        block = ctx.enter_context(nc.Block())

        @block.sync
        def _(sp):
            sp.dma_start(tokens[:], ins["tokens"]).then_inc(loaded, 16)
            sp.dma_start(const[:], ins["const"]).then_inc(loaded, 16)
            sp.dma_start(mats[:], ins["mats"]).then_inc(loaded, 16)
            sp.dma_start(cols[:], ins["cols"]).then_inc(loaded, 16)
            sp.dma_start(rows_in[:], ins["rows"].partition_broadcast(P)).then_inc(loaded, 16)
            sp.dma_start(experts[:], ins["experts"]).then_inc(loaded, 16)
            sp.wait_ge(prepared_pool, 2)
            for e in range(E):
                sp.dma_start(routed[e * REGION:e * REGION + PAD, :].rearrange("(t p) d -> p t d", p=P),
                             zeros[:].rearrange("p (t d) -> p t d", d=D)).then_inc(padded, 16)
            sp.wait_ge(plan_ready, 1)
            for e in range(E):
                at = sp.value_load(tail[0:1, e:e + 1], min_val=e * REGION + PAD, max_val=(e + 1) * REGION - PAD)
                sp.dma_start(routed[bass.ds(at, PAD), :].rearrange("(t p) d -> p t d", p=P),
                             zeros[:].rearrange("p (t d) -> p t d", d=D)).then_inc(padded, 16)
            sp.wait_ge(padded, 2 * E * 16)
            sp.wait_ge(scattered, SEQS * NT * 16)

            def load(s, i, u):
                at = sp.value_load(table[0:1, s, 0:1], min_val=0, max_val=E * REGION - MROWS)
                if later(i):
                    sp.wait_ge(m_xT_psum[u], i)
                apart(sp, "sp")
                sp.dma_start(m_rows[:, u], routed[bass.ds(at, MROWS), :].rearrange("(t p) d -> p t d", p=P)
                             ).then_inc(m_loaded[u], 16)

            def store(s):
                j = sp.value_load(table[0:1, s, 3:4], min_val=0, max_val=MTILES - 1)
                sp.wait_ge(m_added, MT * s + MT)
                apart(sp, "sp")
                if later(s):
                    sp.wait_ge(m_stored, 16 * s)
                apart(sp, "sp")
                sp.dma_start(out[bass.ds(j * MROWS, MROWS), :].rearrange("(t p) d -> p t d", p=P),
                             h2[:, bass.ds(j * MT, MT), :]).then_inc(m_stored, 16)

            load(0, 0, 0)
            load(1, 0, 1)
            def pair(i):
                load(2 * i + 2, i + 1, 0)
                store(2 * i)
                load(2 * i + 3, i + 1, 1)
                store(2 * i + 1)

            pair(0)
            with sp.Fori(1, STEPS // 2) as i:
                pair(i)
            store(STEPS - 1)
            sp.wait_ge(m_stored, 16 * STEPS)
            sp.wait_ge(m_loaded[1], 16 * (STEPS // 2 + 1))

        @block.gpsimd
        def _(pool):
            nc.gpsimd.memset(minus_half[:], -0.5).then_inc(prepared_pool, 1)
            nc.gpsimd.memset(zeros[:], 0.0).then_inc(prepared_pool, 1)
            nc.gpsimd.memset(eps[:], EPS).then_inc(prepared_pool, 1)
            pool.wait_ge(loaded, 16 * LOADS)
            nc.gpsimd.tensor_tensor(b_b2[:], row("b"), row("b2"), ALU.add).then_inc(prepared_pool, 1)
            pool.wait_ge(prepared_pool, 4)

            def gather(i):
                if later(i):
                    pool.wait_ge(x_ready, i)
                apart(pool, "pool")
                nc.gpsimd.tensor_copy(token_now[:], tokens[:, bass.ds(i * NT, NT)]).then_inc(token_ready, 1)
                pool.wait_ge(token_ready, i + 1)
                apart(pool, "pool")
                for t in range(NT):
                    nc.gpsimd.indirect_dma_start(
                        out=emb[:, t, :], out_offset=None, in_=ins["emb"],
                        in_offset=bass.IndirectOffsetOnAxis(ap=token_now[:, t:t + 1].bitcast(U32), axis=0),
                        bounds_check=VOCAB - 1, oob_is_err=False).then_inc(emb_ready, 16)

            def inv_std(i, k):
                pool.wait_ge(mv_ready[k], NT * i + NT)
                nc.gpsimd.tensor_tensor(var_eps[k][:], mv[k][:, :, 1], eps[:], ALU.add).then_inc(var_ready[k], 1)
                pool.wait_ge(var_ready[k], i + 1)
                nc.gpsimd.tensor_tensor(rstd[k][:], var_eps[k][:], minus_half[:], ALU.pow
                                        ).then_inc(rstd_ready[k], 1)

            def tok_residual(a):
                pool.wait_ge(rhat_ready, NT * a + NT)
                nc.gpsimd.tensor_tensor(r_scaled[:], r_hat[:], over_tiles(row("g")), ALU.mult
                                        ).then_inc(rscaled_ready, 1)
                pool.wait_ge(rscaled_ready, a + 1)
                if later(a):
                    pool.wait_ge(z2_ready, a)
                nc.gpsimd.tensor_tensor(r_res[:], r_scaled[:], over_tiles(b_b2[:]), ALU.add
                                        ).then_inc(rres_ready, 1)

            def gau_norms(b):
                inv_std(b, 2)
                pool.wait_ge(hhat_ready, NT * b + NT)
                nc.gpsimd.tensor_tensor(h_scaled[:], h_hat[:], over_tiles(row("g")), ALU.mult
                                        ).then_inc(hscaled_ready, 1)
                pool.wait_ge(hscaled_ready, b + 1)
                nc.gpsimd.tensor_tensor(h[:], h_scaled[:], over_tiles(row("b")), ALU.add).then_inc(h_ready, 1)
                inv_std(b, 3)
                pool.wait_ge(rstd_ready[3], b + 1)
                t = n_tmp
                nc.gpsimd.tensor_tensor(t[:, 0], rstd[3][:], rstd[3][:], ALU.mult).then_inc(nstd_step, 1)
                pool.wait_ge(nstd_step, 5 * b + 1)
                nc.gpsimd.tensor_tensor(t[:, 1], t[:, 0], mv[3][:, :, 1], ALU.mult).then_inc(nstd_step, 1)
                pool.wait_ge(nstd_step, 5 * b + 2)
                nc.gpsimd.tensor_tensor(t[:, 2], t[:, 1], eps[:], ALU.add).then_inc(nstd_step, 1)
                pool.wait_ge(nstd_step, 5 * b + 3)
                nc.gpsimd.tensor_tensor(t[:, 3], t[:, 2], minus_half[:], ALU.pow).then_inc(nstd_step, 1)
                pool.wait_ge(nstd_step, 5 * b + 4)
                nc.gpsimd.tensor_tensor(n_rstd[:], t[:, 3], rstd[3][:], ALU.mult).then_inc(nstd_step, 1)

            def gau_residual(b):
                pool.wait_ge(y_ready, NT * b + NT)
                nc.gpsimd.tensor_tensor(hy[:], h[:], y[:], ALU.add).then_inc(hy_ready, 1)
                pool.wait_ge(hy_ready, 2 * b + 1)
                nc.gpsimd.tensor_tensor(hy_bo[:], hy[:], over_tiles(row("bo")), ALU.add).then_inc(hy_ready, 1)

            def keep_h2(b):
                pool.wait_ge(h2_ready, b + 1)
                apart(pool, "pool")
                nc.gpsimd.tensor_copy(h2[:, bass.ds(b * NT, NT), :], h2_now[:]).then_inc(h2_kept, 1)

            def gau_square(b):
                for j in range(NT // 2):
                    pool.wait_ge(relu_ready, NT * b + j + 1)
                    nc.gpsimd.tensor_tensor(aT[:, j], relu[:, j], relu[:, j], ALU.mult).then_inc(aT_pool, 1)

            def gau_scatter(b):
                pool.wait_ge(pmax_step, 2 * b + 2)
                if later(b):
                    pool.wait_ge(scattered, 16 * NT * b)
                nc.gpsimd.tensor_tensor(xs[:], y2[:], pmax[:, :, None].to_broadcast([P, NT, D]), ALU.mult
                                        ).then_inc(xs_ready, 1)
                pool.wait_ge(xs_ready, b + 1)
                pool.wait_ge(slot_step, 5 * b + 5)
                apart(pool, "pool")
                for t in range(NT):
                    nc.gpsimd.indirect_dma_start(
                        out=routed, out_offset=bass.IndirectOffsetOnAxis(ap=slot_u[:, t:t + 1], axis=0),
                        in_=xs[:, t, :], in_offset=None, bounds_check=E * REGION - 1, oob_is_err=False,
                    ).then_inc(scattered, 16)

            gather(0)
            gather(1)
            inv_std(0, 1)
            tok_residual(0)
            def both(a):
                b = a - 1
                gather(a + 1)
                gau_norms(b)
                gau_residual(b)
                gau_square(b)
                inv_std(a, 1)
                tok_residual(a)
                keep_h2(b)
                inv_std(b, 5)
                gau_scatter(b)

            both(1)
            with pool.Fori(2, SEQS) as a:
                both(a)
            b = SEQS - 1
            gau_norms(b)
            gau_residual(b)
            gau_square(b)
            keep_h2(b)
            inv_std(b, 5)
            gau_scatter(b)
            pool.wait_ge(emb_ready, 16 * NT * (SEQS + 1))

            def expert_in(s, i, u):
                e = pool.value_load(table[0:1, s, 1:2], min_val=0, max_val=E - 1)
                if later(i):
                    pool.wait_ge(m_y_psum[u], i)
                apart(pool, "pool")
                nc.gpsimd.tensor_copy(m_w[:, u], experts[:, bass.ds(e * EXPERT, EXPERT)]).then_inc(m_w_ready[u], 1)

            pool.wait_ge(plan_ready, 1)
            def pair(i):
                expert_in(2 * i, i, 0)
                expert_in(2 * i + 1, i, 1)

            pair(0)
            with pool.Fori(1, STEPS // 2) as i:
                pair(i)
            expert_in(STEPS - 1, STEPS // 2, 0)

        @block.scalar
        def _(act):
            act.wait_ge(loaded, 16 * LOADS)

            def tok_xT(a):
                act.wait_ge(xT_psum, a + 1)
                nc.scalar.copy(xT[:], ta[0][:]).then_inc(xT_ready, 1)

            def tok_exp(a):
                for c in range(NT):
                    act.wait_ge(max_ready, NT * a + c + 1)
                    nc.scalar.activation(probs[:, c], ta[c][:], ACT.Exp, bias=neg_max[:, c:c + 1],
                                         accum_out=exp_sum[:, c:c + 1]).then_inc(probs_ready, 1)

            def tok_probsT(a):
                for j in range(NT // 2, NT):
                    act.wait_ge(probsT_psum, NT * a + j + 1)
                    nc.scalar.copy(probsT[:, j], ta[j][:]).then_inc(probsT_act, 1)

            def tok_rT(a):
                act.wait_ge(rT_psum, a + 1)
                nc.scalar.activation(rT[:], ta[1][:], ACT.Identity, bias=col("b"), scale=col("g")
                                     ).then_inc(rT_ready, 1)

            def tok_gelu(a):
                for f in range(NF):
                    act.wait_ge(ff_psum, NF * a + f + 1)
                    nc.scalar.activation(geluT[:, f], ta[(f + 2) % 4][:], ACT.Gelu, bias=col(f"b1_{f}")
                                         ).then_inc(gelu_ready, 1)

            def gau_nT(b):
                act.wait_ge(nT_psum, b + 1)
                nc.scalar.activation(nT[:], gb[0][:], ACT.Identity, bias=col("ab"), scale=col("ag")
                                     ).then_inc(nT_ready, 1)

            def gau_silu(b):
                act.wait_ge(z_psum, b + 1)
                nc.scalar.activation(zT[:], gb[1][:], ACT.Silu, bias=col("bqk")).then_inc(z_ready, 1)
                for g in range(NH):
                    act.wait_ge(gate_psum, NH * b + g + 1)
                    nc.scalar.activation(gateT[:, g], gb[2 + g][:], ACT.Silu, bias=col(f"bh_{g}")
                                         ).then_inc(gate_ready, 1)
                for i in range(2):
                    act.wait_ge(vpre_ready, 2 * b + i + 1)
                    nc.scalar.activation(gv[:, 2 * i:2 * i + 2, :], v_pre[:, 2 * i:2 * i + 2, :], ACT.Silu
                                         ).then_inc(gv_ready, 1)

            def gau_square(b):
                for j in range(NT // 2, NT):
                    act.wait_ge(relu_ready, NT * b + j + 1)
                    nc.scalar.activation(aT[:, j], relu[:, j], ACT.Square).then_inc(aT_act, 1)

            def gau_y2T(b):
                act.wait_ge(y2T_psum, b + 1)
                nc.scalar.copy(y2T[:], gb[1][:]).then_inc(y2T_ready, 1)

            def gau_lexp(b):
                act.wait_ge(route_step, ROUTE * b + 2)
                nc.scalar.activation(lexp[:], lshift[:], ACT.Exp).then_inc(lexp_ready, 1)

            tok_xT(0)
            tok_exp(0)
            tok_probsT(0)
            tok_rT(0)
            tok_gelu(0)
            def both(a):
                b = a - 1
                tok_xT(a)
                tok_exp(a)
                gau_nT(b)
                gau_silu(b)
                tok_probsT(a)
                gau_square(b)
                tok_rT(a)
                tok_gelu(a)
                gau_y2T(b)
                gau_lexp(b)

            both(1)
            with act.Fori(2, SEQS) as a:
                both(a)
            b = SEQS - 1
            gau_nT(b)
            gau_silu(b)
            gau_square(b)
            gau_y2T(b)
            gau_lexp(b)

            def expert_hidden(i, u):
                act.wait_ge(m_xT_psum[u], i + 1)
                nc.scalar.copy(m_xT[:, u], bank[u][:, 0:MROWS]).then_inc(m_xT_ready[u], 1)
                act.wait_ge(m_w_ready[u], i + 1)
                for f in range(NF):
                    act.wait_ge(m_h_psum[u], NF // 2 * i + f // 2 + 1)
                    at = (f % 2) * MROWS
                    nc.scalar.activation(m_hT[:, u, f], bank[2 + 2 * u + f // 2][:, at:at + MROWS], ACT.Relu,
                                         bias=m_w[:, u, EXPERT - NF + f:EXPERT - NF + f + 1]
                                         ).then_inc(m_h_ready[u], 1)

            def pair(i):
                expert_hidden(i, 0)
                expert_hidden(i, 1)

            pair(0)
            with act.Fori(1, STEPS // 2) as i:
                pair(i)
            expert_hidden(STEPS // 2, 0)

        @block.vector
        def _(dve):
            dve.wait_ge(loaded, 16 * LOADS)
            nc.vector.tensor_copy(before_bf[:], cst("before")).then_inc(prepared, 1)
            nc.vector.memset(ones_bf[:], 1.0).then_inc(prepared, 1)
            nc.vector.tensor_copy(filled[:], cst("base")).then_inc(prepared, 1)

            def embed(i):
                dve.wait_ge(emb_ready, 16 * NT * (i + 1))
                if later(i):
                    dve.wait_ge(xT_psum, i)
                nc.vector.scalar_tensor_tensor(
                    x[:].rearrange("p t d -> p (t d)"), emb[:].rearrange("p t d -> p (t d)"), float(D) ** 0.5,
                    cst("pos"), ALU.mult, ALU.add).then_inc(x_ready, 1)

            def norm_stats(i, k, src, ready, n_ready_):
                for t in range(NT):
                    dve.wait_ge(ready, n_ready_(t))
                    nc.vector.bn_stats(stats[k][:, t], src(t)).then_inc(stats_ready[k], 1)
                dve.wait_ge(stats_ready[k], NT * i + NT)
                apart(dve, "dve")
                for t in range(NT):
                    nc.vector.bn_aggr(mv[k][:, t], stats[k][:, t]).then_inc(mv_ready[k], 1)

            def norm_apply(k, dst, src, scale, done):
                for t in range(NT):
                    nc.vector.tensor_scalar(dst[:, t], src(t), mv[k][:, t, 0:1], scale[:, t:t + 1],
                                            ALU.subtract, ALU.mult).then_inc(done, 1)

            def tok_kqv(a):
                dve.wait_ge(k_psum, a + 1)
                nc.vector.tensor_scalar(kT[:], ta[1][:], col("bk"), SCORE_SCALE, ALU.add, ALU.mult
                                        ).then_inc(kqv_ready, 1)
                dve.wait_ge(q_psum, a + 1)
                nc.vector.tensor_scalar(qT[:], ta[3][:], col("bq"), None, ALU.add).then_inc(kqv_ready, 1)
                dve.wait_ge(v_psum, a + 1)
                nc.vector.tensor_tensor(v[:], ta[2][:].rearrange("p (t d) -> p t d", d=D), over_tiles(row("bv")),
                                        ALU.add).then_inc(kqv_ready, 1)

            def tok_max(a, c):
                dve.wait_ge(score_psum, NT * a + c + 1)
                nc.vector.reduce_max(neg_max[:, c:c + 1], ta[c][:], AX, negate=True).then_inc(max_ready, 1)

            def tok_probsT(a):
                for j in range(NT // 2):
                    dve.wait_ge(probsT_psum, NT * a + j + 1)
                    nc.vector.tensor_copy(probsT[:, j], ta[j][:]).then_inc(probsT_dve, 1)

            def tok_norm1(a):
                dve.wait_ge(probs_ready, NT * a + NT)
                nc.vector.reciprocal(exp_inv[:], exp_sum[:]).then_inc(inv_ready, 1)
                dve.wait_ge(attn_psum, a + 1)
                dve.wait_ge(inv_ready, a + 1)
                for t in range(NT):
                    nc.vector.scalar_tensor_tensor(z1[:, t], ta[0][:, t * D:(t + 1) * D], exp_inv[:, t:t + 1],
                                                   x[:, t], ALU.mult, ALU.add).then_inc(z1_ready, 1)
                norm_stats(a, 1, lambda t: z1[:, t], z1_ready, lambda t: NT * a + t + 1)

            def tok_apply1(a):
                dve.wait_ge(rstd_ready[1], a + 1)
                if later(a):
                    dve.wait_ge(rres_ready, a)
                norm_apply(1, r_hat, lambda t: z1[:, t], rstd[1], rhat_ready)

            def tok_norm2(a):
                dve.wait_ge(out_psum, a + 1)
                dve.wait_ge(rres_ready, a + 1)
                nc.vector.tensor_tensor(z2[:], ta[2][:].rearrange("p (t d) -> p t d", d=D), r_res[:], ALU.add
                                        ).then_inc(z2_ready, 1)
                norm_stats(a, 2, lambda t: z2[:, t], z2_ready, lambda t: a + 1)

            def gau_hhat(b):
                dve.wait_ge(rstd_ready[2], b + 1)
                norm_apply(2, h_hat, lambda t: z2[:, t], rstd[2], hhat_ready)

            def gau_norm3(b):
                norm_stats(b, 3, lambda t: h[:, t], h_ready, lambda t: b + 1)

            def gau_n(b):
                dve.wait_ge(nstd_step, 5 * b + 5)
                norm_apply(3, n, lambda t: h[:, t], n_rstd, n_ready)
                norm_apply(3, y, lambda t: h[:, t], rstd[3], y_ready)

            def gau_sqk(b):
                dve.wait_ge(z_ready, b + 1)
                for k, t in ((0, sqT), (1, skT)):
                    nc.vector.tensor_scalar(t[:], zT[:], col(f"gamma_{k}"), col(f"beta_{k}"), ALU.mult, ALU.add
                                            ).then_inc(sqk_ready, 1)

            def gau_vpre(b):
                for i in range(2):
                    dve.wait_ge(gv_psum, 2 * b + i + 1)
                    nc.vector.tensor_tensor(v_pre[:, 2 * i:2 * i + 2, :],
                                            gb[i][:].rearrange("p (t d) -> p t d", d=HID),
                                            over_tiles(row("bhv"), 2), ALU.add).then_inc(vpre_ready, 1)

            def gau_relu(b):
                for j in range(NT):
                    dve.wait_ge(sim_psum, NT * b + j + 1)
                    nc.vector.tensor_scalar(relu[:, j], gb[(j + 2) % 4][:], 0.0, SIM_SCALE, ALU.max, ALU.mult
                                            ).then_inc(relu_ready, 1)

            def gau_gated(b):
                for g in range(NH):
                    dve.wait_ge(mix_psum, NH * b + g + 1)
                    nc.vector.tensor_tensor(gatedT[:, g], gb[2 + g][:], gateT[:, g], ALU.mult
                                            ).then_inc(gated_ready, 1)

            def gau_h2(b):
                dve.wait_ge(wo_psum, b + 1)
                dve.wait_ge(hy_ready, 2 * b + 2)
                if later(b):
                    dve.wait_ge(h2_kept, b)
                nc.vector.tensor_tensor(h2_now[:], gb[0][:].rearrange("p (t d) -> p t d", d=D),
                                        hy_bo[:], ALU.add).then_inc(h2_ready, 1)
                norm_stats(b, 5, lambda t: h2_now[:, t], h2_ready, lambda t: b + 1)

            def gau_y2(b):
                dve.wait_ge(rstd_ready[5], b + 1)
                if later(b):
                    dve.wait_ge(xs_ready, b)
                norm_apply(5, y2, lambda t: h2_now[:, t], rstd[5], y2_ready)

            def each(ap):
                return ap[:, :, None].to_broadcast([P, NT, E])

            def gau_route(b):
                done = ROUTE * b
                dve.wait_ge(logit_psum, b + 1)
                nc.vector.tensor_tensor(logits[:], gb[2][:, 0:NT * E].rearrange("p (t e) -> p t e", e=E),
                                        over_tiles(row("bg")), ALU.add).then_inc(logits_ready, 1)
                dve.wait_ge(logits_ready, b + 1)
                nc.vector.reduce_max(lmax[:], logits[:], AX).then_inc(route_step, 1)
                dve.wait_ge(route_step, done + 1)
                nc.vector.tensor_tensor(lshift[:], logits[:], each(lmax), ALU.subtract).then_inc(route_step, 1)
                nc.vector.tensor_tensor(is_max[:], logits[:], each(lmax), ALU.is_equal).then_inc(route_step, 1)
                dve.wait_ge(route_step, done + 3)
                nc.vector.tensor_tensor(ranked[:], is_max[:], over_tiles(cst("down")), ALU.mult
                                        ).then_inc(route_step, 1)
                dve.wait_ge(route_step, done + 4)
                nc.vector.reduce_max(best[:], ranked[:], AX).then_inc(route_step, 1)
                dve.wait_ge(route_step, done + 5)
                if later(b):
                    dve.wait_ge(rank_psum, b)
                nc.vector.tensor_tensor(route_bf[:], ranked[:], each(best), ALU.is_equal).then_inc(route_step, 1)
                dve.wait_ge(lexp_ready, b + 1)
                nc.vector.reduce_sum(lsum[:], lexp[:], AX).then_inc(pmax_step, 1)
                dve.wait_ge(pmax_step, 2 * b + 1)
                nc.vector.reciprocal(pmax[:], lsum[:]).then_inc(pmax_step, 1)

            def gau_slot(b):
                done = 5 * b
                dve.wait_ge(rank_psum, b + 1)
                dve.wait_ge(route_step, ROUTE * b + 6)
                nc.vector.tensor_tensor(slot_all[:], gb[3][:, 0:NT * E].rearrange("p (t e) -> p t e", e=E),
                                        over_tiles(filled[:]), ALU.add).then_inc(slot_step, 1)
                dve.wait_ge(slot_step, done + 1)
                nc.vector.tensor_tensor(filled[:], gb[3][:, NT * E:(NT + 1) * E], filled[:], ALU.add
                                        ).then_inc(slot_step, 1)
                nc.vector.tensor_tensor(slot_own[:], slot_all[:], route_bf[:], ALU.mult).then_inc(slot_step, 1)
                dve.wait_ge(slot_step, done + 3)
                nc.vector.reduce_sum(slot[:], slot_own[:], AX).then_inc(slot_step, 1)
                dve.wait_ge(slot_step, done + 4)
                if later(b):
                    dve.wait_ge(scattered, 16 * NT * b)
                nc.vector.tensor_copy(slot_u[:], slot[:]).then_inc(slot_step, 1)

            embed(0)
            tok_kqv(0)
            for c in range(NT):
                tok_max(0, c)
            tok_probsT(0)
            tok_norm1(0)
            tok_apply1(0)
            embed(1)
            tok_norm2(0)
            def both(a):
                b = a - 1
                tok_kqv(a)
                gau_hhat(b)
                tok_max(a, 0)
                tok_max(a, 1)
                gau_norm3(b)
                tok_max(a, 2)
                tok_max(a, 3)
                gau_n(b)
                gau_sqk(b)
                gau_vpre(b)
                tok_probsT(a)
                gau_relu(b)
                tok_norm1(a)
                tok_apply1(a)
                embed(a + 1)
                gau_gated(b)
                gau_h2(b)
                gau_y2(b)
                tok_norm2(a)
                gau_route(b)
                gau_slot(b)

            both(1)
            with dve.Fori(2, SEQS) as a:
                both(a)
            b = SEQS - 1
            gau_hhat(b)
            gau_norm3(b)
            gau_n(b)
            gau_sqk(b)
            gau_vpre(b)
            gau_relu(b)
            gau_gated(b)
            gau_h2(b)
            gau_y2(b)
            gau_route(b)
            gau_slot(b)

            steps = [0]

            def then(ins_):
                steps[0] += 1
                ins_.then_inc(plan_step, 1)
                dve.wait_ge(plan_step, steps[0])

            V = nc.vector
            dve.wait_ge(slot_step, 5 * SEQS)
            then(V.tensor_tensor(count[:], filled[:], cst("base"), ALU.subtract))
            then(V.memset(start[:, 0:1], 0.0))
            for e in range(1, E):
                then(V.tensor_tensor(start[:, e:e + 1], start[:, e - 1:e], count[:, e - 1:e], ALU.add))
            then(V.tensor_tensor(end[:], start[:], count[:], ALU.add))
            used, first, last, ntile, since, until, shift, rowat = (pl[:, i] for i in range(8))
            then(V.tensor_scalar(used, count[:], 0.0, None, ALU.is_gt))
            then(V.tensor_scalar(last, end[:], -1.0, 0.0, ALU.add, ALU.max))
            bits = MROWS.bit_length() - 1
            for src, at, dst in ((start[:], 0, first), (last, 1, last)):
                then(V.tensor_copy(pli[:, at], src))
                then(V.tensor_scalar(pli[:, at], pli[:, at], bits, None, ALU.logical_shift_right))
                then(V.tensor_copy(dst, pli[:, at]))
            then(V.tensor_tensor(ntile, last, first, ALU.subtract))
            then(V.tensor_scalar(ntile, ntile, 1.0, None, ALU.add))
            then(V.tensor_tensor(ntile, ntile, used, ALU.mult))
            then(V.memset(since[:, 0:1], 0.0))
            for e in range(1, E):
                then(V.tensor_tensor(since[:, e:e + 1], since[:, e - 1:e], ntile[:, e - 1:e], ALU.add))
            then(V.tensor_tensor(until, since, ntile, ALU.add))
            then(V.tensor_tensor(shift, first, since, ALU.subtract))
            then(V.tensor_tensor(rowat, cst("base"), start[:], ALU.subtract))

            def by_step(ap):
                return ap[:, None, :].to_broadcast([P, TABLE, E])

            step_no = cst("step")
            step_e = step_no[:, :, None].to_broadcast([P, TABLE, E])
            of, ge, a_, b_, c_, _ = (po[:, i] for i in range(6))
            valid, expert, jshift, j, r0, m0 = (pv[:, i] for i in range(6))
            then(V.tensor_tensor(ge, step_e, by_step(since), ALU.is_ge))
            then(V.tensor_tensor(of, step_e, by_step(until), ALU.is_lt))
            then(V.tensor_tensor(of, of, ge, ALU.mult))
            then(V.reduce_sum(valid, of, AX))
            then(V.tensor_tensor(a_, of, by_step(cst("up")), ALU.mult))
            then(V.reduce_sum(expert, a_, AX))
            then(V.tensor_tensor(b_, of, by_step(shift), ALU.mult))
            then(V.reduce_sum(jshift, b_, AX))
            then(V.tensor_tensor(c_, of, by_step(rowat), ALU.mult))
            then(V.reduce_sum(r0, c_, AX))
            then(V.tensor_tensor(j, step_no, jshift, ALU.add))
            then(V.tensor_scalar(j, j, -float(MTILES - 1), None, ALU.add))
            then(V.tensor_tensor(j, j, valid, ALU.mult))
            then(V.tensor_scalar(j, j, float(MTILES - 1), None, ALU.add))
            then(V.tensor_scalar(m0, j, float(MROWS), None, ALU.mult))
            then(V.tensor_tensor(m0, m0, valid, ALU.mult))
            then(V.tensor_tensor(r0, r0, m0, ALU.add))
            then(V.tensor_copy(table[:, :, 0], r0))
            then(V.tensor_copy(table[:, :, 1], expert))
            then(V.tensor_copy(table[:, :, 3], j))
            then(V.tensor_scalar(valid, valid, -float(E), float(E), ALU.mult, ALU.add))
            then(V.tensor_tensor(expert, expert, valid, ALU.add))
            then(V.tensor_scalar(expert, expert, float(TILES), None, ALU.mult))
            then(V.tensor_scalar(j, j, float(MT), None, ALU.mult))
            then(V.tensor_tensor(j, j, expert, ALU.add))
            then(V.tensor_copy(table[:, :, 2], j))
            then(V.tensor_copy(tail[:], filled[:]))

            def by_row(ap):
                return ap[:, :, None].to_broadcast([P, E, TILES])

            row_e = cst("row")[:, None, :].to_broadcast([P, E, TILES])
            then(V.tensor_tensor(own[:, 0:E, :], row_e, by_row(start), ALU.is_ge))
            then(V.tensor_tensor(own2[:], row_e, by_row(end), ALU.is_lt))
            then(V.tensor_tensor(own[:, 0:E, :], own[:, 0:E, :], own2[:], ALU.mult))
            then(V.memset(own[:, E, :], 0.0))
            V.memset(pv[:, 0, 0:1], 0.0).then_inc(plan_ready, 1)

            own_flat = own[:].rearrange("p e t -> p (e t)")
            b2_at = ROWS["moe_b2"][0]

            def add_expert(s, i, u):
                e = dve.value_load(table[0:1, s, 1:2], min_val=0, max_val=E - 1)
                m = dve.value_load(table[0:1, s, 2:3], min_val=0, max_val=(E + 1) * TILES - MT)
                jj = dve.value_load(table[0:1, s, 3:4], min_val=0, max_val=MTILES - 1)
                dve.wait_ge(m_y_psum[u], i + 1)
                b2e = rows_in[:, bass.ds(b2_at + e * D, D)]
                nc.vector.tensor_tensor(m_y[:, u], bank[6 + u][:, 0:MT * D].rearrange("p (t d) -> p t d", d=D),
                                        over_tiles(b2e, MT), ALU.add).then_inc(m_y_ready[u], 1)
                dve.wait_ge(m_y_ready[u], i + 1)
                if later(s):
                    dve.wait_ge(m_stored, 16 * s)
                if later(s):
                    dve.wait_ge(m_added, MT * s)
                for t in range(MT):
                    at = h2[:, jj * MT + t, :]
                    nc.vector.scalar_tensor_tensor(at, m_y[:, u, t], own_flat[:, bass.ds(m + t, 1)], at,
                                                   ALU.mult, ALU.add).then_inc(m_added, 1)

            def pair(i):
                add_expert(2 * i, i, 0)
                add_expert(2 * i + 1, i, 1)

            pair(0)
            with dve.Fori(1, STEPS // 2) as i:
                pair(i)
            add_expert(STEPS - 1, STEPS // 2, 0)

        @block.tensor
        def _(pe):
            pe.wait_ge(loaded, 16 * LOADS)
            pe.wait_ge(prepared, 3)
            mm = nc.tensor.matmul

            def transposed(dst, src, done):
                for t in range(NT):
                    last = nc.tensor.transpose(dst[:, t * P:(t + 1) * P], src[:, t], ident)
                last.then_inc(done, 1)

            def tok_xT(a):
                pe.wait_ge(x_ready, a + 1)
                if later(a):
                    pe.wait_ge(gelu_ready, NF * a)
                transposed(ta[0], x, xT_psum)

            def tok_kqv(a):
                pe.wait_ge(xT_ready, a + 1)
                mm(ta[1][:], mat("wk"), xT[:], start=True, stop=True).then_inc(k_psum, 1)
                mm(ta[3][:], mat("wq"), xT[:], start=True, stop=True).then_inc(q_psum, 1)
                if later(a):
                    pe.wait_ge(z2_ready, a)
                for t in range(NT):
                    last = mm(ta[2][:, t * D:(t + 1) * D], xT[:, t * P:(t + 1) * P], mat("wv"),
                              start=True, stop=True)
                last.then_inc(v_psum, 1)

            def tok_scores(a):
                pe.wait_ge(kqv_ready, 3 * a + 3)
                for c in range(NT):
                    mm(ta[c][:], kT[:, c * P:(c + 1) * P], qT[:], start=True, stop=True).then_inc(score_psum, 1)

            def tok_probsT(a):
                pe.wait_ge(probs_ready, NT * a + NT)
                for j in range(NT):
                    for i in range(NT):
                        last = nc.tensor.transpose(ta[j][:, i * P:(i + 1) * P], probs[:, i, j * P:(j + 1) * P],
                                                   ident)
                    last.then_inc(probsT_psum, 1)

            def tok_attend(a):
                pe.wait_ge(probsT_dve, NT // 2 * (a + 1))
                pe.wait_ge(probsT_act, NT // 2 * (a + 1))
                for i in range(NT):
                    for j in range(NT):
                        last = mm(ta[0][:, i * D:(i + 1) * D], probsT[:, j, i * P:(i + 1) * P], v[:, j],
                                  start=(j == 0), stop=(j == NT - 1))
                last.then_inc(attn_psum, 1)

            def tok_ff1(a):
                pe.wait_ge(rhat_ready, NT * a + NT)
                transposed(ta[1], r_hat, rT_psum)
                pe.wait_ge(rT_ready, a + 1)
                for f in range(NF):
                    mm(ta[(f + 2) % 4][:], mat("w1", f * P, (f + 1) * P), rT[:], start=True, stop=True
                       ).then_inc(ff_psum, 1)

            def tok_ff2(a):
                pe.wait_ge(gelu_ready, NF * a + NF)
                for i in range(NT):
                    for f in range(NF):
                        last = mm(ta[2][:, i * D:(i + 1) * D], geluT[:, f, i * P:(i + 1) * P],
                                  mat("w2", f * D, (f + 1) * D), start=(f == 0), stop=(f == NF - 1))
                last.then_inc(out_psum, 1)

            def gau_nT(b):
                pe.wait_ge(n_ready, NT * b + NT)
                if later(b):
                    pe.wait_ge(h2_ready, b)
                transposed(gb[0], n, nT_psum)

            def gau_project(b):
                pe.wait_ge(nT_ready, b + 1)
                if later(b):
                    pe.wait_ge(y2T_ready, b)
                mm(gb[1][:], mat("wqk"), nT[:], start=True, stop=True).then_inc(z_psum, 1)
                if later(b):
                    pe.wait_ge(slot_step, 5 * b)
                for g in range(NH):
                    mm(gb[2 + g][:], mat("wh", HID + g * P, HID + (g + 1) * P), nT[:], start=True, stop=True
                       ).then_inc(gate_psum, 1)
                pe.wait_ge(z_ready, b + 1)
                for t in range(NT):
                    last = mm(gb[t // 2][:, (t % 2) * HID:(t % 2 + 1) * HID], nT[:, t * P:(t + 1) * P],
                              mat("wh", 0, HID), start=True, stop=True)
                    if t % 2:
                        last.then_inc(gv_psum, 1)

            def gau_sim(b):
                pe.wait_ge(sqk_ready, 2 * b + 2)
                pe.wait_ge(gate_ready, NH * b + NH)
                pe.wait_ge(vpre_ready, 2 * b + 2)
                for j in range(NT):
                    mm(gb[(j + 2) % 4][:], skT[:, j * P:(j + 1) * P], sqT[:], start=True, stop=True
                       ).then_inc(sim_psum, 1)

            def gau_mix(b):
                pe.wait_ge(gv_ready, 2 * b + 2)
                pe.wait_ge(aT_pool, 2 * b + 2)
                pe.wait_ge(aT_act, 2 * b + 2)
                for g in range(NH):
                    for j in range(NT):
                        last = mm(gb[2 + g][:], gv[:, j, g * P:(g + 1) * P], aT[:, j], start=(j == 0),
                                  stop=(j == NT - 1))
                    last.then_inc(mix_psum, 1)

            def gau_wo(b):
                pe.wait_ge(gated_ready, NH * b + NH)
                for i in range(NT):
                    for g in range(NH):
                        last = mm(gb[0][:, i * D:(i + 1) * D], gatedT[:, g, i * P:(i + 1) * P],
                                  mat("wo", g * D, (g + 1) * D), start=(g == 0), stop=(g == NH - 1))
                last.then_inc(wo_psum, 1)

            def gau_logits(b):
                pe.wait_ge(y2_ready, NT * b + NT)
                transposed(gb[1], y2, y2T_psum)
                pe.wait_ge(y2T_ready, b + 1)
                for t in range(NT):
                    last = mm(gb[2][:, t * E:(t + 1) * E], y2T[:, t * P:(t + 1) * P], mat("wg"),
                              start=True, stop=True)
                last.then_inc(logit_psum, 1)

            def gau_rank(b):
                pe.wait_ge(route_step, ROUTE * b + 6)
                mm(gb[3][:, 0:NT * E], before_bf[:], route_bf[:].rearrange("p t e -> p (t e)"),
                   start=True, stop=False, skip_group_check=True)
                for t in range(NT):
                    last = mm(gb[3][:, (t + 1) * E:(NT + 1) * E], ones_bf[:],
                              route_bf[:, t:t + 1, :].to_broadcast([P, NT - t, E]),
                              start=False, stop=(t == NT - 1), skip_group_check=True)
                last.then_inc(rank_psum, 1)

            tok_xT(0)
            tok_kqv(0)
            tok_scores(0)
            tok_probsT(0)
            tok_attend(0)
            tok_ff1(0)
            tok_ff2(0)
            def both(a):
                b = a - 1
                tok_xT(a)
                tok_kqv(a)
                tok_scores(a)
                gau_nT(b)
                gau_project(b)
                tok_probsT(a)
                gau_sim(b)
                tok_attend(a)
                gau_mix(b)
                tok_ff1(a)
                gau_wo(b)
                tok_ff2(a)
                gau_logits(b)
                gau_rank(b)

            both(1)
            with pe.Fori(2, SEQS) as a:
                both(a)
            b = SEQS - 1
            gau_nT(b)
            gau_project(b)
            gau_sim(b)
            gau_mix(b)
            gau_wo(b)
            gau_logits(b)
            gau_rank(b)

            def expert_up(i, u):
                pe.wait_ge(m_loaded[u], 16 * (i + 1))
                if later(i):
                    pe.wait_ge(m_xT_ready[u], i)
                for t in range(MT):
                    last = nc.tensor.transpose(bank[u][:, t * P:(t + 1) * P], m_rows[:, u, t], ident)
                last.then_inc(m_xT_psum[u], 1)
                pe.wait_ge(m_xT_ready[u], i + 1)
                pe.wait_ge(m_w_ready[u], i + 1)
                if later(i):
                    pe.wait_ge(m_h_ready[u], NF * i)
                for f in range(NF):
                    at = (f % 2) * MROWS
                    last = mm(bank[2 + 2 * u + f // 2][:, at:at + MROWS], m_w[:, u, f * P:(f + 1) * P],
                              m_xT[:, u], start=True, stop=True)
                    if f % 2:
                        last.then_inc(m_h_psum[u], 1)

            def expert_down(i, u):
                pe.wait_ge(m_h_ready[u], NF * (i + 1))
                if later(i):
                    pe.wait_ge(m_y_ready[u], i)
                for t in range(MT):
                    for f in range(NF):
                        last = mm(bank[6 + u][:, t * D:(t + 1) * D], m_hT[:, u, f, t * P:(t + 1) * P],
                                  m_w[:, u, DFF + f * D:DFF + (f + 1) * D], start=(f == 0), stop=(f == NF - 1))
                last.then_inc(m_y_psum[u], 1)

            pe.wait_ge(plan_ready, 1)
            expert_up(0, 0)
            def pair(i):
                expert_up(i, 1)
                expert_down(i, 0)
                expert_up(i + 1, 0)
                expert_down(i, 1)

            pair(0)
            with pe.Fori(1, STEPS // 2) as i:
                pair(i)
            expert_down(STEPS // 2, 0)


def constants():
    c = np.zeros((P, CONST_W), np.float32)

    def put(name, a):
        at, w = CONST[name]
        c[:, at:at + w] = a

    pos = np.arange(S, dtype=np.float32)[:, None]
    i = np.arange(D, dtype=np.float32)[None, :]
    ang = (pos / np.power(np.float32(10000.0), np.float32(2.0) * i / np.float32(D))).astype(np.float64)
    pe = np.where((np.arange(D) % 2 == 0)[None, :], np.sin(ang), np.cos(ang)) * D ** 0.5
    put("pos", pe.reshape(NT, P, D).transpose(1, 0, 2).reshape(P, NT * D))
    put("ident", np.eye(P))
    put("before", np.triu(np.ones((P, P)), 1))
    put("base", np.arange(E) * REGION + PAD)
    put("down", E - np.arange(E))
    put("up", np.arange(E))
    put("row", np.arange(TILES)[None, :] * P + np.arange(P)[:, None])
    put("step", np.arange(TABLE))
    return c


def kernel(**inputs):
    import concourse.bacc as _bacc
    from concourse.bass_utils import run_bass_kernel_spmd as _run

    g = {k: np.asarray(a) for k, a in inputs.items()}
    tok = {k[7:]: a for k, a in g.items() if k.startswith("L0_tok_")}
    att = {k[8:]: a for k, a in g.items() if k.startswith("L0_attn_")}
    ffn = {k[7:]: a for k, a in g.items() if k.startswith("L0_ffn_")}

    def chunks(w):
        return w.reshape(-1, P, w.shape[1]).transpose(1, 0, 2).reshape(P, -1)

    col_of = {"bk": tok["bk"], "bq": tok["bq"], "g": tok["ln_g"], "b": tok["ln_b"], "ag": att["ln_g"],
              "ab": att["ln_b"], "bqk": att["bqk"]}
    for f in range(NF):
        col_of[f"b1_{f}"] = tok["b1"][f * P:(f + 1) * P]
    for k in range(NH):
        col_of[f"bh_{k}"] = att["bh"][HID + k * P:HID + (k + 1) * P]
    for k in range(2):
        col_of[f"gamma_{k}"] = att["gamma"][k]
        col_of[f"beta_{k}"] = att["beta"][k]
    row_of = {"bv": tok["bv"], "g": tok["ln_g"], "b": tok["ln_b"], "b2": tok["b2"], "bo": att["bo"],
              "bhv": att["bh"][:HID], "bg": ffn["bg"], "moe_b2": ffn["b2"].reshape(-1)}
    mat_of = {"wk": tok["wk"], "wq": tok["wq"], "wv": tok["wv"], "w1": tok["w1"], "w2": chunks(tok["w2"]),
              "wh": att["Wh"], "wqk": att["Wqk"], "wo": chunks(att["Wo"]), "wg": ffn["Wg"]}
    w1 = ffn["W1"].transpose(1, 0, 2)
    w2 = ffn["W2"].reshape(E, NF, P, D).transpose(2, 0, 1, 3).reshape(P, E, NF * D)
    b1 = ffn["b1"].reshape(E, NF, P).transpose(2, 0, 1)
    tokens = np.zeros((P, (SEQS + 1) * NT), np.int32)
    tokens[:, :TILES] = g["x"].reshape(TILES, P).T
    arrays = {
        "tokens": tokens,
        "const": constants(),
        "mats": np.ascontiguousarray(np.concatenate([mat_of[k] for k in MATS], axis=1)),
        "cols": np.ascontiguousarray(np.stack([col_of[k] for k in COLS], axis=1)),
        "rows": np.concatenate([row_of[k] for k in ROWS]),
        "experts": np.ascontiguousarray(np.concatenate([w1, w2, b1], axis=2).reshape(P, E * EXPERT)),
        "emb": np.ascontiguousarray(tok["emb"]),
    }
    nc = _bacc.Bacc("TRN2", target_bir_lowering=False, num_devices=1)
    ins = {k: nc.dram_tensor(f"in_{k}_dram", a.shape, mybir.dt.from_np(a.dtype), kind="ExternalInput").ap()
           for k, a in arrays.items()}
    out = nc.dram_tensor("out_0_dram", (SEQS * S, D), F32, kind="ExternalOutput").ap()
    build(nc, ins, out)
    r = _run(nc, [{f"in_{k}_dram": a for k, a in arrays.items()}], core_ids=[0])
    return r.results[0]["out_0_dram"].reshape(SEQS, S, D)
```

```python
from contextlib import ExitStack

import concourse.bass as bass
import numpy as np
from concourse import mybir

ALU = mybir.AluOpType
ACT = mybir.ActivationFunctionType
AX = mybir.AxisListType.X
F32 = mybir.dt.float32
BF16 = mybir.dt.bfloat16
I32 = mybir.dt.int32
U32 = mybir.dt.uint32

P = 128
VOCAB = 50257
SEQS, S, D = 16, 512, 128
NT = S // P
TILES = SEQS * NT
DFF = 512
NF = DFF // P
HID = 256
NH = HID // P
E = 8
EPS = 1e-5
SCORE_SCALE = float(D) ** -0.5
SIM_SCALE = 1.0 / S

MT = 2
MROWS = MT * P
MTILES = TILES // MT
STEPS = MTILES + E - 1
PAD = MROWS
REGION = SEQS * S + 2 * PAD
TABLE = STEPS + 2
UP, DOWN = DFF + NF, NF * D
EXPERT = UP + DOWN

COLS = ["bk", "bq", "g", "b", "b1_0", "b1_1", "b1_2", "b1_3", "ag", "ab", "bqk", "bh_0", "bh_1",
        "gamma_0", "beta_0", "gamma_1", "beta_1"]
ROWS = {}
_at = 0
for _n, _w in (("bv", D), ("g", D), ("b", D), ("b2", D), ("bo", D), ("bhv", HID), ("bg", E), ("moe_b2", E * D)):
    ROWS[_n] = (_at, _w)
    _at += _w
ROWS_W = _at
MATS = {}
_at = 0
for _n, _w in (("wk", D), ("wq", D), ("wv", D), ("w1", DFF), ("w2", NF * D), ("wh", 2 * HID), ("wqk", D),
               ("wo", NH * D), ("wg", E)):
    MATS[_n] = (_at, _w)
    _at += _w
MATS_W = _at
CONST = {}
_at = 0
for _n, _w in (("pos", NT * D), ("ident", P), ("before", P), ("base", E), ("down", E), ("up", E),
               ("row", TILES), ("step", TABLE)):
    CONST[_n] = (_at, _w)
    _at += _w
CONST_W = _at


def build(nc, ins, out):
    with ExitStack() as ctx:
        def sb(name, shape, dt=F32):
            return ctx.enter_context(nc.sbuf_tensor(name, shape, dt))

        def sem(name):
            return ctx.enter_context(nc.semaphore(name))

        routed = nc.dram_tensor("routed_rows", [E * REGION, D], F32, kind="Internal").ap()

        cols = sb("cols", [P, len(COLS)])
        rows_in = sb("rows_in", [P, ROWS_W])
        mats = sb("mats", [P, MATS_W])
        const = sb("const", [P, CONST_W])
        experts = sb("experts", [P, E * EXPERT])
        tokens = sb("tokens", [P, (SEQS + 1) * NT], I32)

        def col(name):
            i = COLS.index(name)
            return cols[:, i:i + 1]

        def row(name):
            at, w = ROWS[name]
            return rows_in[:, at:at + w]

        def mat(name, lo=0, hi=None):
            at, w = MATS[name]
            return mats[:, at + lo:at + (w if hi is None else hi)]

        def cst(name):
            at, w = CONST[name]
            return const[:, at:at + w]

        def over_tiles(ap, n=NT):
            return ap[:, None, :].to_broadcast([P, n, ap.shape[1]])

        ident = cst("ident")
        before_bf = sb("before_bf", [P, P], BF16)
        ones_bf = sb("ones_bf", [P, P], BF16)
        b_b2 = sb("b_b2", [P, D])
        bk_scaled = sb("bk_scaled", [P, 1])
        minus_half = sb("minus_half", [P, NT])
        zeros = sb("zeros", [P, MT * D])

        token_now = sb("token_now", [P, NT], I32)
        emb = sb("emb_rows", [P, NT, D])
        x = sb("x", [P, NT, D])
        xT = sb("xT", [P, S])
        kT = sb("kT", [P, S])
        qT = sb("qT", [P, S])
        v = sb("v", [P, NT, D])
        neg_max = sb("neg_max", [P, NT])
        exp_sum = sb("exp_sum", [P, NT])
        exp_inv = sb("exp_inv", [P, NT])
        probs_buf = sb("probs", [P, 2 * EXPERT])
        probs = probs_buf[:, 0:NT * S].rearrange("p (t s) -> p t s", s=S)
        probsT = sb("probsT", [P, NT, S])
        z1 = sb("z1", [P, NT, D])
        r_hat = sb("r_hat", [P, NT, D])
        r_scaled = sb("r_scaled", [P, NT, D])
        r_res = sb("r_res", [P, NT, D])
        rT = sb("rT", [P, S])
        geluT = sb("geluT", [P, NF, S])
        z2 = sb("z2", [P, NT, D])
        h_scaled = sb("h_scaled", [P, NT, D])
        h = sb("h", [P, NT, D])
        y = sb("y", [P, NT, D])
        n = sb("n", [P, NT, D])
        hy = sb("hy", [P, NT, D])
        hy_bo = sb("hy_bo", [P, NT, D])
        nT = sb("nT", [P, S])
        zT = sb("zT", [P, S])
        sqT = sb("sqT", [P, S])
        skT = sb("skT", [P, S])
        gateT = sb("gateT", [P, NH, S])
        v_pre = sb("v_pre", [P, NT, HID])
        gv = sb("gv", [P, NT, HID])
        relu = sb("relu", [P, NT, S])
        aT = sb("aT", [P, NT, S])
        gatedT = sb("gatedT", [P, NH, S])
        h2 = sb("h2", [P, TILES, D])
        h2_now = sb("h2_now", [P, NT, D])
        y2 = sb("y2", [P, NT, D])
        y2T = sb("y2T", [P, S])
        xs = sb("xs", [P, NT, D])
        stats = {k: sb(f"stats{k}", [P, NT, 6]) for k in (1, 2, 3, 5)}
        mv = {k: sb(f"mv{k}", [P, NT, 2]) for k in (1, 2, 3, 5)}
        norms = {1: 1, 2: 1, 3: 2, 5: 1}
        var_eps = {k: sb(f"var_eps{k}", [P, w, NT]) for k, w in norms.items()}
        rstd = {k: sb(f"rstd{k}", [P, w, NT]) for k, w in norms.items()}
        y_bias = sb("y_bias", [P, NT])
        y2_bias = sb("y2_bias", [P, NT])
        logits = sb("logits", [P, NT, E])
        lmax = sb("lmax", [P, NT])
        lshift = sb("lshift", [P, NT, E])
        lexp = sb("lexp", [P, NT, E])
        lsum = sb("lsum", [P, NT])
        pmax = sb("pmax", [P, NT])
        is_max = sb("is_max", [P, NT, E])
        ranked = sb("ranked", [P, NT, E])
        best = sb("best", [P, NT])
        route = sb("route", [P, NT, E])
        route_bf = sb("route_bf", [P, NT, E], BF16)
        filled = sb("filled", [P, E])
        slot_all = sb("slot_all", [P, NT, E])
        slot_own = sb("slot_own", [P, NT, E])
        slot = sb("slot", [P, NT])
        slot_u = sb("slot_u", [P, NT], U32)
        count = sb("count", [P, E])
        start = sb("start", [P, E])
        end = sb("end", [P, E])
        pl = sb("plan_tmp", [P, 8, E])
        pli = sb("plan_int", [P, 2, E], I32)
        po = geluT[:].rearrange("p f s -> p (f s)")[:, 0:6 * TABLE * E].rearrange(
            "p (i s e) -> p i s e", s=TABLE, e=E)
        pv = sb("plan_cols", [P, 6, TABLE])
        table = sb("table", [P, TABLE, 4], I32)
        tail = sb("tail", [P, E], I32)
        own = sb("own", [P, E + 1, TILES])
        own2 = sb("own2", [P, E, TILES])
        m_rows = probsT[:, 0].rearrange("p (u t d) -> p u t d", u=2, t=MT)
        m_xT = probsT[:, 1].rearrange("p (u r) -> p u r", u=2)
        m_w = probs_buf[:].rearrange("p (u w) -> p u w", u=2)
        m_hT = relu[:].rearrange("p t (a r) -> p t a r", r=MROWS).rearrange("p (u t) a r -> p u (t a) r", u=2)
        m_y = probsT[:, 2].rearrange("p (u t d) -> p u t d", u=2, t=MT)

        bank = [ctx.enter_context(nc.psum_tensor(f"bank{i}", [P, 512], F32)) for i in range(8)]
        ta, gb = bank[:4], bank[4:]

        loaded = sem("loaded")
        experts_loaded = sem("experts_loaded")
        prepared = sem("prepared")
        prepared_pool = sem("prepared_pool")
        token_ready = sem("token_ready")
        emb_ready = sem("emb_ready")
        x_ready = sem("x_ready")
        xT_psum = sem("xT_psum"); xT_ready = sem("xT_ready")
        k_psum = sem("k_psum"); q_psum = sem("q_psum"); v_psum = sem("v_psum")
        kq_ready = sem("kq_ready")
        v_ready = sem("v_ready")
        score_psum = sem("score_psum")
        max_ready = sem("max_ready")
        probs_ready = sem("probs_ready")
        probsT_psum = sem("probsT_psum")
        probsT_dve = sem("probsT_dve")
        probsT_act = sem("probsT_act")
        attn_psum = sem("attn_psum")
        inv_ready = sem("inv_ready")
        z1_ready = sem("z1_ready")
        stats_ready = {k: sem(f"stats{k}_ready") for k in (1, 2, 3, 5)}
        mv_ready = {k: sem(f"mv{k}_ready") for k in (1, 2, 3, 5)}
        var_ready = {k: sem(f"var{k}_ready") for k in (1, 2, 3, 5)}
        rstd_ready = {k: sem(f"rstd{k}_ready") for k in (1, 2, 3, 5)}
        rhat_ready = sem("rhat_ready")
        rscaled_ready = sem("rscaled_ready"); rres_ready = sem("rres_ready")
        rT_psum = sem("rT_psum"); rT_ready = sem("rT_ready")
        ff_psum = sem("ff_psum")
        gelu_ready = sem("gelu_ready")
        out_psum = sem("out_psum")
        z2_ready = sem("z2_ready")
        hscaled_ready = sem("hscaled_ready"); h_ready = sem("h_ready")
        bias_ready = sem("bias_ready"); bias2_ready = sem("bias2_ready")
        y_ready = sem("y_ready")
        n_ready = sem("n_ready")
        hy_ready = sem("hy_ready")
        nT_psum = sem("nT_psum"); nT_ready = sem("nT_ready")
        z_psum = sem("z_psum"); z_ready = sem("z_ready")
        gate_psum = sem("gate_psum"); gate_ready = sem("gate_ready")
        gv_psum = sem("gv_psum"); vpre_ready = sem("vpre_ready"); gv_ready = sem("gv_ready")
        sqk_ready = sem("sqk_ready")
        sim_psum = sem("sim_psum")
        relu_ready = sem("relu_ready")
        aT_pool = sem("aT_pool"); aT_act = sem("aT_act")
        mix_psum = sem("mix_psum"); gated_ready = sem("gated_ready")
        wo_psum = sem("wo_psum"); h2_ready = sem("h2_ready"); h2_kept = sem("h2_kept")
        y2_ready = sem("y2_ready")
        y2T_psum = sem("y2T_psum"); y2T_ready = sem("y2T_ready")
        logit_psum = sem("logit_psum")
        logits_ready = sem("logits_ready")
        route_step = sem("route_step")
        lexp_ready = sem("lexp_ready")
        pmax_step = sem("pmax_step")
        rank_psum = sem("rank_psum")
        slot_step = sem("slot_step")
        xs_ready = sem("xs_ready")
        scattered = sem("scattered")
        padded = sem("padded")
        plan_step = sem("plan_step")
        plan_ready = sem("plan_ready")
        m_loaded = [sem(f"m_loaded{u}") for u in range(2)]
        m_w_ready = [sem(f"m_w_ready{u}") for u in range(2)]
        m_xT_psum = [sem(f"m_xT_psum{u}") for u in range(2)]
        m_xT_ready = [sem(f"m_xT_ready{u}") for u in range(2)]
        m_h_psum = [sem(f"m_h_psum{u}") for u in range(2)]
        m_h_ready = [sem(f"m_h_ready{u}") for u in range(2)]
        m_y_psum = [sem(f"m_y_psum{u}") for u in range(2)]
        m_y_ready = [sem(f"m_y_ready{u}") for u in range(2)]
        m_added = sem("m_added")
        m_stored = sem("m_stored")

        ROUTE = 6
        LOADS = 5

        waited = {e: sem(f"waited_{e}") for e in ("sp", "pool", "dve")}

        def later(i):
            return not (isinstance(i, int) and i <= 0)

        def apart(eng, name):
            eng.sem_inc(waited[name], 1)

        block = ctx.enter_context(nc.Block())

        @block.sync
        def _(sp):
            sp.dma_start(tokens[:], ins["tokens"]).then_inc(loaded, 16)
            sp.dma_start(const[:], ins["const"]).then_inc(loaded, 16)
            sp.dma_start(mats[:], ins["mats"]).then_inc(loaded, 16)
            sp.dma_start(cols[:], ins["cols"]).then_inc(loaded, 16)
            sp.dma_start(rows_in[:], ins["rows"].partition_broadcast(P)).then_inc(loaded, 16)
            sp.dma_start(experts[:], ins["experts"]).then_inc(experts_loaded, 16)
            sp.wait_ge(prepared_pool, 2)
            for e in range(E):
                sp.dma_start(routed[e * REGION:e * REGION + PAD, :].rearrange("(t p) d -> p t d", p=P),
                             zeros[:].rearrange("p (t d) -> p t d", d=D)).then_inc(padded, 16)
            sp.wait_ge(plan_ready, 1)
            for e in range(E):
                at = sp.value_load(tail[0:1, e:e + 1], min_val=e * REGION + PAD, max_val=(e + 1) * REGION - PAD)
                sp.dma_start(routed[bass.ds(at, PAD), :].rearrange("(t p) d -> p t d", p=P),
                             zeros[:].rearrange("p (t d) -> p t d", d=D)).then_inc(padded, 16)
            sp.wait_ge(padded, 2 * E * 16)
            sp.wait_ge(scattered, SEQS * NT * 16)

            def load(s, i, u):
                at = sp.value_load(table[0:1, s, 0:1], min_val=0, max_val=E * REGION - MROWS)
                if later(i):
                    sp.wait_ge(m_xT_psum[u], i)
                apart(sp, "sp")
                sp.dma_start(m_rows[:, u], routed[bass.ds(at, MROWS), :].rearrange("(t p) d -> p t d", p=P)
                             ).then_inc(m_loaded[u], 16)

            load(0, 0, 0)
            load(1, 0, 1)
            def pair(i):
                load(2 * i + 2, i + 1, 0)
                load(2 * i + 3, i + 1, 1)

            pair(0)
            with sp.Fori(1, STEPS // 2) as i:
                pair(i)
            sp.wait_ge(m_loaded[1], 16 * (STEPS // 2 + 1))

        @block.gpsimd
        def _(pool):
            nc.gpsimd.memset(minus_half[:], -0.5).then_inc(prepared_pool, 1)
            nc.gpsimd.memset(zeros[:], 0.0).then_inc(prepared_pool, 1)
            pool.wait_ge(loaded, 16 * LOADS)
            nc.gpsimd.tensor_tensor(b_b2[:], row("b"), row("b2"), ALU.add).then_inc(prepared_pool, 1)
            pool.wait_ge(prepared_pool, 3)

            def gather(i):
                if later(i):
                    pool.wait_ge(x_ready, i)
                apart(pool, "pool")
                nc.gpsimd.tensor_copy(token_now[:], tokens[:, bass.ds(i * NT, NT)]).then_inc(token_ready, 1)
                pool.wait_ge(token_ready, i + 1)
                apart(pool, "pool")
                for t in range(NT):
                    nc.gpsimd.indirect_dma_start(
                        out=emb[:, t, :], out_offset=None, in_=ins["emb"],
                        in_offset=bass.IndirectOffsetOnAxis(ap=token_now[:, t:t + 1].bitcast(U32), axis=0),
                        bounds_check=VOCAB - 1, oob_is_err=False).then_inc(emb_ready, 16)

            def inv_std(i, k):
                for n_, w in enumerate(reversed(range(norms[k]))):
                    pool.wait_ge(var_ready[k], norms[k] * i + n_ + 1)
                    nc.gpsimd.tensor_tensor(rstd[k][:, w], var_eps[k][:, w], minus_half[:], ALU.pow
                                            ).then_inc(rstd_ready[k], 1)

            def tok_residual(a):
                pool.wait_ge(rhat_ready, NT * a + NT)
                nc.gpsimd.tensor_tensor(r_scaled[:], r_hat[:], over_tiles(row("g")), ALU.mult
                                        ).then_inc(rscaled_ready, 1)
                pool.wait_ge(rscaled_ready, a + 1)
                if later(a):
                    pool.wait_ge(z2_ready, a)
                nc.gpsimd.tensor_tensor(r_res[:], r_scaled[:], over_tiles(b_b2[:]), ALU.add
                                        ).then_inc(rres_ready, 1)

            def gau_residual(b):
                pool.wait_ge(y_ready, NT * b + NT)
                nc.gpsimd.tensor_tensor(hy[:], h[:], y[:], ALU.add).then_inc(hy_ready, 1)
                pool.wait_ge(hy_ready, 2 * b + 1)
                if later(b):
                    pool.wait_ge(h2_ready, b)
                nc.gpsimd.tensor_tensor(hy_bo[:], hy[:], over_tiles(row("bo")), ALU.add).then_inc(hy_ready, 1)

            def keep_h2(b):
                pool.wait_ge(h2_ready, b + 1)
                apart(pool, "pool")
                nc.gpsimd.tensor_copy(h2[:, bass.ds(b * NT, NT), :], h2_now[:]).then_inc(h2_kept, 1)

            def gau_square(b):
                for j in range(NT // 2):
                    pool.wait_ge(relu_ready, NT * b + j + 1)
                    nc.gpsimd.tensor_tensor(aT[:, j], relu[:, j], relu[:, j], ALU.mult).then_inc(aT_pool, 1)

            def gau_xs(b):
                pool.wait_ge(pmax_step, 2 * b + 2)
                if later(b):
                    pool.wait_ge(scattered, 16 * NT * b)
                nc.gpsimd.tensor_tensor(xs[:], y2[:], pmax[:, :, None].to_broadcast([P, NT, D]), ALU.mult
                                        ).then_inc(xs_ready, 1)

            def gau_scatter(b):
                pool.wait_ge(xs_ready, b + 1)
                pool.wait_ge(slot_step, 5 * b + 5)
                apart(pool, "pool")
                for t in range(NT):
                    nc.gpsimd.indirect_dma_start(
                        out=routed, out_offset=bass.IndirectOffsetOnAxis(ap=slot_u[:, t:t + 1], axis=0),
                        in_=xs[:, t, :], in_offset=None, bounds_check=E * REGION - 1, oob_is_err=False,
                    ).then_inc(scattered, 16)

            def both(a):
                b = a - 1
                if later(b - 1):
                    gau_xs(b - 2)
                if later(a):
                    inv_std(b, 3)
                if later(b):
                    inv_std(b - 1, 5)
                    keep_h2(b - 1)
                if later(b - 1):
                    gau_scatter(b - 2)
                gather(a + 1)
                if later(a):
                    gau_square(b)
                    gau_residual(b)
                inv_std(a, 1)
                tok_residual(a)
                inv_std(a, 2)

            gather(0)
            both(0)
            both(1)
            both(2)
            with pool.Fori(3, SEQS) as a:
                both(a)
            b = SEQS - 1
            gau_xs(b - 2)
            inv_std(b, 3)
            inv_std(b - 1, 5)
            keep_h2(b - 1)
            gau_scatter(b - 2)
            gau_square(b)
            gau_residual(b)
            gau_xs(b - 1)
            gau_scatter(b - 1)
            inv_std(b, 5)
            keep_h2(b)
            gau_xs(b)
            gau_scatter(b)
            pool.wait_ge(emb_ready, 16 * NT * (SEQS + 1))

            def store(s):
                j = pool.value_load(table[0:1, s, 3:4], min_val=0, max_val=MTILES - 1)
                pool.wait_ge(m_added, MT * s + MT)
                apart(pool, "pool")
                if later(s):
                    pool.wait_ge(m_stored, 16 * s)
                apart(pool, "pool")
                pool.dma_start(out[bass.ds(j * MROWS, MROWS), :].rearrange("(t p) d -> p t d", p=P),
                             h2[:, bass.ds(j * MT, MT), :]).then_inc(m_stored, 16)

            def pair(i):
                store(2 * i)
                store(2 * i + 1)

            pool.wait_ge(plan_ready, 1)
            pair(0)
            with pool.Fori(1, STEPS // 2) as i:
                pair(i)
            store(STEPS - 1)
            pool.wait_ge(m_stored, 16 * STEPS)

        @block.scalar
        def _(act):
            act.wait_ge(loaded, 16 * LOADS)
            act.wait_ge(prepared, 4)

            def tok_xT(a):
                act.wait_ge(xT_psum, a + 1)
                nc.scalar.copy(xT[:], gb[3][:]).then_inc(xT_ready, 1)

            def tok_kq(a):
                act.wait_ge(k_psum, a + 1)
                nc.scalar.activation(kT[:], ta[1][:], ACT.Identity, bias=bk_scaled[:], scale=SCORE_SCALE
                                     ).then_inc(kq_ready, 1)
                act.wait_ge(q_psum, a + 1)
                nc.scalar.activation(qT[:], ta[2][:], ACT.Identity, bias=col("bq")).then_inc(kq_ready, 1)

            def tok_exp(a, lo, hi):
                for c in range(lo, hi):
                    act.wait_ge(max_ready, NT * a + c + 1)
                    nc.scalar.activation(probs[:, c], ta[c][:], ACT.Exp, bias=neg_max[:, c:c + 1],
                                         accum_out=exp_sum[:, c:c + 1]).then_inc(probs_ready, 1)

            def tok_probsT(a):
                for j in range(NT // 2, NT):
                    act.wait_ge(probsT_psum, NT * a + j + 1)
                    nc.scalar.copy(probsT[:, j], ta[j][:]).then_inc(probsT_act, 1)

            def tok_rT(a):
                act.wait_ge(rT_psum, a + 1)
                nc.scalar.activation(rT[:], ta[1][:], ACT.Identity, bias=col("b"), scale=col("g")
                                     ).then_inc(rT_ready, 1)

            def tok_gelu(a):
                for f in range(NF):
                    act.wait_ge(ff_psum, NF * a + f + 1)
                    nc.scalar.activation(geluT[:, f], ta[(f + 2) % 4][:], ACT.Gelu, bias=col(f"b1_{f}")
                                         ).then_inc(gelu_ready, 1)

            def gau_nT(b):
                act.wait_ge(nT_psum, b + 1)
                nc.scalar.activation(nT[:], gb[0][:], ACT.Identity, bias=col("ab"), scale=col("ag")
                                     ).then_inc(nT_ready, 1)

            def gau_silu(b):
                act.wait_ge(z_psum, b + 1)
                nc.scalar.activation(zT[:], gb[1][:], ACT.Silu, bias=col("bqk")).then_inc(z_ready, 1)
                for g in range(NH):
                    act.wait_ge(gate_psum, NH * b + g + 1)
                    nc.scalar.activation(gateT[:, g], gb[2 + g][:], ACT.Silu, bias=col(f"bh_{g}")
                                         ).then_inc(gate_ready, 1)

            def gau_gv(b):
                for i in range(2):
                    act.wait_ge(vpre_ready, 2 * b + i + 1)
                    nc.scalar.activation(gv[:, 2 * i:2 * i + 2, :], v_pre[:, 2 * i:2 * i + 2, :], ACT.Silu
                                         ).then_inc(gv_ready, 1)

            def gau_y(b):
                act.wait_ge(bias_ready, b + 1)
                for t in range(NT):
                    nc.scalar.activation(y[:, t], h[:, t], ACT.Identity, bias=y_bias[:, t:t + 1],
                                         scale=rstd[3][:, 0, t:t + 1]).then_inc(y_ready, 1)

            def gau_y2(b):
                act.wait_ge(bias2_ready, b + 1)
                if later(b):
                    act.wait_ge(xs_ready, b)
                for t in range(NT):
                    nc.scalar.activation(y2[:, t], h2_now[:, t], ACT.Identity, bias=y2_bias[:, t:t + 1],
                                         scale=rstd[5][:, 0, t:t + 1]).then_inc(y2_ready, 1)

            def gau_square(b):
                for j in range(NT // 2, NT):
                    act.wait_ge(relu_ready, NT * b + j + 1)
                    nc.scalar.activation(aT[:, j], relu[:, j], ACT.Square).then_inc(aT_act, 1)

            def gau_y2T(b):
                act.wait_ge(y2T_psum, b + 1)
                nc.scalar.copy(y2T[:], ta[3][:]).then_inc(y2T_ready, 1)

            def gau_lexp(b):
                act.wait_ge(route_step, ROUTE * b + 2)
                nc.scalar.activation(lexp[:], lshift[:], ACT.Exp).then_inc(lexp_ready, 1)

            def both(a):
                b = a - 1
                tok_kq(a)
                tok_exp(a, 0, 2)
                if later(a):
                    gau_nT(b)
                tok_exp(a, 2, NT)
                if later(a):
                    gau_silu(b)
                if later(b):
                    gau_y2(b - 1)
                if later(a):
                    gau_gv(b)
                tok_probsT(a)
                if later(b):
                    gau_y2T(b - 1)
                if later(a):
                    gau_square(b)
                    gau_y(b)
                tok_rT(a)
                tok_gelu(a)
                tok_xT(a + 1)
                if later(b):
                    gau_lexp(b - 1)

            tok_xT(0)
            both(0)
            both(1)
            both(2)
            with act.Fori(3, SEQS) as a:
                both(a)
            b = SEQS - 1
            gau_nT(b)
            gau_silu(b)
            gau_y2(b - 1)
            gau_gv(b)
            gau_y2T(b - 1)
            gau_square(b)
            gau_y(b)
            gau_lexp(b - 1)
            gau_y2(b)
            gau_y2T(b)
            gau_lexp(b)

            def expert_xT(i, u):
                act.wait_ge(m_xT_psum[u], i + 1)
                nc.scalar.copy(m_xT[:, u], bank[u][:, 0:MROWS]).then_inc(m_xT_ready[u], 1)

            def expert_hidden(i, u):
                act.wait_ge(m_w_ready[u], 2 * i + 1)
                for f in range(NF):
                    act.wait_ge(m_h_psum[u], NF // 2 * i + f // 2 + 1)
                    at = (f % 2) * MROWS
                    nc.scalar.activation(m_hT[:, u, f], bank[2 + 2 * u + f // 2][:, at:at + MROWS], ACT.Relu,
                                         bias=m_w[:, u, DFF + f:DFF + f + 1]
                                         ).then_inc(m_h_ready[u], 1)

            def pair(i):
                expert_hidden(i, 0)
                expert_xT(i, 1)
                expert_hidden(i, 1)
                expert_xT(i + 1, 0)

            expert_xT(0, 0)
            pair(0)
            with act.Fori(1, STEPS // 2) as i:
                pair(i)
            expert_hidden(STEPS // 2, 0)

        @block.vector
        def _(dve):
            dve.wait_ge(loaded, 16 * LOADS)
            nc.vector.tensor_copy(before_bf[:], cst("before")).then_inc(prepared, 1)
            nc.vector.memset(ones_bf[:], 1.0).then_inc(prepared, 1)
            nc.vector.tensor_copy(filled[:], cst("base")).then_inc(prepared, 1)
            nc.vector.tensor_scalar(bk_scaled[:], col("bk"), SCORE_SCALE, None, ALU.mult).then_inc(prepared, 1)

            def embed(i):
                dve.wait_ge(emb_ready, 16 * NT * (i + 1))
                if later(i):
                    dve.wait_ge(xT_psum, i)
                nc.vector.scalar_tensor_tensor(
                    x[:].rearrange("p t d -> p (t d)"), emb[:].rearrange("p t d -> p (t d)"), float(D) ** 0.5,
                    cst("pos"), ALU.mult, ALU.add).then_inc(x_ready, 1)

            def norm_stats(i, k, src, ready, n_ready_):
                for t in range(NT):
                    dve.wait_ge(ready, n_ready_(t))
                    nc.vector.bn_stats(stats[k][:, t], src(t)).then_inc(stats_ready[k], 1)
                dve.wait_ge(stats_ready[k], NT * i + NT)
                apart(dve, "dve")
                for t in range(NT):
                    nc.vector.bn_aggr(mv[k][:, t], stats[k][:, t]).then_inc(mv_ready[k], 1)
                dve.wait_ge(mv_ready[k], NT * i + NT)
                if k == 3:
                    nc.vector.tensor_scalar(var_eps[k][:, 1], mv[k][:, :, 1], 1.0 + EPS, EPS * EPS, ALU.mult,
                                            ALU.add).then_inc(var_ready[k], 1)
                nc.vector.tensor_scalar(var_eps[k][:, 0], mv[k][:, :, 1], EPS, None, ALU.add
                                        ).then_inc(var_ready[k], 1)

            def norm_apply(k, dst, src, scale, done):
                for t in range(NT):
                    nc.vector.tensor_scalar(dst[:, t], src(t), mv[k][:, t, 0:1], rstd[k][:, scale, t:t + 1],
                                            ALU.subtract, ALU.mult).then_inc(done, 1)

            def tok_v(a):
                dve.wait_ge(v_psum, a + 1)
                nc.vector.tensor_tensor(v[:], ta[3][:].rearrange("p (t d) -> p t d", d=D), over_tiles(row("bv")),
                                        ALU.add).then_inc(v_ready, 1)

            def tok_max(a, c):
                dve.wait_ge(score_psum, NT * a + c + 1)
                nc.vector.reduce_max(neg_max[:, c:c + 1], ta[c][:], AX, negate=True).then_inc(max_ready, 1)

            def tok_probsT(a):
                for j in range(NT // 2):
                    dve.wait_ge(probsT_psum, NT * a + j + 1)
                    nc.vector.tensor_copy(probsT[:, j], ta[j][:]).then_inc(probsT_dve, 1)

            def tok_norm1(a):
                dve.wait_ge(probs_ready, NT * a + NT)
                nc.vector.reciprocal(exp_inv[:], exp_sum[:]).then_inc(inv_ready, 1)
                dve.wait_ge(attn_psum, a + 1)
                dve.wait_ge(inv_ready, a + 1)
                for t in range(NT):
                    nc.vector.scalar_tensor_tensor(z1[:, t], ta[0][:, t * D:(t + 1) * D], exp_inv[:, t:t + 1],
                                                   x[:, t], ALU.mult, ALU.add).then_inc(z1_ready, 1)
                norm_stats(a, 1, lambda t: z1[:, t], z1_ready, lambda t: NT * a + t + 1)

            def tok_apply1(a):
                dve.wait_ge(rstd_ready[1], a + 1)
                if later(a):
                    dve.wait_ge(rres_ready, a)
                norm_apply(1, r_hat, lambda t: z1[:, t], 0, rhat_ready)

            def tok_norm2(a):
                dve.wait_ge(out_psum, a + 1)
                dve.wait_ge(rres_ready, a + 1)
                nc.vector.tensor_tensor(z2[:], ta[2][:].rearrange("p (t d) -> p t d", d=D), r_res[:], ALU.add
                                        ).then_inc(z2_ready, 1)
                norm_stats(a, 2, lambda t: z2[:, t], z2_ready, lambda t: a + 1)

            def tok_h(a):
                for t in range(NT):
                    nc.vector.scalar_tensor_tensor(h_scaled[:, t], z2[:, t], mv[2][:, t, 0:1], row("g"),
                                                   ALU.subtract, ALU.mult).then_inc(hscaled_ready, 1)

            def gau_h(b):
                dve.wait_ge(rstd_ready[2], b + 1)
                if later(b):
                    dve.wait_ge(hy_ready, 2 * b)
                for t in range(NT):
                    dve.wait_ge(hscaled_ready, NT * b + t + 1)
                    nc.vector.scalar_tensor_tensor(h[:, t], h_scaled[:, t], rstd[2][:, 0, t:t + 1], row("b"),
                                                   ALU.mult, ALU.add).then_inc(h_ready, 1)

            def gau_norm3(b):
                norm_stats(b, 3, lambda t: h[:, t], h_ready, lambda t: NT * b + t + 1)

            def gau_n(b):
                dve.wait_ge(rstd_ready[3], 2 * b + 1)
                norm_apply(3, n, lambda t: h[:, t], 1, n_ready)


            def gau_bias(b):
                dve.wait_ge(rstd_ready[3], 2 * b + 2)
                if later(b):
                    dve.wait_ge(y_ready, NT * b)
                nc.vector.scalar_tensor_tensor(y_bias[:], mv[3][:, :, 0], -1.0, rstd[3][:, 0], ALU.mult, ALU.mult
                                               ).then_inc(bias_ready, 1)

            def gau_sqk(b):
                dve.wait_ge(z_ready, b + 1)
                for k, t in ((0, sqT), (1, skT)):
                    nc.vector.tensor_scalar(t[:], zT[:], col(f"gamma_{k}"), col(f"beta_{k}"), ALU.mult, ALU.add
                                            ).then_inc(sqk_ready, 1)

            def gau_vpre(b):
                for i in range(2):
                    dve.wait_ge(gv_psum, 2 * b + i + 1)
                    nc.vector.tensor_tensor(v_pre[:, 2 * i:2 * i + 2, :],
                                            gb[i][:].rearrange("p (t d) -> p t d", d=HID),
                                            over_tiles(row("bhv"), 2), ALU.add).then_inc(vpre_ready, 1)

            def gau_relu(b):
                for j in range(NT):
                    dve.wait_ge(sim_psum, NT * b + j + 1)
                    nc.vector.tensor_scalar(relu[:, j], gb[(j + 2) % 4][:], 0.0, SIM_SCALE, ALU.max, ALU.mult
                                            ).then_inc(relu_ready, 1)

            def gau_gated(b, g):
                dve.wait_ge(mix_psum, NH * b + g + 1)
                nc.vector.tensor_tensor(gatedT[:, g], gb[2 + g][:], gateT[:, g], ALU.mult
                                        ).then_inc(gated_ready, 1)

            def gau_h2(b):
                dve.wait_ge(wo_psum, b + 1)
                dve.wait_ge(hy_ready, 2 * b + 2)
                if later(b):
                    dve.wait_ge(h2_kept, b)
                    dve.wait_ge(y2_ready, NT * b)
                nc.vector.tensor_tensor(h2_now[:], gb[0][:].rearrange("p (t d) -> p t d", d=D),
                                        hy_bo[:], ALU.add).then_inc(h2_ready, 1)

            def gau_norm5(b):
                norm_stats(b, 5, lambda t: h2_now[:, t], h2_ready, lambda t: b + 1)

            def gau_bias2(b):
                dve.wait_ge(rstd_ready[5], b + 1)
                nc.vector.scalar_tensor_tensor(y2_bias[:], mv[5][:, :, 0], -1.0, rstd[5][:, 0], ALU.mult, ALU.mult
                                               ).then_inc(bias2_ready, 1)

            def each(ap):
                return ap[:, :, None].to_broadcast([P, NT, E])

            def gau_route(b):
                done = ROUTE * b
                dve.wait_ge(logit_psum, b + 1)
                nc.vector.tensor_tensor(logits[:], ta[2][:, 0:NT * E].rearrange("p (t e) -> p t e", e=E),
                                        over_tiles(row("bg")), ALU.add).then_inc(logits_ready, 1)
                dve.wait_ge(logits_ready, b + 1)
                nc.vector.reduce_max(lmax[:], logits[:], AX).then_inc(route_step, 1)
                dve.wait_ge(route_step, done + 1)
                nc.vector.tensor_tensor(lshift[:], logits[:], each(lmax), ALU.subtract).then_inc(route_step, 1)
                nc.vector.tensor_tensor(is_max[:], logits[:], each(lmax), ALU.is_equal).then_inc(route_step, 1)
                dve.wait_ge(route_step, done + 3)
                nc.vector.tensor_tensor(ranked[:], is_max[:], over_tiles(cst("down")), ALU.mult
                                        ).then_inc(route_step, 1)
                dve.wait_ge(route_step, done + 4)
                nc.vector.reduce_max(best[:], ranked[:], AX).then_inc(route_step, 1)
                dve.wait_ge(route_step, done + 5)
                if later(b):
                    dve.wait_ge(rank_psum, b)
                nc.vector.tensor_tensor(route_bf[:], ranked[:], each(best), ALU.is_equal).then_inc(route_step, 1)

            def gau_pmax(b):
                dve.wait_ge(lexp_ready, b + 1)
                nc.vector.reduce_sum(lsum[:], lexp[:], AX).then_inc(pmax_step, 1)
                dve.wait_ge(pmax_step, 2 * b + 1)
                nc.vector.reciprocal(pmax[:], lsum[:]).then_inc(pmax_step, 1)

            def gau_slot(b):
                done = 5 * b
                dve.wait_ge(rank_psum, b + 1)
                dve.wait_ge(route_step, ROUTE * b + 6)
                nc.vector.tensor_tensor(slot_all[:], ta[2][:, 0:NT * E].rearrange("p (t e) -> p t e", e=E),
                                        over_tiles(filled[:]), ALU.add).then_inc(slot_step, 1)
                dve.wait_ge(slot_step, done + 1)
                nc.vector.tensor_tensor(filled[:], ta[2][:, NT * E:(NT + 1) * E], filled[:], ALU.add
                                        ).then_inc(slot_step, 1)
                nc.vector.tensor_tensor(slot_own[:], slot_all[:], route_bf[:], ALU.mult).then_inc(slot_step, 1)
                dve.wait_ge(slot_step, done + 3)
                nc.vector.reduce_sum(slot[:], slot_own[:], AX).then_inc(slot_step, 1)
                dve.wait_ge(slot_step, done + 4)
                if later(b):
                    dve.wait_ge(scattered, 16 * NT * b)
                nc.vector.tensor_copy(slot_u[:], slot[:]).then_inc(slot_step, 1)

            def both(a):
                b = a - 1
                if later(b - 1):
                    gau_pmax(b - 2)
                if later(b):
                    gau_h2(b - 1)
                if later(a):
                    gau_h(b)
                tok_v(a)
                if later(a):
                    gau_norm3(b)
                tok_max(a, 0)
                tok_max(a, 1)
                if later(a):
                    gau_n(b)
                tok_max(a, 2)
                tok_max(a, 3)
                if later(a):
                    gau_bias(b)
                if later(b):
                    gau_norm5(b - 1)
                if later(a):
                    gau_sqk(b)
                if later(b):
                    gau_bias2(b - 1)
                if later(a):
                    gau_vpre(b)
                tok_probsT(a)
                if later(a):
                    gau_relu(b)
                tok_norm1(a)
                if later(b):
                    gau_route(b - 1)
                tok_apply1(a)
                embed(a + 1)
                if later(a):
                    gau_gated(b, 0)
                if later(b):
                    gau_slot(b - 1)
                if later(a):
                    gau_gated(b, 1)
                tok_norm2(a)
                tok_h(a)

            embed(0)
            both(0)
            both(1)
            both(2)
            with dve.Fori(3, SEQS) as a:
                both(a)
            b = SEQS - 1
            gau_pmax(b - 2)
            gau_h2(b - 1)
            gau_h(b)
            gau_norm3(b)
            gau_n(b)
            gau_bias(b)
            gau_norm5(b - 1)
            gau_sqk(b)
            gau_bias2(b - 1)
            gau_vpre(b)
            gau_relu(b)
            gau_route(b - 1)
            gau_gated(b, 0)
            gau_slot(b - 1)
            gau_gated(b, 1)
            gau_pmax(b - 1)
            gau_h2(b)
            gau_norm5(b)
            gau_bias2(b)
            gau_route(b)
            gau_slot(b)
            gau_pmax(b)

            steps = [0]

            def then(ins_):
                steps[0] += 1
                ins_.then_inc(plan_step, 1)
                dve.wait_ge(plan_step, steps[0])

            V = nc.vector
            dve.wait_ge(slot_step, 5 * SEQS)
            then(V.tensor_tensor(count[:], filled[:], cst("base"), ALU.subtract))
            then(V.memset(start[:, 0:1], 0.0))
            for e in range(1, E):
                then(V.tensor_tensor(start[:, e:e + 1], start[:, e - 1:e], count[:, e - 1:e], ALU.add))
            then(V.tensor_tensor(end[:], start[:], count[:], ALU.add))
            used, first, last, ntile, since, until, shift, rowat = (pl[:, i] for i in range(8))
            then(V.tensor_scalar(used, count[:], 0.0, None, ALU.is_gt))
            then(V.tensor_scalar(last, end[:], -1.0, 0.0, ALU.add, ALU.max))
            bits = MROWS.bit_length() - 1
            for src, at, dst in ((start[:], 0, first), (last, 1, last)):
                then(V.tensor_copy(pli[:, at], src))
                then(V.tensor_scalar(pli[:, at], pli[:, at], bits, None, ALU.logical_shift_right))
                then(V.tensor_copy(dst, pli[:, at]))
            then(V.tensor_tensor(ntile, last, first, ALU.subtract))
            then(V.tensor_scalar(ntile, ntile, 1.0, None, ALU.add))
            then(V.tensor_tensor(ntile, ntile, used, ALU.mult))
            then(V.memset(since[:, 0:1], 0.0))
            for e in range(1, E):
                then(V.tensor_tensor(since[:, e:e + 1], since[:, e - 1:e], ntile[:, e - 1:e], ALU.add))
            then(V.tensor_tensor(until, since, ntile, ALU.add))
            then(V.tensor_tensor(shift, first, since, ALU.subtract))
            then(V.tensor_tensor(rowat, cst("base"), start[:], ALU.subtract))

            def by_step(ap):
                return ap[:, None, :].to_broadcast([P, TABLE, E])

            step_no = cst("step")
            step_e = step_no[:, :, None].to_broadcast([P, TABLE, E])
            of, ge, a_, b_, c_, _ = (po[:, i] for i in range(6))
            valid, expert, jshift, j, r0, m0 = (pv[:, i] for i in range(6))
            then(V.tensor_tensor(ge, step_e, by_step(since), ALU.is_ge))
            then(V.tensor_tensor(of, step_e, by_step(until), ALU.is_lt))
            then(V.tensor_tensor(of, of, ge, ALU.mult))
            then(V.reduce_sum(valid, of, AX))
            then(V.tensor_tensor(a_, of, by_step(cst("up")), ALU.mult))
            then(V.reduce_sum(expert, a_, AX))
            then(V.tensor_tensor(b_, of, by_step(shift), ALU.mult))
            then(V.reduce_sum(jshift, b_, AX))
            then(V.tensor_tensor(c_, of, by_step(rowat), ALU.mult))
            then(V.reduce_sum(r0, c_, AX))
            then(V.tensor_tensor(j, step_no, jshift, ALU.add))
            then(V.tensor_scalar(j, j, -float(MTILES - 1), None, ALU.add))
            then(V.tensor_tensor(j, j, valid, ALU.mult))
            then(V.tensor_scalar(j, j, float(MTILES - 1), None, ALU.add))
            then(V.tensor_scalar(m0, j, float(MROWS), None, ALU.mult))
            then(V.tensor_tensor(m0, m0, valid, ALU.mult))
            then(V.tensor_tensor(r0, r0, m0, ALU.add))
            then(V.tensor_copy(table[:, :, 0], r0))
            then(V.tensor_copy(table[:, :, 1], expert))
            then(V.tensor_copy(table[:, :, 3], j))
            then(V.tensor_scalar(valid, valid, -float(E), float(E), ALU.mult, ALU.add))
            then(V.tensor_tensor(expert, expert, valid, ALU.add))
            then(V.tensor_scalar(expert, expert, float(TILES), None, ALU.mult))
            then(V.tensor_scalar(j, j, float(MT), None, ALU.mult))
            then(V.tensor_tensor(j, j, expert, ALU.add))
            then(V.tensor_copy(table[:, :, 2], j))
            then(V.tensor_copy(tail[:], filled[:]))

            def by_row(ap):
                return ap[:, :, None].to_broadcast([P, E, TILES])

            row_e = cst("row")[:, None, :].to_broadcast([P, E, TILES])
            then(V.tensor_tensor(own[:, 0:E, :], row_e, by_row(start), ALU.is_ge))
            then(V.tensor_tensor(own2[:], row_e, by_row(end), ALU.is_lt))
            then(V.tensor_tensor(own[:, 0:E, :], own[:, 0:E, :], own2[:], ALU.mult))
            then(V.memset(own[:, E, :], 0.0))
            V.memset(pv[:, 0, 0:1], 0.0).then_inc(plan_ready, 1)

            own_flat = own[:].rearrange("p e t -> p (e t)")
            b2_at = ROWS["moe_b2"][0]

            def expert_in(s, i, u, part):
                e = dve.value_load(table[0:1, s, 1:2], min_val=0, max_val=E - 1)
                lo, w = ((0, UP), (UP, DOWN))[part]
                if later(i):
                    if part == 0:
                        dve.wait_ge(m_h_ready[u], NF * i)
                    else:
                        dve.wait_ge(m_y_psum[u], i)
                nc.vector.tensor_copy(m_w[:, u, lo:lo + w], experts[:, bass.ds(e * EXPERT + lo, w)]
                                      ).then_inc(m_w_ready[u], 1)

            def add_expert(s, i, u):
                e = dve.value_load(table[0:1, s, 1:2], min_val=0, max_val=E - 1)
                m = dve.value_load(table[0:1, s, 2:3], min_val=0, max_val=(E + 1) * TILES - MT)
                jj = dve.value_load(table[0:1, s, 3:4], min_val=0, max_val=MTILES - 1)
                dve.wait_ge(m_y_psum[u], i + 1)
                b2e = rows_in[:, bass.ds(b2_at + e * D, D)]
                nc.vector.tensor_tensor(m_y[:, u], bank[6 + u][:, 0:MT * D].rearrange("p (t d) -> p t d", d=D),
                                        over_tiles(b2e, MT), ALU.add).then_inc(m_y_ready[u], 1)
                dve.wait_ge(m_y_ready[u], i + 1)
                if later(s):
                    dve.wait_ge(m_stored, 16 * s)
                if later(s):
                    dve.wait_ge(m_added, MT * s)
                for t in range(MT):
                    at = h2[:, jj * MT + t, :]
                    nc.vector.scalar_tensor_tensor(at, m_y[:, u, t], own_flat[:, bass.ds(m + t, 1)], at,
                                                   ALU.mult, ALU.add).then_inc(m_added, 1)

            def pair(i):
                expert_in(2 * i + 2, i + 1, 0, 0)
                add_expert(2 * i, i, 0)
                expert_in(2 * i + 2, i + 1, 0, 1)
                expert_in(2 * i + 3, i + 1, 1, 0)
                add_expert(2 * i + 1, i, 1)
                expert_in(2 * i + 3, i + 1, 1, 1)

            dve.wait_ge(experts_loaded, 16)
            for u in range(2):
                expert_in(u, 0, u, 0)
                expert_in(u, 0, u, 1)
            pair(0)
            with dve.Fori(1, STEPS // 2) as i:
                pair(i)
            add_expert(STEPS - 1, STEPS // 2, 0)

        @block.tensor
        def _(pe):
            pe.wait_ge(loaded, 16 * LOADS)
            pe.wait_ge(prepared, 4)
            mm = nc.tensor.matmul

            def transposed(dst, src, done):
                for t in range(NT):
                    last = nc.tensor.transpose(dst[:, t * P:(t + 1) * P], src[:, t], ident)
                last.then_inc(done, 1)

            def tok_xT(a):
                pe.wait_ge(x_ready, a + 1)
                if later(a - 1):
                    pe.wait_ge(gated_ready, NH * (a - 1))
                transposed(gb[3], x, xT_psum)

            def tok_kqv(a):
                pe.wait_ge(xT_ready, a + 1)
                mm(ta[1][:], mat("wk"), xT[:], start=True, stop=True).then_inc(k_psum, 1)
                if later(a):
                    pe.wait_ge(z2_ready, a)
                mm(ta[2][:], mat("wq"), xT[:], start=True, stop=True).then_inc(q_psum, 1)
                for t in range(NT):
                    last = mm(ta[3][:, t * D:(t + 1) * D], xT[:, t * P:(t + 1) * P], mat("wv"),
                              start=True, stop=True)
                last.then_inc(v_psum, 1)

            def tok_scores(a):
                pe.wait_ge(kq_ready, 2 * a + 2)
                for c in range(NT):
                    if c == NT - 1:
                        pe.wait_ge(v_ready, a + 1)
                    mm(ta[c][:], kT[:, c * P:(c + 1) * P], qT[:], start=True, stop=True).then_inc(score_psum, 1)

            def tok_probsT(a):
                pe.wait_ge(probs_ready, NT * a + NT)
                for j in range(NT):
                    for i in range(NT):
                        last = nc.tensor.transpose(ta[j][:, i * P:(i + 1) * P], probs[:, i, j * P:(j + 1) * P],
                                                   ident)
                    last.then_inc(probsT_psum, 1)

            def tok_attend(a):
                for i in range(NT):
                    for j in range(NT):
                        last = mm(ta[0][:, i * D:(i + 1) * D], probsT[:, j, i * P:(i + 1) * P], v[:, j],
                                  start=(j == 0), stop=(j == NT - 1))
                last.then_inc(attn_psum, 1)

            def tok_rT(a):
                pe.wait_ge(rhat_ready, NT * a + NT)
                transposed(ta[1], r_hat, rT_psum)

            def tok_ff1(a):
                pe.wait_ge(rT_ready, a + 1)
                for f in range(NF):
                    mm(ta[(f + 2) % 4][:], mat("w1", f * P, (f + 1) * P), rT[:], start=True, stop=True
                       ).then_inc(ff_psum, 1)

            def tok_ff2(a):
                for f in range(NF):
                    pe.wait_ge(gelu_ready, NF * a + f + 1)
                    for i in range(NT):
                        last = mm(ta[2][:, i * D:(i + 1) * D], geluT[:, f, i * P:(i + 1) * P],
                                  mat("w2", f * D, (f + 1) * D), start=(f == 0 and i == 0), stop=(f == NF - 1),
                                  skip_group_check=True)
                last.then_inc(out_psum, 1)

            def gau_nT(b):
                pe.wait_ge(n_ready, NT * b + NT)
                if later(b):
                    pe.wait_ge(h2_ready, b)
                transposed(gb[0], n, nT_psum)

            def gau_project(b):
                pe.wait_ge(nT_ready, b + 1)
                mm(gb[1][:], mat("wqk"), nT[:], start=True, stop=True).then_inc(z_psum, 1)
                for g in range(NH):
                    mm(gb[2 + g][:], mat("wh", HID + g * P, HID + (g + 1) * P), nT[:], start=True, stop=True
                       ).then_inc(gate_psum, 1)
                for i in range(2):
                    if i == 1:
                        pe.wait_ge(z_ready, b + 1)
                    for t in (2 * i, 2 * i + 1):
                        last = mm(gb[i][:, (t % 2) * HID:(t % 2 + 1) * HID], nT[:, t * P:(t + 1) * P],
                                  mat("wh", 0, HID), start=True, stop=True)
                    last.then_inc(gv_psum, 1)

            def gau_sim(b):
                pe.wait_ge(sqk_ready, 2 * b + 2)
                pe.wait_ge(gate_ready, NH * b + NH)
                pe.wait_ge(vpre_ready, 2 * b + 2)
                for j in range(NT):
                    mm(gb[(j + 2) % 4][:], skT[:, j * P:(j + 1) * P], sqT[:], start=True, stop=True
                       ).then_inc(sim_psum, 1)

            def gau_mix(b, after_first, before_last):
                pe.wait_ge(gv_ready, 2 * b + 2)
                pe.wait_ge(aT_pool, 2 * b + 2)
                pe.wait_ge(aT_act, 2 * b + 2)
                for g in range(NH):
                    if g == 1:
                        after_first()
                    for j in range(NT):
                        if g == NH - 1 and j == NT // 2:
                            before_last()
                        last = mm(gb[2 + g][:], gv[:, j, g * P:(g + 1) * P], aT[:, j], start=(j == 0),
                                  stop=(j == NT - 1))
                    last.then_inc(mix_psum, 1)

            def gau_wo(b):
                pe.wait_ge(gated_ready, NH * b + NH)
                for i in range(NT):
                    for g in range(NH):
                        last = mm(gb[0][:, i * D:(i + 1) * D], gatedT[:, g, i * P:(i + 1) * P],
                                  mat("wo", g * D, (g + 1) * D), start=(g == 0), stop=(g == NH - 1))
                last.then_inc(wo_psum, 1)

            def gau_y2T(b):
                pe.wait_ge(y2_ready, NT * b + NT)
                transposed(ta[3], y2, y2T_psum)

            def gau_logits(b):
                pe.wait_ge(y2T_ready, b + 1)
                for t in range(NT):
                    last = mm(ta[2][:, t * E:(t + 1) * E], y2T[:, t * P:(t + 1) * P], mat("wg"),
                              start=True, stop=True)
                last.then_inc(logit_psum, 1)

            def gau_rank(b):
                pe.wait_ge(route_step, ROUTE * b + 6)
                mm(ta[2][:, 0:NT * E], before_bf[:], route_bf[:].rearrange("p t e -> p (t e)"),
                   start=True, stop=False, skip_group_check=True)
                for t in range(NT):
                    last = mm(ta[2][:, (t + 1) * E:(NT + 1) * E], ones_bf[:],
                              route_bf[:, t:t + 1, :].to_broadcast([P, NT - t, E]),
                              start=False, stop=(t == NT - 1), skip_group_check=True)
                last.then_inc(rank_psum, 1)

            def both(a):
                b = a - 1
                tok_kqv(a)
                tok_scores(a)
                if later(a):
                    gau_nT(b)
                    gau_project(b)
                tok_probsT(a)
                if later(a):
                    gau_sim(b)
                pe.wait_ge(probsT_dve, NT // 2 * (a + 1))
                pe.wait_ge(probsT_act, NT // 2 * (a + 1))
                if later(b):
                    gau_y2T(b - 1)
                tok_attend(a)
                if later(b):
                    gau_logits(b - 1)
                if later(a):
                    gau_mix(b, lambda: gau_rank(b - 1) if later(b) else None, lambda: tok_rT(a))
                else:
                    tok_rT(a)
                if later(b):
                    pe.wait_ge(slot_step, 5 * b)
                tok_ff1(a)
                tok_xT(a + 1)
                tok_ff2(a)
                if later(a):
                    gau_wo(b)

            tok_xT(0)
            both(0)
            both(1)
            both(2)
            with pe.Fori(3, SEQS) as a:
                both(a)
            b = SEQS - 1
            pe.wait_ge(z2_ready, b + 1)
            gau_nT(b)
            gau_project(b)
            gau_y2T(b - 1)
            gau_sim(b)
            gau_logits(b - 1)
            gau_mix(b, lambda: gau_rank(b - 1), lambda: None)
            gau_wo(b)
            gau_y2T(b)
            pe.wait_ge(slot_step, 5 * b)
            gau_logits(b)
            gau_rank(b)

            def expert_xT(i, u):
                pe.wait_ge(m_loaded[u], 16 * (i + 1))
                if later(i):
                    pe.wait_ge(m_xT_ready[u], i)
                for t in range(MT):
                    last = nc.tensor.transpose(bank[u][:, t * P:(t + 1) * P], m_rows[:, u, t], ident)
                last.then_inc(m_xT_psum[u], 1)

            def expert_up(i, u):
                pe.wait_ge(m_xT_ready[u], i + 1)
                pe.wait_ge(m_w_ready[u], 2 * i + 1)
                if later(i):
                    pe.wait_ge(m_h_ready[u], NF * i)
                for f in range(NF):
                    at = (f % 2) * MROWS
                    last = mm(bank[2 + 2 * u + f // 2][:, at:at + MROWS], m_w[:, u, f * P:(f + 1) * P],
                              m_xT[:, u], start=True, stop=True)
                    if f % 2:
                        last.then_inc(m_h_psum[u], 1)

            def expert_down(i, u):
                pe.wait_ge(m_h_ready[u], NF * (i + 1))
                pe.wait_ge(m_w_ready[u], 2 * i + 2)
                if later(i):
                    pe.wait_ge(m_y_ready[u], i)
                for t in range(MT):
                    for f in range(NF):
                        last = mm(bank[6 + u][:, t * D:(t + 1) * D], m_hT[:, u, f, t * P:(t + 1) * P],
                                  m_w[:, u, UP + f * D:UP + (f + 1) * D], start=(f == 0), stop=(f == NF - 1))
                last.then_inc(m_y_psum[u], 1)

            pe.wait_ge(plan_ready, 1)
            expert_xT(0, 0)
            expert_up(0, 0)
            expert_xT(0, 1)

            def pair(i):
                expert_up(i, 1)
                expert_xT(i + 1, 0)
                expert_down(i, 0)
                expert_up(i + 1, 0)
                expert_xT(i + 1, 1)
                expert_down(i, 1)

            pair(0)
            with pe.Fori(1, STEPS // 2) as i:
                pair(i)
            expert_down(STEPS // 2, 0)


def constants():
    c = np.zeros((P, CONST_W), np.float32)

    def put(name, a):
        at, w = CONST[name]
        c[:, at:at + w] = a

    pos = np.arange(S, dtype=np.float32)[:, None]
    i = np.arange(D, dtype=np.float32)[None, :]
    ang = (pos / np.power(np.float32(10000.0), np.float32(2.0) * i / np.float32(D))).astype(np.float64)
    pe = np.where((np.arange(D) % 2 == 0)[None, :], np.sin(ang), np.cos(ang)) * D ** 0.5
    put("pos", pe.reshape(NT, P, D).transpose(1, 0, 2).reshape(P, NT * D))
    put("ident", np.eye(P))
    put("before", np.triu(np.ones((P, P)), 1))
    put("base", np.arange(E) * REGION + PAD)
    put("down", E - np.arange(E))
    put("up", np.arange(E))
    put("row", np.arange(TILES)[None, :] * P + np.arange(P)[:, None])
    put("step", np.arange(TABLE))
    return c


def kernel(**inputs):
    import concourse.bacc as _bacc
    from concourse.bass_utils import run_bass_kernel_spmd as _run

    g = {k: np.asarray(a) for k, a in inputs.items()}
    tok = {k[7:]: a for k, a in g.items() if k.startswith("L0_tok_")}
    att = {k[8:]: a for k, a in g.items() if k.startswith("L0_attn_")}
    ffn = {k[7:]: a for k, a in g.items() if k.startswith("L0_ffn_")}

    def chunks(w):
        return w.reshape(-1, P, w.shape[1]).transpose(1, 0, 2).reshape(P, -1)

    col_of = {"bk": tok["bk"], "bq": tok["bq"], "g": tok["ln_g"], "b": tok["ln_b"], "ag": att["ln_g"],
              "ab": att["ln_b"], "bqk": att["bqk"]}
    for f in range(NF):
        col_of[f"b1_{f}"] = tok["b1"][f * P:(f + 1) * P]
    for k in range(NH):
        col_of[f"bh_{k}"] = att["bh"][HID + k * P:HID + (k + 1) * P]
    for k in range(2):
        col_of[f"gamma_{k}"] = att["gamma"][k]
        col_of[f"beta_{k}"] = att["beta"][k]
    row_of = {"bv": tok["bv"], "g": tok["ln_g"], "b": tok["ln_b"], "b2": tok["b2"], "bo": att["bo"],
              "bhv": att["bh"][:HID], "bg": ffn["bg"], "moe_b2": ffn["b2"].reshape(-1)}
    mat_of = {"wk": tok["wk"], "wq": tok["wq"], "wv": tok["wv"], "w1": tok["w1"], "w2": chunks(tok["w2"]),
              "wh": att["Wh"], "wqk": att["Wqk"], "wo": chunks(att["Wo"]), "wg": ffn["Wg"]}
    w1 = ffn["W1"].transpose(1, 0, 2)
    w2 = ffn["W2"].reshape(E, NF, P, D).transpose(2, 0, 1, 3).reshape(P, E, NF * D)
    b1 = ffn["b1"].reshape(E, NF, P).transpose(2, 0, 1)
    tokens = np.zeros((P, (SEQS + 1) * NT), np.int32)
    tokens[:, :TILES] = g["x"].reshape(TILES, P).T
    arrays = {
        "tokens": tokens,
        "const": constants(),
        "mats": np.ascontiguousarray(np.concatenate([mat_of[k] for k in MATS], axis=1)),
        "cols": np.ascontiguousarray(np.stack([col_of[k] for k in COLS], axis=1)),
        "rows": np.concatenate([row_of[k] for k in ROWS]),
        "experts": np.ascontiguousarray(np.concatenate([w1, b1, w2], axis=2).reshape(P, E * EXPERT)),
        "emb": np.ascontiguousarray(tok["emb"]),
    }
    nc = _bacc.Bacc("TRN2", target_bir_lowering=False, num_devices=1)
    ins = {k: nc.dram_tensor(f"in_{k}_dram", a.shape, mybir.dt.from_np(a.dtype), kind="ExternalInput").ap()
           for k, a in arrays.items()}
    out = nc.dram_tensor("out_0_dram", (SEQS * S, D), F32, kind="ExternalOutput").ap()
    build(nc, ins, out)
    r = _run(nc, [{f"in_{k}_dram": a for k, a in arrays.items()}], core_ids=[0])
    return r.results[0]["out_0_dram"].reshape(SEQS, S, D)
```

```python
from contextlib import ExitStack

import concourse.bass as bass
import numpy as np
from concourse import mybir

ALU = mybir.AluOpType
ACT = mybir.ActivationFunctionType
AX = mybir.AxisListType.X
F32 = mybir.dt.float32
F32R = mybir.dt.float32r
BF16 = mybir.dt.bfloat16
I32 = mybir.dt.int32
U32 = mybir.dt.uint32

P = 128
VOCAB = 50257
SEQS, S, D = 16, 512, 128
NT = S // P
TILES = SEQS * NT
DFF = 512
NF = DFF // P
HID = 256
NH = HID // P
E = 8
EPS = 1e-5
SCORE_SCALE = float(D) ** -0.5
SIM_SCALE = 1.0 / S

MT = 2
MROWS = MT * P
MTILES = TILES // MT
STEPS = MTILES + E - 1
PAD = MROWS
REGION = SEQS * S + 2 * PAD
TABLE = STEPS + 2
FACTS = 5
UP, REST = DFF + NF, (NF + 1) * D
EXPERT = UP + REST

COLS = ["bk", "bq", "g", "b", "b1_0", "b1_1", "b1_2", "b1_3", "ag", "ab", "bqk", "bh_0", "bh_1",
        "gamma_0", "beta_0", "gamma_1", "beta_1"]
ROWS = {}
_at = 0
for _n, _w in (("bv", D), ("g", D), ("b", D), ("b2", D), ("bo", D), ("bhv", HID), ("bg", E)):
    ROWS[_n] = (_at, _w)
    _at += _w
ROWS_W = _at
SPLIT = {}
_at = 0
for _n, _w in (("wk", D), ("wq", D), ("w1", DFF), ("wh", 2 * HID), ("wqk", D)):
    SPLIT[_n] = (_at, _w)
    _at += _w
SPLIT_W = _at
MATS = {}
_at = 0
for _n, _w in (("wv", D), ("w2", NF * D), ("wo", NH * D), ("wg", E)):
    MATS[_n] = (_at, _w)
    _at += _w
MATS_W = _at
CONST = {}
_at = 0
for _n, _w in (("pos", NT * D), ("ident", P), ("before", P), ("base", E), ("down", E), ("up", E),
               ("earlier", E * E), ("row", MT), ("step", TABLE)):
    CONST[_n] = (_at, _w)
    _at += _w
CONST_W = _at


def build(nc, ins, out):
    with ExitStack() as ctx:
        def sb(name, shape, dt=F32):
            return ctx.enter_context(nc.sbuf_tensor(name, shape, dt))

        def sem(name):
            return ctx.enter_context(nc.semaphore(name))

        routed = nc.dram_tensor("routed_rows", [E * REGION, D], F32, kind="Internal").ap()

        cols = sb("cols", [P, len(COLS)])
        rows_in = sb("rows_in", [P, ROWS_W])
        mats = sb("mats", [P, MATS_W])
        const = sb("const", [P, CONST_W])
        experts = sb("experts", [P, E * EXPERT])
        whole = experts[:, 0:SPLIT_W]
        w_hi = sb("w_hi", [P, SPLIT_W], F32R)
        w_lo = sb("w_lo", [P, SPLIT_W], F32R)
        tokens = sb("tokens", [P, (SEQS + 2) * NT], I32)

        def col(name):
            i = COLS.index(name)
            return cols[:, i:i + 1]

        def row(name):
            at, w = ROWS[name]
            return rows_in[:, at:at + w]

        def mat(name, lo=0, hi=None):
            at, w = MATS[name]
            return mats[:, at + lo:at + (w if hi is None else hi)]

        def part(of, name, lo=0, hi=None):
            at, w = SPLIT[name]
            return of[:, at + lo:at + (w if hi is None else hi)]

        def cst(name):
            at, w = CONST[name]
            return const[:, at:at + w]

        def over_tiles(ap, n=NT):
            return ap[:, None, :].to_broadcast([P, n, ap.shape[1]])

        ident = cst("ident")
        before_bf = sb("before_bf", [P, P], BF16)
        ones_bf = sb("ones_bf", [P, P], BF16)
        b_b2 = sb("b_b2", [P, D])
        bk_scaled = sb("bk_scaled", [P, 1])
        minus_half = sb("minus_half", [P, NT])
        zeros = sb("zeros", [P, MT * D])
        f_hi = sb("f_hi", [P, S], F32R)
        f_lo = sb("f_lo", [P, S], F32R)

        token_now = sb("token_now", [P, NT], I32)
        emb = sb("emb_rows", [P, NT, D])
        x = sb("x", [P, NT, D])
        x_bv = sb("x_bv", [P, NT, D])
        xT = sb("xT", [P, S])
        kT = sb("kT", [P, S])
        qT = sb("qT", [P, S])
        v = sb("v", [P, NT, D])
        neg_max = sb("neg_max", [P, NT])
        exp_sum = sb("exp_sum", [P, NT])
        exp_inv = sb("exp_inv", [P, NT])
        probs = sb("probs", [P, NT, S])
        probs_flat = probs[:].rearrange("p t s -> p (t s)")
        probsT = sb("probsT", [P, NT, S])
        z1 = sb("z1", [P, NT, D])
        r_hat = sb("r_hat", [P, NT, D])
        r_res = sb("r_res", [P, NT, D])
        geluT = sb("geluT", [P, NF, S])
        z2 = sb("z2", [P, NT, D])
        h_scaled = sb("h_scaled", [P, NT, D])
        h = sb("h", [P, NT, D])
        y = sb("y", [P, NT, D])
        n = sb("n", [P, NT, D])
        hy_bo = sb("hy_bo", [P, NT, D])
        zT = sb("zT", [P, S])
        sqT = sb("sqT", [P, S])
        skT = sb("skT", [P, S])
        gateT = sb("gateT", [P, NH, S])
        v_pre = sb("v_pre", [P, NT, HID])
        gv = sb("gv", [P, NT, HID])
        relu = sb("relu", [P, NT, S])
        aT = sb("aT", [P, NT, S])
        gatedT = sb("gatedT", [P, NH, S])
        wide = gatedT[:, 0, 0:P]
        h2 = sb("h2", [P, TILES, D])
        h2_now = sb("h2_now", [P, NT, D])
        y2 = sb("y2", [P, NT, D])
        y2T = sb("y2T", [P, S])
        xs = sb("xs", [P, NT, D])
        stats = {k: sb(f"stats{k}", [P, NT, 6]) for k in (1, 2, 3, 5)}
        mv = {k: sb(f"mv{k}", [P, NT, 2]) for k in (1, 2, 3, 5)}
        norms = {1: 1, 2: 1, 3: 2, 5: 1}
        var_eps = {k: sb(f"var_eps{k}", [P, w, NT]) for k, w in norms.items()}
        rstd = {k: sb(f"rstd{k}", [P, w, NT]) for k, w in norms.items()}
        y_bias = sb("y_bias", [P, NT])
        y2_bias = sb("y2_bias", [P, NT])
        logits = sb("logits", [P, NT, E])
        lmax = sb("lmax", [P, NT])
        lshift = sb("lshift", [P, NT, E])
        lexp = sb("lexp", [P, NT, E])
        lsum = sb("lsum", [P, NT])
        pmax = sb("pmax", [P, NT])
        is_max = sb("is_max", [P, NT, E])
        ranked = sb("ranked", [P, NT, E])
        best = sb("best", [P, NT])
        route = sb("route", [P, NT, E])
        route_bf = sb("route_bf", [P, NT, E], BF16)
        filled = sb("filled", [P, E])
        slot_all = sb("slot_all", [P, NT, E])
        slot_own = sb("slot_own", [P, NT, E])
        slot = sb("slot", [P, NT])
        slot_u = sb("slot_u", [P, NT], U32)
        count = sb("count", [P, E])
        used = sb("used", [P, E])
        ntile = sb("ntile", [P, E])
        summed = sb("summed", [P, E, E])
        tiles_of = sb("tiles_of", [P, 2, E])
        tiles_int = sb("tiles_int", [P, 2, E], I32)
        since = sb("since", [P, E])
        facts = sb("facts", [P, FACTS, E])
        rise = sb("rise", [P, FACTS, E])
        begun = sb("begun", [P, TABLE, E])
        risen = geluT[:].rearrange("p f s -> p (f s)")[:, 0:FACTS * TABLE * E].rearrange(
            "p (i s e) -> p i s e", s=TABLE, e=E)
        at_step = sb("at_step", [P, FACTS, TABLE])
        tile_at = sb("tile_at", [P, TABLE])
        table = sb("table", [P, 3, TABLE], I32)
        tail = sb("tail", [P, E], I32)
        row_at = sb("row_at", [P, TABLE, MT])
        own = sb("own", [P, TABLE, MT])
        own2 = sb("own2", [P, TABLE, MT])
        again = sb("again", [P, TABLE])
        m_rows = probsT[:, 0].rearrange("p (u t d) -> p u t d", u=2, t=MT)
        m_x_hi = f_hi[:].rearrange("p (u r) -> p u r", u=2)
        m_x_lo = f_lo[:].rearrange("p (u r) -> p u r", u=2)
        m_w1_hi = w_hi[:, 0:2 * DFF].rearrange("p (u w) -> p u w", u=2)
        m_w1_lo = w_lo[:, 0:2 * DFF].rearrange("p (u w) -> p u w", u=2)
        m_rest = probs_flat[:, 0:2 * REST].rearrange("p (u w) -> p u w", u=2)
        m_hT = relu[:].rearrange("p t (a r) -> p t a r", r=MROWS).rearrange("p (u t) a r -> p u (t a) r", u=2)
        m_y = probsT[:, 2].rearrange("p (u t d) -> p u t d", u=2, t=MT)
        m_kept = probsT[:, 3, 0:MT * D].rearrange("p (t d) -> p t d", t=MT)
        m_b1 = aT[:, 2, 0:2 * NF].rearrange("p (u f) -> p u f", u=2)
        m_sum = aT[:, 0].rearrange("p (u t d) -> p u t d", u=2, t=MT)
        m_out = aT[:, 1].rearrange("p (u t d) -> p u t d", u=2, t=MT)

        bank = [ctx.enter_context(nc.psum_tensor(f"bank{i}", [P, 512], F32)) for i in range(8)]
        ta, gb = bank[:4], bank[4:]

        tokens_loaded = sem("tokens_loaded")
        const_loaded = sem("const_loaded")
        mats_loaded = sem("mats_loaded")
        split_loaded = sem("split_loaded")
        cols_loaded = sem("cols_loaded")
        rows_loaded = sem("rows_loaded")
        experts_loaded = sem("experts_loaded")
        prepared = sem("prepared")
        wide_ready = sem("wide_ready")
        scaled_ready = sem("scaled_ready")
        hi_ready = sem("hi_ready")
        split_ready = sem("split_ready")
        fold_psum = sem("fold_psum")
        folded = sem("folded")
        prepared_pool = sem("prepared_pool")
        token_ready = sem("token_ready")
        emb_ready = sem("emb_ready")
        x_ready = sem("x_ready")
        xbv_ready = sem("xbv_ready")
        xT_psum = sem("xT_psum"); xT_ready = sem("xT_ready"); xT_lo_ready = sem("xT_lo_ready")
        xT_whole_ready = sem("xT_whole_ready")
        k_psum = sem("k_psum"); q_psum = sem("q_psum"); v_psum = sem("v_psum")
        kq_ready = sem("kq_ready")
        v_ready = sem("v_ready")
        score_psum = sem("score_psum")
        max_ready = sem("max_ready")
        probs_ready = sem("probs_ready")
        probsT_psum = sem("probsT_psum")
        probsT_dve = sem("probsT_dve")
        probsT_act = sem("probsT_act")
        attn_psum = sem("attn_psum")
        inv_ready = sem("inv_ready")
        z1_ready = sem("z1_ready")
        stats_ready = {k: sem(f"stats{k}_ready") for k in (1, 2, 3, 5)}
        mv_ready = {k: sem(f"mv{k}_ready") for k in (1, 2, 3, 5)}
        var_ready = {k: sem(f"var{k}_ready") for k in (1, 2, 3, 5)}
        rstd_ready = {k: sem(f"rstd{k}_ready") for k in (1, 2, 3, 5)}
        rhat_ready = sem("rhat_ready")
        rscaled_ready = sem("rscaled_ready"); rres_ready = sem("rres_ready")
        rT_psum = sem("rT_psum"); rT_ready = sem("rT_ready"); rT_lo_ready = sem("rT_lo_ready")
        ff_psum = sem("ff_psum")
        gelu_ready = sem("gelu_ready")
        out_psum = sem("out_psum")
        z2_ready = sem("z2_ready")
        hscaled_ready = sem("hscaled_ready"); h_ready = sem("h_ready")
        bias_ready = sem("bias_ready"); bias2_ready = sem("bias2_ready")
        y_ready = sem("y_ready")
        n_ready = sem("n_ready")
        hy_ready = sem("hy_ready")
        nT_psum = sem("nT_psum"); nT_ready = sem("nT_ready"); nT_lo_ready = sem("nT_lo_ready")
        z_psum = sem("z_psum"); z_ready = sem("z_ready")
        gate_psum = sem("gate_psum"); gate_ready = sem("gate_ready")
        gv_psum = sem("gv_psum"); vpre_ready = sem("vpre_ready"); gv_ready = sem("gv_ready")
        sqk_ready = sem("sqk_ready")
        sim_psum = sem("sim_psum")
        relu_ready = sem("relu_ready")
        aT_pool = sem("aT_pool"); aT_act = sem("aT_act")
        mix_psum = sem("mix_psum"); gated_ready = sem("gated_ready")
        wo_psum = sem("wo_psum"); h2_ready = sem("h2_ready"); h2_kept = sem("h2_kept")
        y2_ready = sem("y2_ready")
        y2T_psum = sem("y2T_psum"); y2T_ready = sem("y2T_ready")
        logit_psum = sem("logit_psum")
        logits_ready = sem("logits_ready")
        route_step = sem("route_step")
        lexp_ready = sem("lexp_ready")
        pmax_step = sem("pmax_step")
        rank_psum = sem("rank_psum")
        slot_step = sem("slot_step")
        xs_ready = sem("xs_ready")
        scattered = sem("scattered")
        padded = sem("padded")
        tail_ready = sem("tail_ready")
        own_ready = sem("own_ready")
        plan_step = sem("plan_step")
        plan_ready = sem("plan_ready")
        m_loaded = [sem(f"m_loaded{u}") for u in range(2)]
        m_w1_ready = [sem(f"m_w1_ready{u}") for u in range(2)]
        m_b1_ready = [sem(f"m_b1_ready{u}") for u in range(2)]
        m_rest_ready = [sem(f"m_rest_ready{u}") for u in range(2)]
        m_xT_psum = [sem(f"m_xT_psum{u}") for u in range(2)]
        m_xT_ready = [sem(f"m_xT_ready{u}") for u in range(2)]
        m_xlo_ready = [sem(f"m_xlo_ready{u}") for u in range(2)]
        m_h_psum = [sem(f"m_h_psum{u}") for u in range(2)]
        m_h_ready = [sem(f"m_h_ready{u}") for u in range(2)]
        m_y_psum = [sem(f"m_y_psum{u}") for u in range(2)]
        m_y_ready = [sem(f"m_y_ready{u}") for u in range(2)]
        m_kept_ready = sem("m_kept_ready")
        m_sum_ready = sem("m_sum_ready")
        m_out_ready = sem("m_out_ready")
        m_stored = sem("m_stored")

        ROUTE = 6

        waited = {e: sem(f"waited_{e}") for e in ("sp", "pool", "dve")}

        def at_(s):
            return slice(s, s + 1) if isinstance(s, int) else bass.ds(s, 1)

        def later(i):
            return not (isinstance(i, int) and i <= 0)

        def apart(eng, name):
            eng.sem_inc(waited[name], 1)

        def zero_tails(eng, lo, hi):
            for e in range(lo, hi):
                at = eng.value_load(tail[0:1, e:e + 1], min_val=e * REGION + PAD, max_val=(e + 1) * REGION - PAD)
                eng.dma_start(routed[bass.ds(at, PAD), :].rearrange("(t p) d -> p t d", p=P),
                              zeros[:].rearrange("p (t d) -> p t d", d=D)).then_inc(padded, 16)

        block = ctx.enter_context(nc.Block())

        @block.sync
        def _(sp):
            sp.dma_start(tokens[:], ins["tokens"]).then_inc(tokens_loaded, 16)
            sp.dma_start(const[:], ins["const"]).then_inc(const_loaded, 16)
            sp.dma_start(whole, ins["split"]).then_inc(split_loaded, 16)
            sp.wait_ge(x_ready, 1)
            sp.dma_start(mats[:], ins["mats"]).then_inc(mats_loaded, 16)
            sp.wait_ge(prepared_pool, 2)
            for e in range(E):
                sp.dma_start(routed[e * REGION:e * REGION + PAD, :].rearrange("(t p) d -> p t d", p=P),
                             zeros[:].rearrange("p (t d) -> p t d", d=D)).then_inc(padded, 16)
            sp.wait_ge(split_ready, 3)
            sp.wait_ge(fold_psum, 2)
            sp.dma_start(experts[:], ins["experts"]).then_inc(experts_loaded, 16)
            sp.wait_ge(tail_ready, 1)
            zero_tails(sp, 0, E // 2)
            sp.wait_ge(plan_ready, 3)
            sp.wait_ge(padded, 2 * E * 16)
            sp.wait_ge(scattered, SEQS * NT * 16)

            def load(s, i, u):
                at = sp.value_load(table[0:1, 0, at_(s)], min_val=0, max_val=E * REGION - MROWS)
                if later(i):
                    sp.wait_ge(m_xT_psum[u], i)
                apart(sp, "sp")
                sp.dma_start(m_rows[:, u], routed[bass.ds(at, MROWS), :].rearrange("(t p) d -> p t d", p=P)
                             ).then_inc(m_loaded[u], 16)

            load(0, 0, 0)
            load(1, 0, 1)

            def pair(i):
                load(2 * i + 2, i + 1, 0)
                load(2 * i + 3, i + 1, 1)

            pair(0)
            with sp.Fori(1, STEPS // 2) as i:
                pair(i)
            sp.wait_ge(m_loaded[1], 16 * (STEPS // 2 + 1))

        @block.gpsimd
        def _(pool):
            nc.gpsimd.memset(minus_half[:], -0.5).then_inc(prepared_pool, 1)
            nc.gpsimd.memset(zeros[:], 0.0).then_inc(prepared_pool, 1)

            def gather(i):
                if later(i):
                    pool.wait_ge(x_ready, i)
                apart(pool, "pool")
                nc.gpsimd.tensor_copy(token_now[:], tokens[:, bass.ds(i * NT, NT)]).then_inc(token_ready, 1)
                pool.wait_ge(token_ready, i + 1)
                apart(pool, "pool")
                for t in range(NT):
                    nc.gpsimd.indirect_dma_start(
                        out=emb[:, t, :], out_offset=None, in_=ins["emb"],
                        in_offset=bass.IndirectOffsetOnAxis(ap=token_now[:, t:t + 1].bitcast(U32), axis=0),
                        bounds_check=VOCAB - 1, oob_is_err=False).then_inc(emb_ready, 16)

            def inv_std(i, k):
                for n_, w in enumerate(reversed(range(norms[k]))):
                    pool.wait_ge(var_ready[k], norms[k] * i + n_ + 1)
                    nc.gpsimd.tensor_tensor(rstd[k][:, w], var_eps[k][:, w], minus_half[:], ALU.pow
                                            ).then_inc(rstd_ready[k], 1)

            def add_bv(i):
                pool.wait_ge(x_ready, i + 1)
                if later(i):
                    pool.wait_ge(z1_ready, NT * i)
                nc.gpsimd.tensor_tensor(x_bv[:], x[:], over_tiles(row("bv")), ALU.add).then_inc(xbv_ready, 1)

            def tok_residual(a):
                pool.wait_ge(rhat_ready, NT * a + NT)
                if later(a):
                    pool.wait_ge(z2_ready, a)
                nc.gpsimd.tensor_tensor(r_res[:], r_hat[:], over_tiles(row("g")), ALU.mult
                                        ).then_inc(rscaled_ready, 1)
                pool.wait_ge(rscaled_ready, a + 1)
                nc.gpsimd.tensor_tensor(r_res[:], r_res[:], over_tiles(b_b2[:]), ALU.add
                                        ).then_inc(rres_ready, 1)

            def gau_residual(b):
                pool.wait_ge(y_ready, NT * b + NT)
                if later(b):
                    pool.wait_ge(h2_ready, b)
                nc.gpsimd.tensor_tensor(hy_bo[:], h[:], y[:], ALU.add).then_inc(hy_ready, 1)
                pool.wait_ge(hy_ready, 2 * b + 1)
                nc.gpsimd.tensor_tensor(hy_bo[:], hy_bo[:], over_tiles(row("bo")), ALU.add).then_inc(hy_ready, 1)

            def keep_h2(b):
                pool.wait_ge(h2_ready, b + 1)
                apart(pool, "pool")
                nc.gpsimd.tensor_copy(h2[:, bass.ds(b * NT, NT), :], h2_now[:]).then_inc(h2_kept, 1)

            def gau_square(b):
                for j in range(NT // 2):
                    pool.wait_ge(relu_ready, NT * b + j + 1)
                    nc.gpsimd.tensor_tensor(aT[:, j], relu[:, j], relu[:, j], ALU.mult).then_inc(aT_pool, 1)

            def gau_xs(b):
                pool.wait_ge(pmax_step, 2 * b + 2)
                if later(b):
                    pool.wait_ge(scattered, 16 * NT * b)
                nc.gpsimd.tensor_tensor(xs[:], y2[:], pmax[:, :, None].to_broadcast([P, NT, D]), ALU.mult
                                        ).then_inc(xs_ready, 1)

            def gau_scatter(b):
                pool.wait_ge(xs_ready, b + 1)
                pool.wait_ge(slot_step, 5 * b + 5)
                apart(pool, "pool")
                for t in range(NT):
                    nc.gpsimd.indirect_dma_start(
                        out=routed, out_offset=bass.IndirectOffsetOnAxis(ap=slot_u[:, t:t + 1], axis=0),
                        in_=xs[:, t, :], in_offset=None, bounds_check=E * REGION - 1, oob_is_err=False,
                    ).then_inc(scattered, 16)

            def both(a):
                b = a - 1
                if later(a):
                    inv_std(b, 3)
                if later(b - 1):
                    gau_xs(b - 2)
                if later(b):
                    keep_h2(b - 1)
                    inv_std(b - 1, 5)
                if later(b - 1):
                    gau_scatter(b - 2)
                if later(a):
                    gau_square(b)
                inv_std(a, 1)
                if later(a):
                    gau_residual(b)
                tok_residual(a)
                add_bv(a + 1)
                gather(a + 2)
                inv_std(a, 2)

            pool.wait_ge(tokens_loaded, 16)
            gather(0)
            pool.wait_ge(rows_loaded, 16)
            nc.gpsimd.tensor_tensor(b_b2[:], row("b"), row("b2"), ALU.add).then_inc(prepared_pool, 1)
            pool.wait_ge(prepared_pool, 3)
            add_bv(0)
            gather(1)
            both(0)
            both(1)
            both(2)
            with pool.Fori(3, SEQS) as a:
                both(a)
            b = SEQS - 1
            inv_std(b, 3)
            gau_xs(b - 2)
            keep_h2(b - 1)
            inv_std(b - 1, 5)
            gau_scatter(b - 2)
            gau_square(b)
            gau_residual(b)
            gau_xs(b - 1)
            inv_std(b, 5)
            gau_scatter(b - 1)
            keep_h2(b)
            gau_xs(b)
            gau_scatter(b)
            pool.wait_ge(emb_ready, 16 * NT * (SEQS + 2))

            def store(s, u):
                j = pool.value_load(table[0:1, 2, at_(s)], min_val=0, max_val=MTILES - 1)
                pool.wait_ge(m_sum_ready, MT * s + MT)
                apart(pool, "pool")
                nc.gpsimd.tensor_tensor(m_out[:, u], h2[:, bass.ds(j * MT, MT), :], m_sum[:, u], ALU.add
                                        ).then_inc(m_out_ready, 1)
                pool.wait_ge(m_out_ready, s + 1)
                apart(pool, "pool")
                if later(s):
                    pool.wait_ge(m_stored, 16 * s)
                apart(pool, "pool")
                pool.dma_start(out[bass.ds(j * MROWS, MROWS), :].rearrange("(t p) d -> p t d", p=P),
                             m_out[:, u]).then_inc(m_stored, 16)

            def pair(i):
                store(2 * i, 0)
                store(2 * i + 1, 1)

            pool.wait_ge(plan_ready, 3)
            pair(0)
            with pool.Fori(1, STEPS // 2) as i:
                pair(i)
            store(STEPS - 1, 0)
            pool.wait_ge(m_stored, 16 * STEPS)

        @block.scalar
        def _(act):
            act.dma_start(cols[:], ins["cols"]).then_inc(cols_loaded, 16)
            act.dma_start(rows_in[:], ins["rows"].partition_broadcast(P)).then_inc(rows_loaded, 16)
            act.wait_ge(cols_loaded, 16)
            nc.scalar.copy(wide, col("ab").to_broadcast([P, P])).then_inc(wide_ready, 1)
            act.wait_ge(prepared, 4)

            def tok_xT(a):
                act.wait_ge(xT_psum, a + 1)
                nc.scalar.copy(f_hi[:], gb[0][:]).then_inc(xT_ready, 1)
                nc.scalar.copy(xT[:], gb[0][:]).then_inc(xT_whole_ready, 1)

            def tok_kq(a):
                act.wait_ge(k_psum, a + 1)
                nc.scalar.activation(kT[:], ta[1][:], ACT.Identity, bias=bk_scaled[:], scale=SCORE_SCALE
                                     ).then_inc(kq_ready, 1)
                act.wait_ge(q_psum, a + 1)
                nc.scalar.activation(qT[:], ta[2][:], ACT.Identity, bias=col("bq")).then_inc(kq_ready, 1)

            def tok_v(a):
                act.wait_ge(v_psum, a + 1)
                nc.scalar.copy(v[:].rearrange("p t d -> p (t d)"), ta[3][:]).then_inc(v_ready, 1)

            def tok_exp(a):
                for c in range(NT):
                    act.wait_ge(max_ready, NT * a + c + 1)
                    nc.scalar.activation(probs[:, c], ta[c][:], ACT.Exp, bias=neg_max[:, c:c + 1],
                                         accum_out=exp_sum[:, c:c + 1]).then_inc(probs_ready, 1)

            def tok_probsT(a):
                for j in range(NT // 2, NT):
                    act.wait_ge(probsT_psum, NT * a + j + 1)
                    nc.scalar.copy(probsT[:, j], ta[j][:]).then_inc(probsT_act, 1)

            def tok_rT(a):
                act.wait_ge(rT_psum, a + 1)
                nc.scalar.copy(f_hi[:], ta[1][:]).then_inc(rT_ready, 1)

            def tok_gelu(a):
                for f in range(NF):
                    act.wait_ge(ff_psum, NF * a + f + 1)
                    nc.scalar.activation(geluT[:, f], ta[(f + 2) % 4][:], ACT.Gelu, bias=col(f"b1_{f}")
                                         ).then_inc(gelu_ready, 1)

            def gau_nT(b):
                act.wait_ge(nT_psum, b + 1)
                nc.scalar.copy(f_hi[:], gb[0][:]).then_inc(nT_ready, 1)

            def gau_silu(b):
                act.wait_ge(z_psum, b + 1)
                nc.scalar.activation(zT[:], gb[0][:], ACT.Silu, bias=col("bqk")).then_inc(z_ready, 1)
                for g in range(NH):
                    act.wait_ge(gate_psum, NH * b + g + 1)
                    nc.scalar.activation(gateT[:, g], gb[2 + g][:], ACT.Silu, bias=col(f"bh_{g}")
                                         ).then_inc(gate_ready, 1)

            def gau_gv(b):
                for i in range(2):
                    act.wait_ge(vpre_ready, 2 * b + i + 1)
                    nc.scalar.activation(gv[:, 2 * i:2 * i + 2, :], v_pre[:, 2 * i:2 * i + 2, :], ACT.Silu
                                         ).then_inc(gv_ready, 1)

            def gau_y(b):
                act.wait_ge(bias_ready, b + 1)
                for t in range(NT):
                    nc.scalar.activation(y[:, t], h[:, t], ACT.Identity, bias=y_bias[:, t:t + 1],
                                         scale=rstd[3][:, 0, t:t + 1]).then_inc(y_ready, 1)

            def gau_y2(b):
                act.wait_ge(bias2_ready, b + 1)
                if later(b):
                    act.wait_ge(xs_ready, b)
                for t in range(NT):
                    nc.scalar.activation(y2[:, t], h2_now[:, t], ACT.Identity, bias=y2_bias[:, t:t + 1],
                                         scale=rstd[5][:, 0, t:t + 1]).then_inc(y2_ready, 1)

            def gau_square(b):
                for j in range(NT // 2, NT):
                    act.wait_ge(relu_ready, NT * b + j + 1)
                    nc.scalar.activation(aT[:, j], relu[:, j], ACT.Square).then_inc(aT_act, 1)

            def gau_y2T(b):
                act.wait_ge(y2T_psum, b + 1)
                nc.scalar.copy(y2T[:], ta[3][:]).then_inc(y2T_ready, 1)

            def gau_lexp(b):
                act.wait_ge(route_step, ROUTE * b + 2)
                nc.scalar.activation(lexp[:], lshift[:], ACT.Exp).then_inc(lexp_ready, 1)

            def both(a):
                b = a - 1
                tok_kq(a)
                tok_v(a)
                if later(a):
                    gau_nT(b)
                tok_exp(a)
                if later(a):
                    gau_silu(b)
                tok_probsT(a)
                if later(b):
                    gau_y2(b - 1)
                if later(a):
                    gau_gv(b)
                    gau_y(b)
                if later(b):
                    gau_y2T(b - 1)
                if later(a):
                    gau_square(b)
                tok_rT(a)
                if not later(a):
                    act.wait_ge(folded, 3)
                    act.wait_ge(split_ready, 3)
                tok_gelu(a)
                tok_xT(a + 1)
                if later(b):
                    gau_lexp(b - 1)

            tok_xT(0)
            both(0)
            both(1)
            both(2)
            with act.Fori(3, SEQS) as a:
                both(a)
            b = SEQS - 1
            gau_nT(b)
            gau_silu(b)
            gau_y2(b - 1)
            gau_gv(b)
            gau_y(b)
            gau_y2T(b - 1)
            gau_square(b)
            gau_lexp(b - 1)
            gau_y2(b)
            gau_y2T(b)
            gau_lexp(b)
            act.wait_ge(tail_ready, 1)
            zero_tails(act, E // 2, E)

            act.wait_ge(plan_ready, 3)
            act.wait_ge(experts_loaded, 16)

            def expert_xT(i, u):
                act.wait_ge(m_xT_psum[u], i + 1)
                nc.scalar.copy(m_x_hi[:, u], bank[u][:, 0:MROWS]).then_inc(m_xT_ready[u], 1)

            def step(s, i, u):
                e = act.value_load(table[0:1, 1, at_(s)], min_val=0, max_val=E - 1)
                nc.scalar.copy(m_b1[:, u], experts[:, bass.ds(e * EXPERT + DFF, NF)]).then_inc(m_b1_ready[u], 1)
                act.wait_ge(m_b1_ready[u], i + 1)
                for f in range(NF):
                    if f == NF // 2 and later(s):
                        expert_xT(i + u, 1 - u)
                    act.wait_ge(m_h_psum[u], NF // 2 * i + f // 2 + 1)
                    at = (f % 2) * MROWS
                    nc.scalar.activation(m_hT[:, u, f], bank[2 + 2 * u + f // 2][:, at:at + MROWS], ACT.Relu,
                                         bias=m_b1[:, u, f:f + 1]).then_inc(m_h_ready[u], 1)
                if later(i):
                    act.wait_ge(m_y_ready[u], i)
                nc.scalar.copy(m_rest[:, u], experts[:, bass.ds(e * EXPERT + UP, REST)]
                               ).then_inc(m_rest_ready[u], 1)

            def pair(i):
                step(2 * i, i, 0)
                step(2 * i + 1, i, 1)

            expert_xT(0, 0)
            expert_xT(0, 1)
            pair(0)
            with act.Fori(1, STEPS // 2) as i:
                pair(i)
            step(STEPS - 1, STEPS // 2, 0)

        @block.vector
        def _(dve):
            dve.wait_ge(const_loaded, 16)
            nc.vector.tensor_copy(before_bf[:], cst("before")).then_inc(prepared, 1)
            nc.vector.memset(ones_bf[:], 1.0).then_inc(prepared, 1)
            nc.vector.tensor_copy(filled[:], cst("base")).then_inc(prepared, 1)
            dve.wait_ge(cols_loaded, 16)
            nc.vector.tensor_scalar(bk_scaled[:], col("bk"), SCORE_SCALE, None, ALU.mult).then_inc(prepared, 1)

            V = nc.vector
            dve.wait_ge(split_loaded, 16)
            at_n = SPLIT["wh"][0]
            w1 = part(whole, "w1")
            w1_scaled = geluT[:, 0]
            wn_scaled = geluT[:].rearrange("p f s -> p (f s)")[:, DFF:DFF + SPLIT_W - at_n]
            V.tensor_scalar(w1_scaled, w1, col("g"), None, ALU.mult).then_inc(scaled_ready, 1)
            V.tensor_scalar(wn_scaled, whole[:, at_n:], col("ag"), None, ALU.mult).then_inc(scaled_ready, 1)
            pieces = ((whole[:, 0:2 * D], 0, 2 * D), (w1_scaled, 2 * D, at_n), (wn_scaled, at_n, SPLIT_W))
            for src, lo, hi in pieces:
                if lo == 2 * D:
                    dve.wait_ge(scaled_ready, 2)
                V.tensor_copy(w_hi[:, lo:hi], src).then_inc(hi_ready, 1)

            def low_part(i, bank_, hi_ready_, done, whole_ready=None):
                dve.wait_ge(hi_ready_, i + 1)
                if whole_ready is not None:
                    dve.wait_ge(whole_ready, i + 1)
                nc.vector.tensor_tensor(f_lo[:], bank_[:], f_hi[:].bitcast(F32), ALU.subtract).then_inc(done, 1)

            def embed(i):
                dve.wait_ge(emb_ready, 16 * NT * (i + 1))
                if later(i):
                    dve.wait_ge(xT_psum, i)
                    dve.wait_ge(xbv_ready, i)
                nc.vector.scalar_tensor_tensor(
                    x[:].rearrange("p t d -> p (t d)"), emb[:].rearrange("p t d -> p (t d)"), float(D) ** 0.5,
                    cst("pos"), ALU.mult, ALU.add).then_inc(x_ready, 1)

            def norm_stats(i, k, src, ready, n_ready_):
                for t in range(NT):
                    dve.wait_ge(ready, n_ready_(t))
                    nc.vector.bn_stats(stats[k][:, t], src(t)).then_inc(stats_ready[k], 1)
                dve.wait_ge(stats_ready[k], NT * i + NT)
                apart(dve, "dve")
                for t in range(NT):
                    nc.vector.bn_aggr(mv[k][:, t], stats[k][:, t]).then_inc(mv_ready[k], 1)
                dve.wait_ge(mv_ready[k], NT * i + NT)
                if k == 3:
                    nc.vector.tensor_scalar(var_eps[k][:, 1], mv[k][:, :, 1], 1.0 + EPS, EPS * EPS, ALU.mult,
                                            ALU.add).then_inc(var_ready[k], 1)
                nc.vector.tensor_scalar(var_eps[k][:, 0], mv[k][:, :, 1], EPS, None, ALU.add
                                        ).then_inc(var_ready[k], 1)

            def norm_apply(k, dst, src, scale, done):
                for t in range(NT):
                    nc.vector.tensor_scalar(dst[:, t], src(t), mv[k][:, t, 0:1], rstd[k][:, scale, t:t + 1],
                                            ALU.subtract, ALU.mult).then_inc(done, 1)

            def tok_max(a, c):
                dve.wait_ge(score_psum, NT * a + c + 1)
                nc.vector.reduce_max(neg_max[:, c:c + 1], ta[c][:], AX, negate=True).then_inc(max_ready, 1)

            def tok_probsT(a):
                for j in range(NT // 2):
                    dve.wait_ge(probsT_psum, NT * a + j + 1)
                    nc.vector.tensor_copy(probsT[:, j], ta[j][:]).then_inc(probsT_dve, 1)

            def tok_norm1(a):
                dve.wait_ge(probs_ready, NT * a + NT)
                nc.vector.reciprocal(exp_inv[:], exp_sum[:]).then_inc(inv_ready, 1)
                dve.wait_ge(attn_psum, a + 1)
                dve.wait_ge(inv_ready, a + 1)
                dve.wait_ge(xbv_ready, a + 1)
                for t in range(NT):
                    nc.vector.scalar_tensor_tensor(z1[:, t], ta[0][:, t * D:(t + 1) * D], exp_inv[:, t:t + 1],
                                                   x_bv[:, t], ALU.mult, ALU.add).then_inc(z1_ready, 1)
                norm_stats(a, 1, lambda t: z1[:, t], z1_ready, lambda t: NT * a + t + 1)

            def tok_apply1(a):
                dve.wait_ge(rstd_ready[1], a + 1)
                if later(a):
                    dve.wait_ge(rres_ready, a)
                norm_apply(1, r_hat, lambda t: z1[:, t], 0, rhat_ready)

            def tok_norm2(a):
                dve.wait_ge(out_psum, a + 1)
                dve.wait_ge(rres_ready, a + 1)
                nc.vector.tensor_tensor(z2[:], ta[2][:].rearrange("p (t d) -> p t d", d=D), r_res[:], ALU.add
                                        ).then_inc(z2_ready, 1)
                norm_stats(a, 2, lambda t: z2[:, t], z2_ready, lambda t: a + 1)

            def tok_h(a):
                for t in range(NT):
                    nc.vector.scalar_tensor_tensor(h_scaled[:, t], z2[:, t], mv[2][:, t, 0:1], row("g"),
                                                   ALU.subtract, ALU.mult).then_inc(hscaled_ready, 1)

            def gau_h(b):
                dve.wait_ge(rstd_ready[2], b + 1)
                if later(b):
                    dve.wait_ge(hy_ready, 2 * b)
                for t in range(NT):
                    dve.wait_ge(hscaled_ready, NT * b + t + 1)
                    nc.vector.scalar_tensor_tensor(h[:, t], h_scaled[:, t], rstd[2][:, 0, t:t + 1], row("b"),
                                                   ALU.mult, ALU.add).then_inc(h_ready, 1)

            def gau_norm3(b):
                norm_stats(b, 3, lambda t: h[:, t], h_ready, lambda t: NT * b + t + 1)

            def gau_n(b):
                dve.wait_ge(rstd_ready[3], 2 * b + 1)
                norm_apply(3, n, lambda t: h[:, t], 1, n_ready)

            def gau_bias(b):
                dve.wait_ge(rstd_ready[3], 2 * b + 2)
                if later(b):
                    dve.wait_ge(y_ready, NT * b)
                nc.vector.scalar_tensor_tensor(y_bias[:], mv[3][:, :, 0], -1.0, rstd[3][:, 0], ALU.mult, ALU.mult
                                               ).then_inc(bias_ready, 1)

            def gau_sqk(b):
                dve.wait_ge(z_ready, b + 1)
                for k, t in ((0, sqT), (1, skT)):
                    nc.vector.tensor_scalar(t[:], zT[:], col(f"gamma_{k}"), col(f"beta_{k}"), ALU.mult, ALU.add
                                            ).then_inc(sqk_ready, 1)

            def gau_vpre(b):
                for i in range(2):
                    dve.wait_ge(gv_psum, 2 * b + i + 1)
                    nc.vector.tensor_tensor(v_pre[:, 2 * i:2 * i + 2, :],
                                            gb[1 - i][:].rearrange("p (t d) -> p t d", d=HID),
                                            over_tiles(row("bhv"), 2), ALU.add).then_inc(vpre_ready, 1)

            def gau_relu(b, lo, hi):
                for j in range(lo, hi):
                    dve.wait_ge(sim_psum, NT * b + j + 1)
                    nc.vector.tensor_scalar(relu[:, j], gb[(j + 2) % 4][:], 0.0, SIM_SCALE, ALU.max, ALU.mult
                                            ).then_inc(relu_ready, 1)

            def gau_gated(b, g):
                dve.wait_ge(mix_psum, NH * b + g + 1)
                nc.vector.tensor_tensor(gatedT[:, g], gb[2 + g][:], gateT[:, g], ALU.mult
                                        ).then_inc(gated_ready, 1)

            def gau_h2(b):
                dve.wait_ge(wo_psum, b + 1)
                dve.wait_ge(hy_ready, 2 * b + 2)
                if later(b):
                    dve.wait_ge(h2_kept, b)
                    dve.wait_ge(y2_ready, NT * b)
                nc.vector.tensor_tensor(h2_now[:], gb[1][:].rearrange("p (t d) -> p t d", d=D),
                                        hy_bo[:], ALU.add).then_inc(h2_ready, 1)

            def gau_norm5(b):
                norm_stats(b, 5, lambda t: h2_now[:, t], h2_ready, lambda t: b + 1)

            def gau_bias2(b):
                dve.wait_ge(rstd_ready[5], b + 1)
                nc.vector.scalar_tensor_tensor(y2_bias[:], mv[5][:, :, 0], -1.0, rstd[5][:, 0], ALU.mult, ALU.mult
                                               ).then_inc(bias2_ready, 1)

            def each(ap):
                return ap[:, :, None].to_broadcast([P, NT, E])

            def gau_route(b):
                done = ROUTE * b
                dve.wait_ge(logit_psum, b + 1)
                nc.vector.tensor_tensor(logits[:], ta[2][:, 0:NT * E].rearrange("p (t e) -> p t e", e=E),
                                        over_tiles(row("bg")), ALU.add).then_inc(logits_ready, 1)
                dve.wait_ge(logits_ready, b + 1)
                nc.vector.reduce_max(lmax[:], logits[:], AX).then_inc(route_step, 1)
                dve.wait_ge(route_step, done + 1)
                nc.vector.tensor_tensor(lshift[:], logits[:], each(lmax), ALU.subtract).then_inc(route_step, 1)
                nc.vector.tensor_tensor(is_max[:], logits[:], each(lmax), ALU.is_equal).then_inc(route_step, 1)
                dve.wait_ge(route_step, done + 3)
                nc.vector.tensor_tensor(ranked[:], is_max[:], over_tiles(cst("down")), ALU.mult
                                        ).then_inc(route_step, 1)
                dve.wait_ge(route_step, done + 4)
                nc.vector.reduce_max(best[:], ranked[:], AX).then_inc(route_step, 1)
                dve.wait_ge(route_step, done + 5)
                if later(b):
                    dve.wait_ge(rank_psum, b)
                nc.vector.tensor_tensor(route_bf[:], ranked[:], each(best), ALU.is_equal).then_inc(route_step, 1)

            def gau_pmax(b):
                dve.wait_ge(lexp_ready, b + 1)
                nc.vector.reduce_sum(lsum[:], lexp[:], AX).then_inc(pmax_step, 1)
                dve.wait_ge(pmax_step, 2 * b + 1)
                nc.vector.reciprocal(pmax[:], lsum[:]).then_inc(pmax_step, 1)

            def gau_slot(b):
                done = 5 * b
                dve.wait_ge(rank_psum, b + 1)
                dve.wait_ge(route_step, ROUTE * b + 6)
                nc.vector.tensor_tensor(slot_all[:], ta[2][:, 0:NT * E].rearrange("p (t e) -> p t e", e=E),
                                        over_tiles(filled[:]), ALU.add).then_inc(slot_step, 1)
                dve.wait_ge(slot_step, done + 1)
                nc.vector.tensor_tensor(filled[:], ta[2][:, NT * E:(NT + 1) * E], filled[:], ALU.add
                                        ).then_inc(slot_step, 1)
                nc.vector.tensor_tensor(slot_own[:], slot_all[:], route_bf[:], ALU.mult).then_inc(slot_step, 1)
                dve.wait_ge(slot_step, done + 3)
                nc.vector.reduce_sum(slot[:], slot_own[:], AX).then_inc(slot_step, 1)
                dve.wait_ge(slot_step, done + 4)
                if later(b):
                    dve.wait_ge(scattered, 16 * NT * b)
                nc.vector.tensor_copy(slot_u[:], slot[:]).then_inc(slot_step, 1)

            def fold():
                dve.wait_ge(rows_loaded, 16)
                dve.wait_ge(fold_psum, 2)
                c1, c2 = COLS.index("b1_0"), COLS.index("bqk")
                V.tensor_tensor(cols[:, c1:c1 + NF], gb[2][:, 0:NF], cols[:, c1:c1 + NF], ALU.add
                                ).then_inc(folded, 1)
                V.tensor_tensor(cols[:, c2:c2 + 1 + NH], gb[2][:, NF:NF + 1 + NH], cols[:, c2:c2 + 1 + NH], ALU.add
                                ).then_inc(folded, 1)
                V.tensor_tensor(row("bhv"), gb[3][:, 0:HID], row("bhv"), ALU.add).then_inc(folded, 1)
                dve.wait_ge(folded, 3)

            def both(a):
                b = a - 1
                if later(a):
                    gau_h(b)
                    gau_norm3(b)
                if later(b - 1):
                    gau_pmax(b - 2)
                if later(a):
                    gau_n(b)
                tok_max(a, 0)
                tok_max(a, 1)
                tok_max(a, 2)
                if later(a):
                    low_part(b, gb[0], nT_ready, nT_lo_ready)
                tok_max(a, 3)
                if later(b):
                    gau_h2(b - 1)
                if not later(a):
                    fold()
                if later(a):
                    gau_bias(b)
                if later(b):
                    gau_norm5(b - 1)
                if later(a):
                    gau_sqk(b)
                if later(b):
                    gau_bias2(b - 1)
                tok_probsT(a)
                if later(a):
                    gau_vpre(b)
                    gau_relu(b, 0, NT // 2)
                tok_norm1(a)
                if later(a):
                    gau_relu(b, NT // 2, NT)
                if later(b):
                    gau_route(b - 1)
                tok_apply1(a)
                if later(b):
                    gau_slot(b - 1)
                low_part(a, ta[1], rT_ready, rT_lo_ready)
                embed(a + 1)
                if later(a):
                    gau_gated(b, 0)
                low_part(a + 1, gb[0], xT_ready, xT_lo_ready, xT_whole_ready)
                tok_norm2(a)
                tok_h(a)
                if later(a):
                    gau_gated(b, 1)

            embed(0)
            for n_, (src, lo, hi) in enumerate(pieces):
                dve.wait_ge(hi_ready, n_ + 1)
                V.tensor_tensor(w_lo[:, lo:hi], src, w_hi[:, lo:hi].bitcast(F32), ALU.subtract
                                ).then_inc(split_ready, 1)
            low_part(0, gb[0], xT_ready, xT_lo_ready, xT_whole_ready)
            both(0)
            both(1)
            both(2)
            with dve.Fori(3, SEQS) as a:
                both(a)
            b = SEQS - 1
            gau_h(b)
            gau_norm3(b)
            gau_pmax(b - 2)
            gau_n(b)
            gau_h2(b - 1)
            low_part(b, gb[0], nT_ready, nT_lo_ready)
            gau_bias(b)
            gau_norm5(b - 1)
            gau_sqk(b)
            gau_bias2(b - 1)
            gau_vpre(b)
            gau_relu(b, 0, NT)
            gau_route(b - 1)
            gau_gated(b, 0)
            gau_slot(b - 1)
            gau_gated(b, 1)
            gau_pmax(b - 1)
            gau_h2(b)
            gau_norm5(b)
            gau_bias2(b)
            gau_route(b)
            gau_pmax(b)
            gau_slot(b)

            steps = [0]

            def then(ins_):
                steps[0] += 1
                ins_.then_inc(plan_step, 1)
                dve.wait_ge(plan_step, steps[0])

            dve.wait_ge(slot_step, 5 * SEQS)
            V.tensor_copy(tail[:], filled[:]).then_inc(tail_ready, 1)
            then(V.tensor_tensor(count[:], filled[:], cst("base"), ALU.subtract))
            earlier = cst("earlier").rearrange("p (e k) -> p e k", k=E)

            def sum_earlier(dst, src):
                then(V.tensor_tensor(summed[:], earlier, src[:, None, :].to_broadcast([P, E, E]), ALU.mult))
                then(V.reduce_sum(dst, summed[:], AX))

            def also(ins_):
                steps[0] += 1
                ins_.then_inc(plan_step, 1)

            up, shift, offset, start, end = (facts[:, i] for i in range(FACTS))
            step_no = cst("step")

            def of_step(lo, hi):
                n_ = hi - lo
                also(V.tensor_copy(rise[:, lo:hi, 0:1], facts[:, lo:hi, 0:1]))
                then(V.tensor_tensor(rise[:, lo:hi, 1:E], facts[:, lo:hi, 1:E], facts[:, lo:hi, 0:E - 1], ALU.subtract))
                then(V.tensor_tensor(risen[:, lo:hi], begun[:, None, :, :].to_broadcast([P, n_, TABLE, E]),
                                     rise[:, lo:hi, None, :].to_broadcast([P, n_, TABLE, E]), ALU.mult))
                then(V.reduce_sum(at_step[:, lo:hi], risen[:, lo:hi], AX))

            also(V.tensor_copy(up, cst("up")))
            also(V.tensor_scalar(used[:], count[:], 0.0, None, ALU.is_gt))
            sum_earlier(start, count[:])
            also(V.tensor_copy(tiles_int[:, 0], start))
            then(V.tensor_tensor(end, start, count[:], ALU.add))
            also(V.tensor_tensor(offset, cst("base"), start, ALU.subtract))
            then(V.tensor_scalar(tiles_int[:, 1], end, -1.0, 0.0, ALU.add, ALU.max))
            then(V.tensor_scalar(tiles_int[:], tiles_int[:], MROWS.bit_length() - 1, None, ALU.logical_shift_right))
            then(V.tensor_copy(tiles_of[:], tiles_int[:]))
            then(V.scalar_tensor_tensor(ntile[:], tiles_of[:, 1], 1.0, tiles_of[:, 0], ALU.add, ALU.subtract))
            then(V.tensor_tensor(ntile[:], ntile[:], used[:], ALU.mult))
            sum_earlier(since[:], ntile[:])
            also(V.tensor_tensor(shift, tiles_of[:, 0], since[:], ALU.subtract))
            then(V.tensor_tensor(begun[:], step_no[:, :, None].to_broadcast([P, TABLE, E]),
                                 since[:, None, :].to_broadcast([P, TABLE, E]), ALU.is_ge))
            of_step(0, 3)
            up_s, shift_s, offset_s, start_s, end_s = (at_step[:, i] for i in range(FACTS))
            then(V.tensor_tensor(shift_s, shift_s, step_no, ALU.add))
            V.tensor_copy(table[:, 1], up_s).then_inc(plan_ready, 1)
            then(V.tensor_scalar(tile_at[:], shift_s, float(MTILES - 1), None, ALU.min))
            V.scalar_tensor_tensor(table[:, 0], tile_at[:], float(MROWS), offset_s, ALU.mult, ALU.add
                                   ).then_inc(plan_ready, 1)
            V.tensor_copy(table[:, 2], tile_at[:]).then_inc(plan_ready, 1)
            dve.wait_ge(plan_ready, 3)

            def masks():
                def by_row(ap):
                    return ap[:, :, None].to_broadcast([P, TABLE, MT])

                of_step(3, FACTS)
                then(V.scalar_tensor_tensor(row_at[:], by_row(shift_s), float(MROWS),
                                            cst("row")[:, None, :].to_broadcast([P, TABLE, MT]), ALU.mult, ALU.add))
                also(V.tensor_tensor(own[:], row_at[:], by_row(start_s), ALU.is_ge))
                then(V.tensor_tensor(own2[:], row_at[:], by_row(end_s), ALU.is_lt))
                V.tensor_tensor(own[:], own[:], own2[:], ALU.mult).then_inc(own_ready, 1)
                V.tensor_tensor(again[:, 1:TABLE], tile_at[:, 1:TABLE], tile_at[:, 0:TABLE - 1], ALU.is_equal
                                ).then_inc(own_ready, 1)
                dve.wait_ge(own_ready, 2)

            def expert_of(s):
                return dve.value_load(table[0:1, 1, at_(s)], min_val=0, max_val=E - 1)

            def w1_leading(e, i, u):
                if later(i):
                    dve.wait_ge(m_h_psum[u], NF // 2 * i)
                nc.vector.tensor_copy(m_w1_hi[:, u], experts[:, bass.ds(e * EXPERT, DFF)]
                                      ).then_inc(m_w1_ready[u], 1)

            def w1_low(e, i, u):
                dve.wait_ge(m_w1_ready[u], 2 * i + 1)
                nc.vector.tensor_tensor(m_w1_lo[:, u], experts[:, bass.ds(e * EXPERT, DFF)],
                                        m_w1_hi[:, u].bitcast(F32), ALU.subtract).then_inc(m_w1_ready[u], 1)

            def rows_low(i, u):
                dve.wait_ge(m_xT_ready[u], i + 1)
                nc.vector.tensor_tensor(m_x_lo[:, u], bank[u][:, 0:MROWS], m_x_hi[:, u].bitcast(F32), ALU.subtract
                                        ).then_inc(m_xlo_ready[u], 1)

            def step(s, i, u, ahead=True):
                if ahead:
                    e = expert_of(s + 3)
                if later(s):
                    dve.wait_ge(m_sum_ready, MT * s)
                    nc.vector.tensor_scalar(m_kept, m_sum[:, 1 - u], again[:, at_(s)], None, ALU.mult
                                            ).then_inc(m_kept_ready, 1)
                else:
                    nc.vector.memset(m_kept, 0.0).then_inc(m_kept_ready, 1)
                if ahead:
                    rows_low(i + 1, u)
                dve.wait_ge(m_y_psum[u], i + 1)
                dve.wait_ge(m_rest_ready[u], i + 1)
                nc.vector.tensor_tensor(m_y[:, u], bank[6 + u][:, 0:MT * D].rearrange("p (t d) -> p t d", d=D),
                                        over_tiles(m_rest[:, u, NF * D:REST], MT), ALU.add
                                        ).then_inc(m_y_ready[u], 1)
                if ahead:
                    w1_leading(e, i + 1 + u, 1 - u)
                if later(i):
                    dve.wait_ge(m_out_ready, s - 1)
                dve.wait_ge(m_kept_ready, s + 1)
                dve.wait_ge(m_y_ready[u], i + 1)
                for t in range(MT):
                    nc.vector.scalar_tensor_tensor(m_sum[:, u, t], m_y[:, u, t], own[:, at_(s), t], m_kept[:, t],
                                                   ALU.mult, ALU.add).then_inc(m_sum_ready, 1)
                if ahead:
                    w1_low(e, i + 1 + u, 1 - u)

            def pair(i):
                step(2 * i, i, 0)
                step(2 * i + 1, i, 1)

            dve.wait_ge(experts_loaded, 16)
            for s in range(2):
                e = expert_of(s)
                w1_leading(e, 0, s)
                w1_low(e, 0, s)
            rows_low(0, 0)
            rows_low(0, 1)
            masks()
            e = expert_of(2)
            w1_leading(e, 1, 0)
            w1_low(e, 1, 0)
            pair(0)
            with dve.Fori(1, STEPS // 2) as i:
                pair(i)
            step(STEPS - 1, STEPS // 2, 0, ahead=False)

        @block.tensor
        def _(pe):
            pe.wait_ge(const_loaded, 16)
            pe.wait_ge(prepared, 4)
            mm = nc.tensor.matmul

            def shares():
                pe.wait_ge(split_loaded, 16)
                pe.wait_ge(cols_loaded, 16)
                pe.wait_ge(wide_ready, 1)
                at = 0
                for name, lo, n_, shift in (("w1", 0, NF, "b"), ("wqk", 0, 1, "ab"), ("wh", HID, NH, "ab")):
                    for f in range(n_):
                        last = mm(gb[2][:, at:at + 1], part(whole, name, lo + f * P, lo + (f + 1) * P), col(shift),
                                  start=True, stop=True)
                        at += 1
                last.then_inc(fold_psum, 1)
                mm(gb[3][:, 0:HID], wide, part(whole, "wh", 0, HID), start=True, stop=True).then_inc(fold_psum, 1)


            def leading(dst, weight):
                mm(dst, part(w_hi, *weight), f_hi[:], start=True, stop=False)
                return mm(dst, part(w_lo, *weight), f_hi[:], start=False, stop=False)

            def trailing(dst, weight):
                return mm(dst, part(w_hi, *weight), f_lo[:], start=False, stop=True)

            def by_rows(dst, t, weight):
                at = slice(t * P, (t + 1) * P)
                mm(dst, f_hi[:, at], part(w_hi, *weight), start=True, stop=False)
                mm(dst, f_hi[:, at], part(w_lo, *weight), start=False, stop=False)
                return mm(dst, f_lo[:, at], part(w_hi, *weight), start=False, stop=True)

            def transposed(dst, src, done):
                for t in range(NT):
                    last = nc.tensor.transpose(dst[:, t * P:(t + 1) * P], src[:, t], ident)
                last.then_inc(done, 1)

            def tok_xT(a):
                pe.wait_ge(x_ready, a + 1)
                transposed(gb[0], x, xT_psum)

            def tok_kqv(a):
                pe.wait_ge(xT_ready, a + 1)
                if not later(a):
                    pe.wait_ge(split_ready, 3)
                leading(ta[1][:], ("wk",))
                if later(a):
                    pe.wait_ge(z2_ready, a)
                leading(ta[2][:], ("wq",))
                pe.wait_ge(xT_lo_ready, a + 1)
                trailing(ta[1][:], ("wk",)).then_inc(k_psum, 1)
                trailing(ta[2][:], ("wq",)).then_inc(q_psum, 1)
                pe.wait_ge(xT_whole_ready, a + 1)
                for t in range(NT):
                    last = mm(ta[3][:, t * D:(t + 1) * D], xT[:, t * P:(t + 1) * P], mat("wv"),
                              start=True, stop=True)
                last.then_inc(v_psum, 1)

            def tok_scores(a, lo, hi):
                for c in range(lo, hi):
                    if c == 0:
                        pe.wait_ge(kq_ready, 2 * a + 2)
                    if c == NT - 1:
                        pe.wait_ge(v_ready, a + 1)
                    mm(ta[c][:], kT[:, c * P:(c + 1) * P], qT[:], start=True, stop=True).then_inc(score_psum, 1)

            def tok_probsT(a):
                pe.wait_ge(probs_ready, NT * a + NT)
                for j in range(NT):
                    for i in range(NT):
                        last = nc.tensor.transpose(ta[j][:, i * P:(i + 1) * P], probs[:, i, j * P:(j + 1) * P],
                                                   ident)
                    last.then_inc(probsT_psum, 1)

            def tok_attend(a):
                for i in range(NT):
                    for j in range(NT):
                        last = mm(ta[0][:, i * D:(i + 1) * D], probsT[:, j, i * P:(i + 1) * P], v[:, j],
                                  start=(j == 0), stop=(j == NT - 1))
                last.then_inc(attn_psum, 1)

            def tok_rT(a):
                pe.wait_ge(rhat_ready, NT * a + NT)
                transposed(ta[1], r_hat, rT_psum)

            def tok_ff1(a):
                pe.wait_ge(rT_ready, a + 1)
                for half in (0, 2):
                    for f in (half, half + 1):
                        leading(ta[(f + 2) % 4][:], ("w1", f * P, (f + 1) * P))
                    if half == 0:
                        pe.wait_ge(rT_lo_ready, a + 1)
                    for f in (half, half + 1):
                        trailing(ta[(f + 2) % 4][:], ("w1", f * P, (f + 1) * P)).then_inc(ff_psum, 1)

            def tok_ff2(a):
                for f in range(NF):
                    pe.wait_ge(gelu_ready, NF * a + f + 1)
                    for i in range(NT):
                        last = mm(ta[2][:, i * D:(i + 1) * D], geluT[:, f, i * P:(i + 1) * P],
                                  mat("w2", f * D, (f + 1) * D), start=(f == 0 and i == 0), stop=(f == NF - 1),
                                  skip_group_check=True)
                last.then_inc(out_psum, 1)

            def gau_nT(b):
                pe.wait_ge(n_ready, NT * b + NT)
                transposed(gb[0], n, nT_psum)

            def gau_project(b):
                pe.wait_ge(nT_ready, b + 1)
                if not later(b):
                    pe.wait_ge(folded, 3)
                gate = [("wh", HID + g * P, HID + (g + 1) * P) for g in range(NH)]
                for g in range(NH):
                    leading(gb[2 + g][:], gate[g])
                pe.wait_ge(nT_lo_ready, b + 1)
                for g in range(NH):
                    trailing(gb[2 + g][:], gate[g]).then_inc(gate_psum, 1)
                leading(gb[0][:], ("wqk",))
                trailing(gb[0][:], ("wqk",)).then_inc(z_psum, 1)
                gau_v(b, 0)

            def gau_v(b, i):
                if i == 1:
                    pe.wait_ge(z_ready, b + 1)
                elif later(b):
                    pe.wait_ge(h2_ready, b)
                for t in (2 * i, 2 * i + 1):
                    last = by_rows(gb[1 - i][:, (t % 2) * HID:(t % 2 + 1) * HID], t, ("wh", 0, HID))
                last.then_inc(gv_psum, 1)

            def gau_sim(b, lo, hi):
                if lo == 0:
                    pe.wait_ge(sqk_ready, 2 * b + 2)
                    pe.wait_ge(gate_ready, NH * b + NH)
                if hi == NT:
                    pe.wait_ge(vpre_ready, 2 * b + 2)
                for j in range(lo, hi):
                    mm(gb[(j + 2) % 4][:], skT[:, j * P:(j + 1) * P], sqT[:], start=True, stop=True
                       ).then_inc(sim_psum, 1)

            def gau_mix(b, g, lo, hi):
                for j in range(lo, hi):
                    if g == 0 and j == 0:
                        pe.wait_ge(gv_ready, 2 * b + 2)
                        pe.wait_ge(aT_pool, 2 * b + 2)
                    if g == 0 and j >= NT // 2:
                        pe.wait_ge(aT_act, 2 * b + j - NT // 2 + 1)
                    last = mm(gb[2 + g][:], gv[:, j, g * P:(g + 1) * P], aT[:, j], start=(j == 0),
                              stop=(j == NT - 1))
                if hi == NT:
                    last.then_inc(mix_psum, 1)

            def gau_wo(b):
                pe.wait_ge(gated_ready, NH * b + NH)
                for i in range(NT):
                    for g in range(NH):
                        last = mm(gb[1][:, i * D:(i + 1) * D], gatedT[:, g, i * P:(i + 1) * P],
                                  mat("wo", g * D, (g + 1) * D), start=(g == 0), stop=(g == NH - 1))
                last.then_inc(wo_psum, 1)

            def gau_y2T(b):
                pe.wait_ge(y2_ready, NT * b + NT)
                transposed(ta[3], y2, y2T_psum)

            def gau_logits(b):
                pe.wait_ge(y2T_ready, b + 1)
                for t in range(NT):
                    last = mm(ta[2][:, t * E:(t + 1) * E], y2T[:, t * P:(t + 1) * P], mat("wg"),
                              start=True, stop=True)
                last.then_inc(logit_psum, 1)

            def gau_rank(b):
                pe.wait_ge(route_step, ROUTE * b + 6)
                mm(ta[2][:, 0:NT * E], before_bf[:], route_bf[:].rearrange("p t e -> p (t e)"),
                   start=True, stop=False, skip_group_check=True)
                for t in range(NT):
                    last = mm(ta[2][:, (t + 1) * E:(NT + 1) * E], ones_bf[:],
                              route_bf[:, t:t + 1, :].to_broadcast([P, NT - t, E]),
                              start=False, stop=(t == NT - 1), skip_group_check=True)
                last.then_inc(rank_psum, 1)

            def both(a):
                b = a - 1
                tok_kqv(a)
                if later(b):
                    gau_wo(b - 1)
                tok_scores(a, 0, NT - 1)
                if later(a):
                    gau_nT(b)
                tok_scores(a, NT - 1, NT)
                if not later(a):
                    shares()
                if later(a):
                    gau_project(b)
                tok_probsT(a)
                if later(a):
                    gau_v(b, 1)
                    gau_sim(b, 0, NT // 2)
                pe.wait_ge(probsT_dve, NT // 2 * (a + 1))
                pe.wait_ge(probsT_act, NT // 2 * (a + 1))
                tok_attend(a)
                if later(b):
                    gau_y2T(b - 1)
                if later(a):
                    gau_sim(b, NT // 2, NT)
                if later(b):
                    gau_logits(b - 1)
                if later(a):
                    gau_mix(b, 0, 0, NT - 1)
                if later(b):
                    gau_rank(b - 1)
                if later(a):
                    gau_mix(b, 0, NT - 1, NT)
                tok_rT(a)
                if later(a):
                    gau_mix(b, 1, 0, 1)
                if later(b):
                    pe.wait_ge(slot_step, 5 * b)
                tok_ff1(a)
                tok_xT(a + 1)
                tok_ff2(a)
                if later(a):
                    gau_mix(b, 1, 1, NT)

            tok_xT(0)
            pe.wait_ge(mats_loaded, 16)
            both(0)
            both(1)
            both(2)
            with pe.Fori(3, SEQS) as a:
                both(a)
            b = SEQS - 1
            gau_wo(b - 1)
            pe.wait_ge(z2_ready, b + 1)
            gau_nT(b)
            gau_project(b)
            gau_v(b, 1)
            gau_y2T(b - 1)
            gau_sim(b, 0, NT)
            gau_logits(b - 1)
            gau_mix(b, 0, 0, NT)
            gau_rank(b - 1)
            gau_mix(b, 1, 0, NT)
            gau_wo(b)
            gau_y2T(b)
            pe.wait_ge(slot_step, 5 * b)
            gau_logits(b)
            gau_rank(b)

            def expert_xT(i, u):
                pe.wait_ge(m_loaded[u], 16 * (i + 1))
                if later(i):
                    pe.wait_ge(m_xT_ready[u], i)
                    pe.wait_ge(m_xlo_ready[u], i)
                for t in range(MT):
                    last = nc.tensor.transpose(bank[u][:, t * P:(t + 1) * P], m_rows[:, u, t], ident)
                last.then_inc(m_xT_psum[u], 1)

            def expert_up(i, u):
                pe.wait_ge(m_xT_ready[u], i + 1)
                pe.wait_ge(m_w1_ready[u], 2 * i + 2)
                pe.wait_ge(m_xlo_ready[u], i + 1)
                if later(i):
                    pe.wait_ge(m_h_ready[u], NF * i)
                for f in range(NF):
                    at = (f % 2) * MROWS
                    dst = bank[2 + 2 * u + f // 2][:, at:at + MROWS]
                    w = slice(f * P, (f + 1) * P)
                    mm(dst, m_w1_hi[:, u, w], m_x_hi[:, u], start=True, stop=False)
                    mm(dst, m_w1_lo[:, u, w], m_x_hi[:, u], start=False, stop=False)
                    last = mm(dst, m_w1_hi[:, u, w], m_x_lo[:, u], start=False, stop=True)
                    if f % 2:
                        last.then_inc(m_h_psum[u], 1)

            def expert_down(i, u):
                pe.wait_ge(m_h_ready[u], NF * (i + 1))
                pe.wait_ge(m_rest_ready[u], i + 1)
                if later(i):
                    pe.wait_ge(m_y_ready[u], i)
                for t in range(MT):
                    for f in range(NF):
                        last = mm(bank[6 + u][:, t * D:(t + 1) * D], m_hT[:, u, f, t * P:(t + 1) * P],
                                  m_rest[:, u, f * D:(f + 1) * D], start=(f == 0), stop=(f == NF - 1))
                last.then_inc(m_y_psum[u], 1)

            pe.wait_ge(plan_ready, 3)
            expert_xT(0, 0)
            expert_xT(0, 1)
            expert_up(0, 0)

            def pair(i):
                expert_up(i, 1)
                expert_xT(i + 1, 0)
                expert_down(i, 0)
                expert_up(i + 1, 0)
                expert_xT(i + 1, 1)
                expert_down(i, 1)

            pair(0)
            with pe.Fori(1, STEPS // 2) as i:
                pair(i)
            expert_down(STEPS // 2, 0)


def constants():
    c = np.zeros((P, CONST_W), np.float32)

    def put(name, a):
        at, w = CONST[name]
        c[:, at:at + w] = a

    pos = np.arange(S, dtype=np.float32)[:, None]
    i = np.arange(D, dtype=np.float32)[None, :]
    ang = (pos / np.power(np.float32(10000.0), np.float32(2.0) * i / np.float32(D))).astype(np.float64)
    pe = np.where((np.arange(D) % 2 == 0)[None, :], np.sin(ang), np.cos(ang)) * D ** 0.5
    put("pos", pe.reshape(NT, P, D).transpose(1, 0, 2).reshape(P, NT * D))
    put("ident", np.eye(P))
    put("before", np.triu(np.ones((P, P)), 1))
    put("base", np.arange(E) * REGION + PAD)
    put("down", E - np.arange(E))
    put("up", np.arange(E))
    put("earlier", np.tril(np.ones((E, E)), -1).reshape(-1))
    put("row", np.arange(MT)[None, :] * P + np.arange(P)[:, None])
    put("step", np.arange(TABLE))
    return c


def kernel(**inputs):
    import concourse.bacc as _bacc
    from concourse.bass_utils import run_bass_kernel_spmd as _run

    g = {k: np.asarray(a) for k, a in inputs.items()}
    tok = {k[7:]: a for k, a in g.items() if k.startswith("L0_tok_")}
    att = {k[8:]: a for k, a in g.items() if k.startswith("L0_attn_")}
    ffn = {k[7:]: a for k, a in g.items() if k.startswith("L0_ffn_")}

    def chunks(w):
        return w.reshape(-1, P, w.shape[1]).transpose(1, 0, 2).reshape(P, -1)

    col_of = {"bk": tok["bk"], "bq": tok["bq"], "g": tok["ln_g"], "b": tok["ln_b"], "ag": att["ln_g"],
              "ab": att["ln_b"], "bqk": att["bqk"]}
    for f in range(NF):
        col_of[f"b1_{f}"] = tok["b1"][f * P:(f + 1) * P]
    for k in range(NH):
        col_of[f"bh_{k}"] = att["bh"][HID + k * P:HID + (k + 1) * P]
    for k in range(2):
        col_of[f"gamma_{k}"] = att["gamma"][k]
        col_of[f"beta_{k}"] = att["beta"][k]
    row_of = {"bv": tok["bv"], "g": tok["ln_g"], "b": tok["ln_b"], "b2": tok["b2"], "bo": att["bo"],
              "bhv": att["bh"][:HID], "bg": ffn["bg"]}
    mat_of = {"wk": tok["wk"], "wq": tok["wq"], "wv": tok["wv"], "w1": tok["w1"], "w2": chunks(tok["w2"]),
              "wh": att["Wh"], "wqk": att["Wqk"], "wo": chunks(att["Wo"]), "wg": ffn["Wg"]}
    w1 = ffn["W1"].transpose(1, 0, 2)
    w2 = ffn["W2"].reshape(E, NF, P, D).transpose(2, 0, 1, 3).reshape(P, E, NF * D)
    b1 = ffn["b1"].reshape(E, NF, P).transpose(2, 0, 1)
    b2 = np.broadcast_to(ffn["b2"], (P, E, D))
    tokens = np.zeros((P, (SEQS + 2) * NT), np.int32)
    tokens[:, :TILES] = g["x"].reshape(TILES, P).T
    arrays = {
        "tokens": tokens,
        "const": constants(),
        "split": np.ascontiguousarray(np.concatenate([mat_of[k] for k in SPLIT], axis=1)),
        "mats": np.ascontiguousarray(np.concatenate([mat_of[k] for k in MATS], axis=1)),
        "cols": np.ascontiguousarray(np.stack([col_of[k] for k in COLS], axis=1)),
        "rows": np.concatenate([row_of[k] for k in ROWS]),
        "experts": np.ascontiguousarray(np.concatenate([w1, b1, w2, b2], axis=2).reshape(P, E * EXPERT)),
        "emb": np.ascontiguousarray(tok["emb"]),
    }
    nc = _bacc.Bacc("TRN2", target_bir_lowering=False, num_devices=1)
    ins = {k: nc.dram_tensor(f"in_{k}_dram", a.shape, mybir.dt.from_np(a.dtype), kind="ExternalInput").ap()
           for k, a in arrays.items()}
    out = nc.dram_tensor("out_0_dram", (SEQS * S, D), F32, kind="ExternalOutput").ap()
    build(nc, ins, out)
    r = _run(nc, [{f"in_{k}_dram": a for k, a in arrays.items()}], core_ids=[0])
    return r.results[0]["out_0_dram"].reshape(SEQS, S, D)
```
